# Optimizing a Trainium2 kernel written in Bass

```python
import numpy as np
import jax
import jax.numpy as jnp

def _softmax(x, axis=-1):
    return jax.nn.softmax(x, axis=axis)

def _gelu(x):
    return jax.nn.gelu(x, approximate=True)

def _silu(x):
    return jax.nn.silu(x)

def _sigmoid(x):
    return jax.nn.sigmoid(x)

def _layernorm(x, axis=-1, eps=1e-05):
    m = jnp.mean(x, axis=axis, keepdims=True)
    v = jnp.var(x, axis=axis, keepdims=True)
    return (x - m) / jnp.sqrt(v + eps)

def _scatter_add(tgt, idx, src, axis=0):
    return tgt.at[idx].add(src)

def _segment_sum(src, seg, n):
    return jax.ops.segment_sum(src, seg, n)
kernel_name = 'mk_hybrid_d1_jaxref_r8_252cec'

def setup_inputs(seed: int=0):
    np.random.seed(seed)
    _w = jnp.asarray

    def _L0_attn_a_setup():
        import jax, jax.numpy as jnp
        import numpy as np
        B, S, D = (16, 64, 256)
        NUM_HEADS, NUM_GROUPS = (16, 4)
        HEAD_DIM = D // NUM_HEADS
        MAX_SEQ_LEN, SHARED_SLOTS = (64, 32)
        EPS = 1e-06

        def _rope_tables(seq_positions):
            inv_freq = 1.0 / 10000.0 ** (jnp.arange(0, HEAD_DIM, 2, dtype=jnp.float32) / HEAD_DIM)
            freqs = jnp.outer(seq_positions.astype(jnp.float32), inv_freq)
            return (jnp.cos(freqs), jnp.sin(freqs))

        def _apply_rope(x, cos, sin):
            x1, x2 = jnp.split(x, 2, axis=-1)
            real = x1 * cos - x2 * sin
            imag = x1 * sin + x2 * cos
            return jnp.concatenate([real, imag], axis=-1).astype(x.dtype)

        def _rmsnorm(x, scale):
            x = x.astype(jnp.float32)
            ms = jnp.mean(jnp.square(x), axis=-1, keepdims=True)
            return x * jax.lax.rsqrt(ms + EPS) * scale
        key = jax.random.key(seed)
        ks = jax.random.split(key, 10)
        w = 0.02
        return {'x': jax.random.normal(ks[0], (B, S, D), dtype=jnp.float32), 'wq': jax.random.normal(ks[1], (D, D), dtype=jnp.float32) * w, 'bq': jnp.zeros((D,), dtype=jnp.float32), 'wk': jax.random.normal(ks[2], (D, NUM_GROUPS * HEAD_DIM), dtype=jnp.float32) * w, 'bk': jnp.zeros((NUM_GROUPS * HEAD_DIM,), dtype=jnp.float32), 'wv': jax.random.normal(ks[3], (D, NUM_GROUPS * HEAD_DIM), dtype=jnp.float32) * w, 'bv': jnp.zeros((NUM_GROUPS * HEAD_DIM,), dtype=jnp.float32), 'wo': jax.random.normal(ks[4], (D, D), dtype=jnp.float32) * w, 'bo': jnp.zeros((D,), dtype=jnp.float32), 'q_norm_scale': jnp.ones((HEAD_DIM,), dtype=jnp.float32), 'k_norm_scale': jnp.ones((HEAD_DIM,), dtype=jnp.float32)}
    _L0_attn_a_in = _L0_attn_a_setup()

    def _L0_attn_b_setup():
        import jax, jax.numpy as jnp
        import numpy as np
        B, S, HID = (4, 512, 256)
        H, NB = (16, 4)
        D = HID // H
        EPS = 1e-06

        def elu_plus_one(x):
            return jax.nn.elu(x) + 1.0

        def _reference_tuple_inner(hidden_states, Wq, Wk, Wv, Wo, bank_weights, memories, memory_norms):
            b, s, _ = hidden_states.shape

            def proj(W):
                return (hidden_states @ W.T).reshape(b, s, H, D).transpose(0, 2, 1, 3)
            q, k, v = (proj(Wq), proj(Wk), proj(Wv))
            sigma_q = elu_plus_one(q)
            a_unnorm = jnp.einsum('bhsd,nhde->nbhse', sigma_q, memories)
            norm = jnp.einsum('bhsd,nhd->nbhs', sigma_q, memory_norms)
            a = a_unnorm / jnp.clip(norm, EPS, None)[..., None]
            active = (memory_norms.sum(axis=(1, 2)) >= EPS).astype(a.dtype)
            a = a * active[:, None, None, None, None]
            weights = jax.nn.softmax(bank_weights, axis=-1)
            combined = jnp.einsum('nbhse,hn->bhse', a, weights)
            sigma_k = elu_plus_one(k)
            mem0, norm0 = (memories[0], memory_norms[0])
            retr = jnp.einsum('bhsd,hde->bhse', sigma_k, mem0)
            knorm = jnp.clip(jnp.einsum('bhsd,hd->bhs', sigma_k, norm0), EPS, None)
            delta_v = v - retr / knorm[..., None]
            mem_update = jnp.einsum('bhsd,bhse->hde', sigma_k, delta_v) / (b * s)
            new_mem0 = jax.lax.stop_gradient(mem0 + mem_update)
            new_norm0 = jax.lax.stop_gradient(norm0 + sigma_k.sum(axis=(0, 2)) / b)
            out = combined.transpose(0, 2, 1, 3).reshape(b, s, HID) @ Wo.T
            return (out, new_mem0, new_norm0)
        key = jax.random.key(seed)
        ks = jax.random.split(key, 8)
        return {'hidden_states': jax.random.normal(ks[0], (B, S, HID), jnp.float32), 'Wq': jax.random.normal(ks[1], (HID, HID), jnp.float32) * 0.02, 'Wk': jax.random.normal(ks[2], (HID, HID), jnp.float32) * 0.02, 'Wv': jax.random.normal(ks[3], (HID, HID), jnp.float32) * 0.02, 'Wo': jax.random.normal(ks[4], (HID, HID), jnp.float32) * 0.02, 'bank_weights': jax.random.normal(ks[5], (H, NB), jnp.float32) * 0.02, 'memories': jax.random.uniform(ks[6], (NB, H, D, D), jnp.float32), 'memory_norms': jax.random.uniform(ks[7], (NB, H, D), jnp.float32)}
    _L0_attn_b_in = _L0_attn_b_setup()

    def _L0_ffn_setup():
        import jax, jax.numpy as jnp
        import numpy as np
        H = 256
        I = 176
        E = 8
        K = 2
        B, S = (2, 256)
        key = jax.random.key(seed)
        k0, k1, k2, k3, k4 = jax.random.split(key, 5)
        scale = 1.0 / np.sqrt(H)
        x = jax.random.normal(k0, (B, S, H), dtype=jnp.float32)
        Wr = jax.random.normal(k1, (H, E), dtype=jnp.float32) * scale
        Wg = jax.random.normal(k2, (E, H, I), dtype=jnp.float32) * scale
        Wu = jax.random.normal(k3, (E, H, I), dtype=jnp.float32) * scale
        Wd = jax.random.normal(k4, (E, I, H), dtype=jnp.float32) * (1.0 / np.sqrt(I))
        return {'x': x, 'Wr': Wr, 'Wg': Wg, 'Wu': Wu, 'Wd': Wd}
    _L0_ffn_in = _L0_ffn_setup()
    _d = {'L0_attn_a_x': _L0_attn_a_in['x'], 'L0_attn_a_wq': _L0_attn_a_in['wq'], 'L0_attn_a_bq': _L0_attn_a_in['bq'], 'L0_attn_a_wk': _L0_attn_a_in['wk'], 'L0_attn_a_bk': _L0_attn_a_in['bk'], 'L0_attn_a_wv': _L0_attn_a_in['wv'], 'L0_attn_a_bv': _L0_attn_a_in['bv'], 'L0_attn_a_wo': _L0_attn_a_in['wo'], 'L0_attn_a_bo': _L0_attn_a_in['bo'], 'L0_attn_a_q_norm_scale': _L0_attn_a_in['q_norm_scale'], 'L0_attn_a_k_norm_scale': _L0_attn_a_in['k_norm_scale'], 'L0_attn_b_Wq': _L0_attn_b_in['Wq'], 'L0_attn_b_Wk': _L0_attn_b_in['Wk'], 'L0_attn_b_Wv': _L0_attn_b_in['Wv'], 'L0_attn_b_Wo': _L0_attn_b_in['Wo'], 'L0_attn_b_bank_weights': _L0_attn_b_in['bank_weights'], 'L0_attn_b_memories': _L0_attn_b_in['memories'], 'L0_attn_b_memory_norms': _L0_attn_b_in['memory_norms'], 'L0_ffn_Wr': _L0_ffn_in['Wr'], 'L0_ffn_Wg': _L0_ffn_in['Wg'], 'L0_ffn_Wu': _L0_ffn_in['Wu'], 'L0_ffn_Wd': _L0_ffn_in['Wd']}
    _x0 = _d['L0_attn_a_x']
    _d['L0_attn_a_x'] = jax.random.normal(jax.random.fold_in(jax.random.key(seed), 1), (4, 512, 256), dtype=_x0.dtype)
    del _x0
    return _d

def reference(L0_attn_a_x, L0_attn_a_wq, L0_attn_a_bq, L0_attn_a_wk, L0_attn_a_bk, L0_attn_a_wv, L0_attn_a_bv, L0_attn_a_wo, L0_attn_a_bo, L0_attn_a_q_norm_scale, L0_attn_a_k_norm_scale, L0_attn_b_Wq, L0_attn_b_Wk, L0_attn_b_Wv, L0_attn_b_Wo, L0_attn_b_bank_weights, L0_attn_b_memories, L0_attn_b_memory_norms, L0_ffn_Wr, L0_ffn_Wg, L0_ffn_Wu, L0_ffn_Wd):

    def _L0_attn_a_ref(x, wq, bq, wk, bk, wv, bv, wo, bo, q_norm_scale, k_norm_scale):
        import jax, jax.numpy as jnp
        import numpy as np
        B, S, D = (16, 64, 256)
        NUM_HEADS, NUM_GROUPS = (16, 4)
        HEAD_DIM = D // NUM_HEADS
        MAX_SEQ_LEN, SHARED_SLOTS = (64, 32)
        EPS = 1e-06

        def _rope_tables(seq_positions):
            inv_freq = 1.0 / 10000.0 ** (jnp.arange(0, HEAD_DIM, 2, dtype=jnp.float32) / HEAD_DIM)
            freqs = jnp.outer(seq_positions.astype(jnp.float32), inv_freq)
            return (jnp.cos(freqs), jnp.sin(freqs))

        def _apply_rope(x, cos, sin):
            x1, x2 = jnp.split(x, 2, axis=-1)
            real = x1 * cos - x2 * sin
            imag = x1 * sin + x2 * cos
            return jnp.concatenate([real, imag], axis=-1).astype(x.dtype)

        def _rmsnorm(x, scale):
            x = x.astype(jnp.float32)
            ms = jnp.mean(jnp.square(x), axis=-1, keepdims=True)
            return x * jax.lax.rsqrt(ms + EPS) * scale
        b, s, d = x.shape
        rep = NUM_HEADS // NUM_GROUPS
        head_scale = HEAD_DIM ** (-0.5)
        xh = x.astype(jnp.float16)
        q = (xh @ wq.astype(jnp.float16) + bq.astype(jnp.float16)).reshape(b, s, NUM_HEADS, HEAD_DIM)
        k = (xh @ wk.astype(jnp.float16) + bk.astype(jnp.float16)).reshape(b, s, NUM_GROUPS, HEAD_DIM)
        v = (xh @ wv.astype(jnp.float16) + bv.astype(jnp.float16)).reshape(b, s, NUM_GROUPS, HEAD_DIM)
        q = _rmsnorm(q, q_norm_scale)
        k = _rmsnorm(k, k_norm_scale)
        pos = jnp.arange(s)
        cos, sin = _rope_tables(pos)
        cos = cos[:, None, :]
        sin = sin[:, None, :]
        q = _apply_rope(q, cos, sin) * head_scale
        k = _apply_rope(k, cos, sin)
        q = q.astype(jnp.float16)
        k = k.astype(jnp.float16)
        v = v.astype(jnp.float16)
        qg = q.reshape(b, s, NUM_GROUPS, rep, HEAD_DIM)
        logits = jnp.einsum('btgrh,bsgh->bgrts', qg, k, preferred_element_type=jnp.float32) * head_scale
        causal = pos[:, None] >= pos[None, :]
        logits = jnp.where(causal[None, None, None, :, :], logits, jnp.finfo(jnp.float32).min)
        probs = jax.nn.softmax(logits, axis=-1).astype(jnp.float16)
        out = jnp.einsum('bgrts,bsgh->btgrh', probs, v)
        out = out.reshape(b, s, d)
        return out @ wo.astype(jnp.float16) + bo.astype(jnp.float16)

    def _L0_attn_b_ref(hidden_states, Wq, Wk, Wv, Wo, bank_weights, memories, memory_norms):
        import jax, jax.numpy as jnp
        import numpy as np
        B, S, HID = (4, 512, 256)
        H, NB = (16, 4)
        D = HID // H
        EPS = 1e-06

        def elu_plus_one(x):
            return jax.nn.elu(x) + 1.0

        def _reference_tuple_inner(hidden_states, Wq, Wk, Wv, Wo, bank_weights, memories, memory_norms):
            b, s, _ = hidden_states.shape

            def proj(W):
                return (hidden_states @ W.T).reshape(b, s, H, D).transpose(0, 2, 1, 3)
            q, k, v = (proj(Wq), proj(Wk), proj(Wv))
            sigma_q = elu_plus_one(q)
            a_unnorm = jnp.einsum('bhsd,nhde->nbhse', sigma_q, memories)
            norm = jnp.einsum('bhsd,nhd->nbhs', sigma_q, memory_norms)
            a = a_unnorm / jnp.clip(norm, EPS, None)[..., None]
            active = (memory_norms.sum(axis=(1, 2)) >= EPS).astype(a.dtype)
            a = a * active[:, None, None, None, None]
            weights = jax.nn.softmax(bank_weights, axis=-1)
            combined = jnp.einsum('nbhse,hn->bhse', a, weights)
            sigma_k = elu_plus_one(k)
            mem0, norm0 = (memories[0], memory_norms[0])
            retr = jnp.einsum('bhsd,hde->bhse', sigma_k, mem0)
            knorm = jnp.clip(jnp.einsum('bhsd,hd->bhs', sigma_k, norm0), EPS, None)
            delta_v = v - retr / knorm[..., None]
            mem_update = jnp.einsum('bhsd,bhse->hde', sigma_k, delta_v) / (b * s)
            new_mem0 = jax.lax.stop_gradient(mem0 + mem_update)
            new_norm0 = jax.lax.stop_gradient(norm0 + sigma_k.sum(axis=(0, 2)) / b)
            out = combined.transpose(0, 2, 1, 3).reshape(b, s, HID) @ Wo.T
            return (out, new_mem0, new_norm0)
        return _reference_tuple_inner(hidden_states, Wq, Wk, Wv, Wo, bank_weights, memories, memory_norms)[0]

    def _L0_ffn_ref(x, Wr, Wg, Wu, Wd):
        import jax, jax.numpy as jnp
        import numpy as np
        H = 256
        I = 176
        E = 8
        K = 2
        B, S = (2, 256)
        router_logits = jnp.einsum('bsh,he->bse', x, Wr)
        probs = jax.nn.softmax(router_logits.astype(jnp.float32), axis=-1)
        topk_w, topk_idx = jax.lax.top_k(probs, K)
        topk_w = topk_w / jnp.sum(topk_w, axis=-1, keepdims=True)
        onehot = jax.nn.one_hot(topk_idx, E, dtype=topk_w.dtype)
        combine = jnp.einsum('bsk,bske->bse', topk_w, onehot)
        g = jnp.einsum('bsh,ehi->besi', x, Wg)
        u = jnp.einsum('bsh,ehi->besi', x, Wu)
        h = jax.nn.silu(g) * u
        y = jnp.einsum('besi,eih->besh', h, Wd)
        out = jnp.einsum('bse,besh->bsh', combine.astype(x.dtype), y)
        return out
    x = L0_attn_a_x
    x = x + _L0_attn_a_ref(_layernorm(x, axis=-1), L0_attn_a_wq, L0_attn_a_bq, L0_attn_a_wk, L0_attn_a_bk, L0_attn_a_wv, L0_attn_a_bv, L0_attn_a_wo, L0_attn_a_bo, L0_attn_a_q_norm_scale, L0_attn_a_k_norm_scale)
    x = x + _L0_ffn_ref(_layernorm(x, axis=-1), L0_ffn_Wr, L0_ffn_Wg, L0_ffn_Wu, L0_ffn_Wd)
    x = x + _L0_attn_b_ref(_layernorm(x, axis=-1), L0_attn_b_Wq, L0_attn_b_Wk, L0_attn_b_Wv, L0_attn_b_Wo, L0_attn_b_bank_weights, L0_attn_b_memories, L0_attn_b_memory_norms)
    x = x + _L0_ffn_ref(_layernorm(x, axis=-1), L0_ffn_Wr, L0_ffn_Wg, L0_ffn_Wu, L0_ffn_Wd)
    return x

_drawn_inputs = setup_inputs


def setup_inputs(seed=0):
    import zlib

    import numpy as np

    out = dict(_drawn_inputs(seed))
    spreads = {'L0_attn_a_bq': (0.0, 2.0),
     'L0_attn_a_bk': (0.0, 2.0),
     'L0_attn_a_bv': (0.0, 0.1),
     'L0_attn_a_bo': (0.0, 0.1),
     'L0_attn_a_q_norm_scale': (1.0, 0.6),
     'L0_attn_a_k_norm_scale': (1.0, 0.6)}
    factors = {'L0_attn_a_wq': 35.127, 'L0_attn_a_wk': 26.92, 'L0_attn_b_bank_weights': 36.445}
    for name, (base, spread) in spreads.items():
        noise = np.random.default_rng([zlib.crc32(name.encode()), seed]).standard_normal(out[name].shape)
        drawn = base * np.exp(spread * noise) if base else spread * noise
        out[name] = jnp.asarray(drawn.astype(out[name].dtype))
    for name, factor in factors.items():
        out[name] = (out[name] * factor).astype(out[name].dtype)
    return out
```

```python
from contextlib import ExitStack

import numpy as np

import concourse.bass as bass
from concourse import mybir

ALU = mybir.AluOpType
ACT = mybir.ActivationFunctionType
AX = mybir.AxisListType
F32 = mybir.dt.float32
F32R = mybir.dt.float32r
F16 = mybir.dt.float16
BF16 = mybir.dt.bfloat16
U32 = mybir.dt.uint32

P = 128
B, S, D = 4, 512, 256
NT = S // P
KC = D // P
NH, NG, HD = 16, 4, 16
REP = NH // NG
QKV = D + 2 * NG * HD
NQK = NH + NG
QROW = 32
SHIFT = 16.0
NE, FI = 8, 176
FT = NE * FI
NJ = FT // P
MH, NB = 16, 4
MD = D // MH
HP = P // MD
LN_EPS, RMS_EPS, MEM_EPS = 1e-5, 1e-6, 1e-6
MASKED = -1e30
ATT_SCALE = HD ** -0.5
NS = 3


def first_pass_units():
    return [(i, r, n) for i, n in ((3, 1), (2, 1), (1, 2), (0, 4)) for r in range(0, REP, n)]


def second_pass_units():
    return [(0, 0, 2, 1), (0, 2, 2, 1), (1, 0, 2, 1), (1, 2, 2, 1), (2, 0, 4, 2), (3, 0, 4, 4)]


U1, U2 = first_pass_units(), second_pass_units()
N1, N2 = len(U1), len(U2)


def build(nc, x, wqkv, bqkv, nscale, nscale_sw, cos, sin, wo, bo, wr, wg, wu, wd, mwq, mwo, mem,
          mnorm, mnorm_all, bank, ident, mask, headmask, iota, selc, selr, out):
    x_v = x.rearrange("b (i p) c -> b p i c", p=P)
    out_v = out.rearrange("b (i p) c -> b p i c", p=P)
    with ExitStack() as ctx:
        setup = ctx.enter_context(ExitStack())

        def sb(name, shape, dt=F32, only=ctx):
            return only.enter_context(nc.sbuf_tensor(name, shape, dt))

        sems = []

        def sem(name):
            sems.append(ctx.enter_context(nc.semaphore(name)))
            return sems[-1]

        ident_f = sb("ident_f", [P, P])
        ident_h = sb("ident_h", [P, P], F16)
        ident_b = sb("ident_b", [P, P], BF16)
        mask_b = sb("mask_b", [P, P], BF16)
        iota_s = sb("iota_s", [P, NE])
        wqkv_h = sb("wqkv_h", [P, KC, QKV], F16)
        bqkv_h = sb("bqkv_h", [P, QKV], F16)
        rope = sb("rope", [P, 2, 2, NT, HD])
        wo_h = sb("wo_h", [P, KC, D], F16)
        bo_h = sb("bo_h", [P, D], F16)
        whi = sb("whi", [P, 3, KC * FT], F32R)
        wlo = sb("wlo", [P, 3, KC * FT], F32R)
        gate_hi, gate_lo = (w[:, 0, :].rearrange("p (k f) -> p k f", k=KC) for w in (whi, wlo))
        up_hi, up_lo = (w[:, 1, :].rearrange("p (k f) -> p k f", k=KC) for w in (whi, wlo))
        down_hi, down_lo = (w[:, 2, :].rearrange("p (j c) -> p j c", j=NJ) for w in (whi, wlo))
        wr_hi = sb("wr_hi", [P, KC, NE], F32R)
        wr_lo = sb("wr_lo", [P, KC, NE], F32R)
        mwq_hi = sb("mwq_hi", [P, KC, D], F32R)
        mwq_lo = sb("mwq_lo", [P, KC, D], F32R)
        norm_hi = sb("norm_hi", [P, KC, 2 * NB * MH], F32R)
        norm_lo = sb("norm_lo", [P, KC, 2 * NB * MH], F32R)
        comb_hi = sb("comb_hi", [P, KC, NB, D], F32R)
        comb_lo = sb("comb_lo", [P, KC, NB, D], F32R)
        selc_r = sb("selc_r", [2 * NE, FT], F32R)
        selr_r = sb("selr_r", [P, NB, KC, P], F32R)
        mhalf = sb("mhalf", [P, NT])
        vaug = sb("vaug", [P, NT, NG, HD + 1], F16)
        qa = sb("qa", [P, NT, NH, QROW], F16)
        ka = sb("ka", [P, NT, NG, QROW], F16)
        kbd = sb("kbd", [P, NG, REP, S], F16)

        mask_f = sb("mask_f", [P, P], only=setup)
        headmask_s = sb("headmask_s", [P, HP], only=setup)
        wqkv_f = sb("wqkv_f", [P, KC, QKV], only=setup)
        bqkv_f = sb("bqkv_f", [P, QKV], only=setup)
        nscale_s = sb("nscale_s", [P, 2, 2, HD], only=setup)
        cos_s = sb("cos_s", [P, 2, NT, HD], only=setup)
        wo_f = sb("wo_f", [P, KC, D], only=setup)
        bo_f = sb("bo_f", [P, D], only=setup)
        wstage = sb("wstage", [P, 3, KC * FT], only=setup)
        wr_f = sb("wr_f", [P, KC, NE], only=setup)
        mwq_f = sb("mwq_f", [P, KC, D], only=setup)
        mwo_f = sb("mwo_f", [P, KC, D], only=setup)
        mem_f = sb("mem_f", [P, NB, KC, MD], only=setup)
        mem_bd = sb("mem_bd", [P, NB, KC, P], only=setup)
        mnorm_f = sb("mnorm_f", [P, KC, NB], only=setup)
        norm_f = sb("norm_f", [P, KC, 2, NB, MH], only=setup)
        mnall = sb("mnall", [P, NB, MH * MD], only=setup)
        mnsum = sb("mnsum", [P, NB], only=setup)
        bank_s = sb("bank_s", [P, KC, NB], only=setup)
        bmax = sb("bmax", [P, KC], only=setup)
        bsum = sb("bsum", [P, KC], only=setup)
        bankw = sb("bankw", [P, KC, NB], only=setup)
        comb_f = sb("comb_f", [P, KC, NB, D], only=setup)
        selc_f = sb("selc_f", [2 * NE, FT], only=setup)
        selr_f = sb("selr_f", [P, NB, KC, P], only=setup)

        PS = ctx.enter_context(nc.psum_tensor("PS", [P, 8, 512], F32))

        def bank16(n):
            return PS[:, n, :].bitcast(F16)

        BA, BB, BO, BT = (0, 1), (2, 4), 6, 7
        BG, BU, BC, BY = (0, 1), (2, 3), (4, 5), (6, 7)

        k_loaded = sem("k_loaded")
        k_a, k_v, k_p, k_pe = sem("k_a"), sem("k_v"), sem("k_p"), sem("k_pe")
        x_loaded = sem("x_loaded")
        var_ready, rstd_ready = sem("var_ready"), sem("rstd_ready")
        xh_ready, xhT_made, xhT_ready = sem("xh_ready"), sem("xhT_made"), sem("xhT_ready")
        qkv_made, qkv_rounded = sem("qkv_made"), sem("qkv_rounded")
        qk_biased, v_ready, qk_squared = sem("qk_biased"), sem("v_ready"), sem("qk_squared")
        ms_ready, y0_ready, qk_normed = sem("ms_ready"), sem("y0_ready"), sem("qk_normed")
        sin_made, cos_made = sem("sin_made"), sem("cos_made")
        q_rotated, k_rotated, shift_cleared = sem("q_rotated"), sem("k_rotated"), sem("shift_cleared")
        kT_made, kT_ready, kbd_v, kbd_p = sem("kT_made"), sem("kT_ready"), sem("kbd_v"), sem("kbd_p")
        qT1_made, qT1_ready = sem("qT1_made"), sem("qT1_ready")
        scores1_made, max_taken, shift_ready = sem("scores1_made"), sem("max_taken"), sem("shift_ready")
        qT2_made, qT2_ready = sem("qT2_made"), sem("qT2_ready")
        scores2_made, prob_ready, prob_used = sem("scores2_made"), sem("prob_ready"), sem("prob_used")
        o_made, o_ready = sem("o_made"), sem("o_ready")
        oT_made, oT_ready, att_made, att_rounded = sem("oT_made"), sem("oT_ready"), sem("att_made"), sem("att_rounded")
        att_biased, xr_ready = sem("att_biased"), sem("xr_ready")
        dve_step, act_step = sem("dve_step"), sem("act_step")
        nvar_ready, nrstd_ready = sem("nvar_ready"), sem("nrstd_ready")
        xn_ready, xT_made, xT_hi_ready, xT_lo_ready = sem("xn_ready"), sem("xT_made"), sem("xT_hi_ready"), sem("xT_lo_ready")
        logits_made, gap_ready, e2_ready = sem("logits_made"), sem("gap_ready"), sem("e2_ready")
        c_ready, cT_made, cT_ready = sem("c_ready"), sem("cT_made"), sem("cT_ready")
        gate_made, up_made, cb_made = sem("gate_made"), sem("up_made"), sem("cb_made")
        silu_ready, scaled, h_ready = sem("silu_ready"), sem("scaled"), sem("h_ready")
        hi_ready, lo_ready, h_used = sem("hi_ready"), sem("lo_ready"), sem("h_used")
        y_made = sem("y_made")
        mq_made, mexp_ready, sq_ready = sem("mq_made"), sem("mexp_ready"), sem("sq_ready")
        sq_hi_ready, sq_lo_ready = sem("sq_hi_ready"), sem("sq_lo_ready")
        norm_made, rr_ready, rb_made = sem("norm_made"), sem("rr_ready"), sem("rb_made")
        stored = sem("stored")

        def step(eng, signal, counts, ins):
            counts[0] += 1
            ins.then_inc(signal, 1)
            eng.wait_ge(signal, counts[0])

        def heads(t, h0, h1):
            return t.rearrange("p (i h) d -> p i h d", i=NT)[:, :, h0:h1]

        def turn(n, q, nh):
            return rope[:, n, q].unsqueeze(2).to_broadcast([P, NT, nh, HD])

        def clear():
            nums = [s.num for s in sems]
            assert max(nums) - min(nums) == len(nums) - 1
            nc.sync.sem_clear(range(min(nums), max(nums) + 1))
            nc.all_engine_barrier()

        with nc.Block() as block:
            loads = [
                (ident_f[:], ident), (mask_f[:], mask), (headmask_s[:], headmask), (iota_s[:], iota),
                (wqkv_f[:], wqkv.rearrange("(k p) n -> p k n", p=P)), (bqkv_f[:], bqkv),
                (nscale_s[:, 0], nscale), (nscale_s[:, 1], nscale_sw),
                (cos_s[:, 0], cos), (cos_s[:, 1], sin),
                (wo_f[:], wo.rearrange("(k p) n -> p k n", p=P)), (bo_f[:], bo),
                (wr_f[:], wr.rearrange("(k p) n -> p k n", p=P)),
                (mwq_f[:], mwq.rearrange("(k p) n -> p k n", p=P)),
                (mwo_f[:], mwo.rearrange("(k p) n -> p k n", p=P)),
                (mem_f[:], mem), (mnorm_f[:], mnorm), (mnall[:], mnorm_all), (bank_s[:], bank),
                (selc_f[:], selc), (selr_f[:], selr),
                (wstage[:, 0].rearrange("p (k f) -> p k f", k=KC), wg.rearrange("(k p) f -> p k f", p=P)),
                (wstage[:, 1].rearrange("p (k f) -> p k f", k=KC), wu.rearrange("(k p) f -> p k f", p=P)),
                (wstage[:, 2].rearrange("p (j c) -> p j c", j=NJ), wd.rearrange("(j p) c -> p j c", p=P)),
            ]

            @block.sync
            def _(sp):
                for dst, src in loads:
                    sp.dma_start(dst, src).then_inc(k_loaded, 16)

            @block.gpsimd
            def _(pool):
                pool.memset(mhalf[:], -0.5)
                pool.memset(vaug[:], 1.0)
                pool.memset(qa[:], 0.0)
                pool.memset(kbd[:], 0.0)
                pool.memset(ka[:], 0.0).then_inc(k_p, 1)
                pool.wait_ge(k_p, 1)
                pool.memset(ka[:, :, :, HD:HD + 2], SHIFT)
                pool.wait_ge(k_loaded, 16 * len(loads))
                pool.wait_ge(k_v, 1)
                for n in range(2):
                    for q in range(2):
                        pool.tensor_tensor(rope[:, n, q], cos_s[:, n],
                                           nscale_s[:, n, q].unsqueeze(1).to_broadcast([P, NT, HD]), ALU.mult)
                pool.wait_ge(k_a, 1)
                for n in range(3):
                    pool.tensor_tensor(wlo[:, n], wstage[:, n], whi[:, n].bitcast(F32), ALU.subtract)

            @block.scalar
            def _(act):
                act.wait_ge(k_loaded, 16 * len(loads))
                act.activation(whi[:], wstage[:], ACT.Copy).then_inc(k_a, 1)
                act.activation(wqkv_h[:], wqkv_f[:], ACT.Copy)
                act.activation(bqkv_h[:], bqkv_f[:], ACT.Copy)
                act.activation(wo_h[:], wo_f[:], ACT.Copy)
                act.activation(bo_h[:], bo_f[:], ACT.Copy)
                act.activation(ident_h[:], ident_f[:], ACT.Copy)
                act.activation(ident_b[:], ident_f[:], ACT.Copy)
                act.activation(mask_b[:], mask_f[:], ACT.Copy)
                act.activation(selc_r[:], selc_f[:], ACT.Copy)
                act.activation(selr_r[:], selr_f[:], ACT.Copy)
                act.wait_ge(k_v, 3)
                act.activation(bankw[:], bank_s[:], ACT.Exp).then_inc(k_a, 1)

            @block.tensor
            def _(pe):
                pe.wait_ge(k_v, 2)
                for kc in range(KC):
                    for n in range(NB):
                        mm = pe.matmul(PS[:, n, kc * D:(kc + 1) * D], mem_bd[:, n, kc], mwo_f[:, kc],
                                       start=True, stop=True)
                mm.then_inc(k_pe, 1)

            @block.vector
            def _(dve):
                n_step = [0]
                link = lambda ins: step(dve, dve_step, n_step, ins)
                dve.wait_ge(k_loaded, 16 * len(loads))
                dve.tensor_scalar(nscale_s[:, :, 0], nscale_s[:, :, 0], ATT_SCALE, None,
                                  ALU.mult).then_inc(k_v, 1)
                dve.tensor_tensor(
                    mem_bd[:].rearrange("p n k (h d) -> p (n k) h d", h=HP),
                    mem_f[:].rearrange("p n k d -> p (n k) d").unsqueeze(2).to_broadcast([P, NB * KC, HP, MD]),
                    headmask_s[:].unsqueeze(1).unsqueeze(3).to_broadcast([P, NB * KC, HP, MD]),
                    ALU.mult).then_inc(k_v, 1)
                link(dve.tensor_reduce(bmax[:], bank_s[:], AX.X, ALU.max))
                dve.tensor_tensor(bank_s[:], bank_s[:], bmax[:].unsqueeze(2).to_broadcast([P, KC, NB]),
                                  ALU.subtract).then_inc(k_v, 1)
                link(dve.memset(norm_f[:], 0.0))
                for kc in range(KC):
                    for dup in range(2):
                        last = dve.tensor_tensor(
                            norm_f[:, kc, dup, :, kc * HP:(kc + 1) * HP],
                            mnorm_f[:, kc].unsqueeze(2).to_broadcast([P, NB, HP]),
                            headmask_s[:].unsqueeze(1).to_broadcast([P, NB, HP]), ALU.mult)
                link(last)
                link(dve.tensor_reduce(mnsum[:], mnall[:], AX.X, ALU.add))
                link(dve.tensor_scalar(mnsum[:], mnsum[:], MEM_EPS, None, ALU.is_ge))
                for f, hi, lo in ((norm_f[:].rearrange("p k u n h -> p k (u n h)"), norm_hi, norm_lo),
                                  (wr_f[:], wr_hi, wr_lo), (mwq_f[:], mwq_hi, mwq_lo)):
                    link(dve.tensor_copy(hi[:], f))
                    link(dve.tensor_tensor(lo[:], f, hi[:].bitcast(F32), ALU.subtract))
                dve.wait_ge(k_a, 2)
                link(dve.tensor_reduce(bsum[:], bankw[:], AX.X, ALU.add))
                link(dve.reciprocal(bsum[:], bsum[:]))
                link(dve.tensor_tensor(bankw[:], bankw[:], bsum[:].unsqueeze(2).to_broadcast([P, KC, NB]),
                                       ALU.mult))
                link(dve.tensor_tensor(bankw[:], bankw[:], mnsum[:].unsqueeze(1).to_broadcast([P, KC, NB]),
                                       ALU.mult))
                dve.wait_ge(k_pe, 1)
                for kc in range(KC):
                    for n in range(NB):
                        ins = dve.tensor_scalar(comb_f[:, kc, n], PS[:, n, kc * D:(kc + 1) * D],
                                                bankw[:, kc, n:n + 1], None, ALU.mult)
                link(ins)
                link(dve.tensor_copy(comb_hi[:], comb_f[:]))
                dve.tensor_tensor(comb_lo[:], comb_f[:], comb_hi[:].bitcast(F32), ALU.subtract)
        clear()

        setup.close()
        xin = sb("xin", [P, NT, D])
        stats = sb("stats", [P, NT, 6])
        mv = sb("mv", [P, NT, 2])
        veps = sb("veps", [P, NT])
        rstd = sb("rstd", [P, NT])
        xh = sb("xh", [P, NT, D], F16)
        xhT = sb("xhT", [P, KC, S], F16)
        qkv16 = sb("qkv16", [P, NT, QKV], F16)
        qk16 = sb("qk16", [P, NT, NQK * HD], F16)
        sq = sb("sq", [P, NT * NQK, HD])
        ms = sb("ms", [P, NT * NQK])
        msv = sb("msv", [P, NT * NQK])
        lnv = sb("lnv", [P, NT * NQK])
        y0 = sb("y0", [P, NT * NQK])
        y1 = sb("y1", [P, NT * NQK])
        rota = sq
        rotb = sb("rotb", [P, NT * NQK, HD])
        kT = sb("kT", [P, S], F16)
        qT1 = sb("qT1", [P, NG, S], F16)
        qT2 = sb("qT2", [P, 2, S], F16)
        smax = sb("smax", [P, NT, NH])
        NP_ = 4
        prob = sb("prob", [P, NP_, 2 * S], F16)
        qkn = prob[:].rearrange("p n s -> p (n s)").bitcast(F32)[:, 0:NT * NQK * HD]\
            .rearrange("p (h d) -> p h d", d=HD)
        rsum = sb("rsum", [P, NT, REP])
        o16, oT = xh, xhT
        y16 = qkv16[:].rearrange("p i n -> p (i n)")[:, 0:NT * D].rearrange("p (i c) -> p i c", i=NT)

        xr = sb("xr", [P, NT, D])
        xT_hi = sb("xT_hi", [P, KC, S], F32R)
        xT_lo = sb("xT_lo", [P, KC, S], F32R)
        lg = sb("lg", [P, NT, NE])
        top8 = sb("top8", [P, NT, 8])
        tidx = sb("tidx", [P, NT, 8], U32)
        tidf = sb("tidf", [P, NT, 8])
        gap = sb("gap", [P, NT])
        e2 = sb("e2", [P, NT])
        w12 = sb("w12", [P, 2, NT])
        ceq = sb("ceq", [P, 2, NT, NE])
        cw = sb("cw", [P, NT, NE])
        chl = sb("chl", [P, NT, 2 * NE], F32R)
        RH = 2
        sg = sb("sg", [P, RH, S])
        xn = sg[:].rearrange("p a s -> p (a s)").rearrange("p (i c) -> p i c", i=NT)
        mexp = sg
        sc = sb("sc", [P, RH, S])
        mrelu = sc
        hf = sb("hf", [P, RH, S])
        hhi = sb("hhi", [P, RH, S], F32R)
        hlo = sb("hlo", [P, RH, S], F32R)
        sq_f = sb("sq_f", [P, KC, S])
        sq_hi, sq_lo = hhi, hlo
        nrec = sb("nrec", [P, S])
        rr = sb("rr", [P, S], F32R)
        cT = rr[0:2 * NE]

        with nc.Fori(0, B) as b:
            with nc.Block() as block:

                @block.sync
                def _(sp):
                    sp.dma_start(xin[:], x_v[bass.ds(b, 1)].rearrange("a p i c -> (a p) i c")).then_inc(x_loaded, 16)
                    sp.wait_ge(xr_ready, 1 + NS)
                    sp.dma_start(out_v[bass.ds(b, 1)].rearrange("a p i c -> (a p) i c"), xr[:]).then_inc(stored, 16)
                    sp.wait_ge(stored, 16)

                @block.gpsimd
                def _(pool):
                    pool.memset(qa[:, :, :, HD:HD + 2], 0.0).then_inc(shift_cleared, 1)
                    pool.wait_ge(var_ready, 1)
                    pool.tensor_tensor(rstd[:], veps[:], mhalf[:], ALU.pow).then_inc(rstd_ready, 1)
                    pool.wait_ge(qkv_rounded, NT)
                    pool.tensor_tensor(
                        vaug[:, :, :, 0:HD],
                        qkv16[:, :, D + NG * HD:].rearrange("p i (g d) -> p i g d", g=NG),
                        bqkv_h[:, D + NG * HD:].rearrange("p (g d) -> p g d", g=NG).unsqueeze(1)
                        .to_broadcast([P, NT, NG, HD]), ALU.add).then_inc(v_ready, 1)
                    pool.wait_ge(qk_normed, 1)
                    for q, h0, h1 in ((1, NH, NQK), (0, 0, NH)):
                        for a, z in ((0, HD // 2), (HD // 2, 0)):
                            last = pool.tensor_tensor(
                                heads(rotb[:], h0, h1)[:, :, :, a:a + HD // 2], heads(qkn, h0, h1)[:, :, :, z:z + HD // 2],
                                turn(1, q, h1 - h0)[:, :, :, a:a + HD // 2], ALU.mult)
                    last.then_inc(sin_made, 1)
                    pool.wait_ge(kT_ready, 1)
                    for g in range(NG // 2, NG):
                        for r in range(REP):
                            last = pool.tensor_copy(kbd[r * QROW:(r + 1) * QROW, g, r], kT[g * QROW:(g + 1) * QROW])
                    last.then_inc(kbd_p, 1)

                    def pool_norm(n):
                        pool.wait_ge(nvar_ready, n + 1)
                        pool.tensor_tensor(rstd[:], veps[:], mhalf[:], ALU.pow).then_inc(nrstd_ready, 1)

                    def pool_low(m):
                        pool.wait_ge(hi_ready, m + 1)
                        if m >= RH:
                            pool.wait_ge(h_used, m + 1 - RH)
                        pool.tensor_tensor(hlo[:, m % RH], hf[:, m % RH], hhi[:, m % RH].bitcast(F32),
                                           ALU.subtract).then_inc(lo_ready, 1)

                    pool_norm(0)
                    for j in range(NJ):
                        pool_low(j)
                    pool_norm(1)
                    pool.wait_ge(sq_hi_ready, 1)
                    pool.tensor_tensor(sq_lo[:], sq_f[:], sq_hi[:].bitcast(F32), ALU.subtract).then_inc(sq_lo_ready, 1)
                    for m in range(NB * KC):
                        pool_low(NJ + m)
                    pool_norm(2)
                    for j in range(NJ):
                        pool_low(NJ + NB * KC + j)

                @block.scalar
                def _(act):
                    n_step = [0]
                    link = lambda ins: step(act, act_step, n_step, ins)
                    for i in range(NT):
                        act.wait_ge(qkv_made, i + 1)
                        act.activation(qkv16[:, i], PS[:, BB[0] + i, 0:QKV], ACT.Copy).then_inc(qkv_rounded, 1)
                    act.wait_ge(qk_biased, 1)
                    act.activation(sq[:].rearrange("p h d -> p (h d)"), qk16[:].rearrange("p i n -> p (i n)"),
                                   ACT.Square).then_inc(qk_squared, 1)
                    act.wait_ge(ms_ready, 1)
                    link(act.activation(lnv[:], msv[:], ACT.Ln))
                    act.activation(y0[:], lnv[:], ACT.Exp, scale=-0.5).then_inc(y0_ready, 1)
                    for n in range(2):
                        act.wait_ge(qT1_made, n + 1)
                        act.activation(qT1[:, 2 * n:2 * n + 2].rearrange("p g s -> p (g s)"), bank16((BT, BO)[n]),
                                       ACT.Copy).then_inc(qT1_ready, 1)
                    for g in range(NG):
                        act.wait_ge(qT2_made, g + 1)
                        act.activation(qT2[:, g % 2], bank16(BT)[:, 0:S], ACT.Copy).then_inc(qT2_ready, 1)
                        for n, (j, r0, nr, nb) in enumerate(U2):
                            u = N2 * g + n
                            act.wait_ge(scores2_made, u + 1)
                            if u >= NP_:
                                act.wait_ge(prob_used, u + 1 - NP_)
                            w = S - j * P
                            bank = BB[u % 2]
                            src = PS[:, bank:bank + nr // nb, 0:nb * w]
                            dst = prob[:, u % NP_, 0:nr * w].rearrange("p (a w) -> p a w", a=nr // nb)
                            act.activation(dst, src, ACT.Exp, scale=ATT_SCALE).then_inc(prob_ready, 1)
                    for i in range(NT):
                        act.wait_ge(att_made, i + 1)
                        act.activation(y16[:, i], PS[:, BB[0] + i, 0:D], ACT.Copy).then_inc(att_rounded, 1)

                    def act_xT(n):
                        for kc in range(KC):
                            act.wait_ge(xT_made, KC * n + kc + 1)
                            act.activation(xT_hi[:, kc], PS[:, BG[kc]], ACT.Copy).then_inc(xT_hi_ready, 1)

                    def act_high(m):
                        act.wait_ge(h_ready, m + 1)
                        if m == NJ:
                            act.wait_ge(norm_made, 1)
                        if m >= RH:
                            act.wait_ge(h_used, m + 1 - RH)
                        act.activation(hhi[:, m % RH], hf[:, m % RH], ACT.Copy).then_inc(hi_ready, 1)

                    def act_ffn(f, m0):
                        act.wait_ge(gap_ready, f + 1)
                        act.activation(e2[:], gap[:], ACT.Exp).then_inc(e2_ready, 1)
                        act.wait_ge(cT_made, f + 1)
                        act.activation(cT, PS[0:2 * NE, BC[1]], ACT.Copy).then_inc(cT_ready, 1)
                        for j in range(NJ):
                            q = NJ * f + j
                            act.wait_ge(gate_made, q + 1)
                            if q >= RH:
                                act.wait_ge(scaled, q + 1 - RH)
                            act.activation(sg[:, q % RH], PS[:, BG[q % 2]], ACT.Silu).then_inc(silu_ready, 1)
                            if j >= 1:
                                act_high(m0 + j - 1)
                        act_high(m0 + NJ - 1)

                    act_xT(0)
                    act_ffn(0, 0)
                    act_xT(1)
                    for kc in range(KC):
                        act.wait_ge(mq_made, kc + 1)
                        act.activation(mexp[:, kc], PS[:, BU[kc]], ACT.Exp)
                        act.activation(mrelu[:, kc], PS[:, BU[kc]], ACT.Relu).then_inc(mexp_ready, 1)
                    act.wait_ge(sq_ready, 1)
                    act.activation(sq_hi[:], sq_f[:], ACT.Copy).then_inc(sq_hi_ready, 1)
                    for m in range(NB * KC):
                        act_high(NJ + m)
                    act_xT(2)
                    act_ffn(1, NJ + NB * KC)

                @block.vector
                def _(dve):
                    n_step = [0]
                    link = lambda ins: step(dve, dve_step, n_step, ins)

                    def dve_stats(src):
                        for i in range(NT):
                            last = dve.bn_stats(stats[:, i], src[:, i])
                        link(last)
                        for i in range(NT):
                            last = dve.bn_aggr(mv[:, i], stats[:, i])
                        link(last)
                        return dve.tensor_scalar(veps[:], mv[:, :, 1], LN_EPS, None, ALU.add)

                    dve.wait_ge(x_loaded, 16)
                    dve_stats(xin).then_inc(var_ready, 1)
                    dve.wait_ge(rstd_ready, 1)
                    for i in range(NT):
                        dve.tensor_scalar(xh[:, i], xin[:, i], mv[:, i, 0:1], rstd[:, i:i + 1],
                                          ALU.subtract, ALU.mult).then_inc(xh_ready, 1)
                    dve.wait_ge(xhT_made, 1)
                    dve.tensor_copy(xhT[:].rearrange("p k s -> p (k s)"), bank16(BT)).then_inc(xhT_ready, 1)
                    dve.wait_ge(qkv_rounded, NT)
                    dve.tensor_tensor(qk16[:], qkv16[:, :, 0:NQK * HD],
                                      bqkv_h[:, 0:NQK * HD].unsqueeze(1).to_broadcast([P, NT, NQK * HD]),
                                      ALU.add).then_inc(qk_biased, 1)
                    dve.wait_ge(qk_squared, 1)
                    link(dve.tensor_reduce(ms[:], sq[:], AX.X, ALU.add))
                    dve.tensor_scalar(msv[:], ms[:], 1.0 / HD, RMS_EPS, ALU.mult, ALU.add).then_inc(ms_ready, 1)
                    dve.wait_ge(ms_ready, 1)
                    dve.wait_ge(y0_ready, 1)
                    link(dve.scalar_tensor_tensor(y1[:], msv[:], -0.5, y0[:], ALU.mult, ALU.mult))
                    link(dve.tensor_tensor(y1[:], y1[:], y0[:], ALU.mult))
                    link(dve.scalar_tensor_tensor(y1[:], y1[:], 1.5, y0[:], ALU.add, ALU.mult))
                    dve.tensor_tensor(qkn, qk16[:].rearrange("p i (h d) -> p (i h) d", d=HD),
                                      y1[:].unsqueeze(2).to_broadcast([P, NT * NQK, HD]), ALU.mult)\
                       .then_inc(qk_normed, 1)
                    dve.wait_ge(qk_normed, 1)
                    for q, h0, h1 in ((1, NH, NQK), (0, 0, NH)):
                        last = dve.tensor_tensor(heads(rota[:], h0, h1), heads(qkn, h0, h1), turn(0, q, h1 - h0), ALU.mult)
                    last.then_inc(cos_made, 1)
                    dve.wait_ge(cos_made, 1)
                    dve.wait_ge(sin_made, 1)
                    ra = rota[:].rearrange("p (i h) d -> p i h d", i=NT)
                    rb = rotb[:].rearrange("p (i h) d -> p i h d", i=NT)
                    dve.tensor_tensor(ka[:, :, :, 0:HD], ra[:, :, NH:], rb[:, :, NH:], ALU.add).then_inc(k_rotated, 1)
                    dve.tensor_tensor(qa[:, :, :, 0:HD], ra[:, :, 0:NH], rb[:, :, 0:NH], ALU.add).then_inc(q_rotated, 1)
                    dve.wait_ge(kT_made, 1)
                    dve.tensor_copy(kT[:], bank16(BA[0])[:, 0:S]).then_inc(kT_ready, 1)
                    dve.wait_ge(kT_ready, 1)
                    for g in range(NG // 2):
                        for r in range(REP):
                            last = dve.tensor_copy(kbd[r * QROW:(r + 1) * QROW, g, r], kT[g * QROW:(g + 1) * QROW])
                    last.then_inc(kbd_v, 1)

                    def dve_output(g):
                        dve.wait_ge(o_made, g + 1)
                        o = PS[:, BO, 0:NT * REP * (HD + 1)].rearrange("p (i r d) -> p i r d", i=NT, r=REP)
                        link(dve.reciprocal(rsum[:], o[:, :, :, HD]))
                        dve.tensor_tensor(
                            o16[:, :, g * REP * HD:(g + 1) * REP * HD].rearrange("p i (r d) -> p i r d", r=REP),
                            o[:, :, :, 0:HD], rsum[:].unsqueeze(3).to_broadcast([P, NT, REP, HD]),
                            ALU.mult).then_inc(o_ready, 1)

                    for g in range(NG):
                        for n, (i, r0, nr) in enumerate(U1):
                            u = N1 * g + n
                            dve.wait_ge(scores1_made, u + 1)
                            w = (i + 1) * P
                            last = dve.tensor_reduce(
                                smax[:, i, REP * g + r0:REP * g + r0 + nr],
                                PS[:, BA[u % 2], 0:nr * w].rearrange("p (r w) -> p r w", r=nr),
                                AX.X, ALU.max)
                            last.then_inc(max_taken, 1)
                        dve.wait_ge(max_taken, N1 * (g + 1))
                        if g == 0:
                            dve.wait_ge(qT1_made, 2)
                        hs = slice(REP * g, REP * g + REP)
                        link(dve.tensor_scalar(qa[:, :, hs, HD], smax[:, :, hs], -1.0 / SHIFT, None, ALU.mult))
                        dve.scalar_tensor_tensor(qa[:, :, hs, HD + 1], smax[:, :, hs], -1.0 / SHIFT, qa[:, :, hs, HD],
                                                 ALU.mult, ALU.subtract).then_inc(shift_ready, 1)
                        if g >= 1:
                            dve_output(g - 1)
                    dve_output(NG - 1)
                    dve.wait_ge(oT_made, 1)
                    dve.tensor_copy(oT[:].rearrange("p k s -> p (k s)"), bank16(BT)).then_inc(oT_ready, 1)
                    dve.wait_ge(att_rounded, NT)
                    link(dve.tensor_tensor(y16, y16, bo_h[:].unsqueeze(1).to_broadcast([P, NT, D]), ALU.add))
                    dve.tensor_tensor(xr[:], xin[:], y16, ALU.add).then_inc(xr_ready, 1)

                    def dve_norm(n):
                        dve.wait_ge(xr_ready, n + 1)
                        dve_stats(xr).then_inc(nvar_ready, 1)
                        dve.wait_ge(nrstd_ready, n + 1)
                        for i in range(NT):
                            dve.tensor_scalar(xn[:, i], xr[:, i], mv[:, i, 0:1], rstd[:, i:i + 1],
                                              ALU.subtract, ALU.mult).then_inc(xn_ready, 1)
                        for kc in range(KC):
                            dve.wait_ge(xT_hi_ready, KC * n + kc + 1)
                            dve.tensor_tensor(xT_lo[:, kc], PS[:, BG[kc]], xT_hi[:, kc].bitcast(F32),
                                              ALU.subtract).then_inc(xT_lo_ready, 1)

                    def dve_router(f):
                        dve.wait_ge(logits_made, f + 1)
                        link(dve.tensor_copy(lg[:], PS[:, BC[0], 0:NT * NE].rearrange("p (i e) -> p i e", i=NT)))
                        for i in range(NT):
                            last = dve.max(top8[:, i], lg[:, i])
                        link(last)
                        for i in range(NT):
                            last = dve.max_index(tidx[:, i], top8[:, i], lg[:, i])
                        dve.tensor_tensor(gap[:], top8[:, :, 1], top8[:, :, 0], ALU.subtract).then_inc(gap_ready, 1)
                        link(last)
                        link(dve.tensor_copy(tidf[:], tidx[:]))
                        for k in range(2):
                            last = dve.tensor_tensor(
                                ceq[:, k], iota_s[:].unsqueeze(1).to_broadcast([P, NT, NE]),
                                tidf[:, :, k:k + 1].to_broadcast([P, NT, NE]), ALU.is_equal)
                        dve.wait_ge(e2_ready, f + 1)
                        link(dve.tensor_scalar(w12[:, 1], e2[:], 1.0, None, ALU.add))
                        link(dve.reciprocal(w12[:, 0], w12[:, 1]))
                        link(dve.tensor_tensor(w12[:, 1], w12[:, 0], e2[:], ALU.mult))
                        link(dve.tensor_tensor(ceq[:].rearrange("p k i e -> p (k i) e"),
                                               ceq[:].rearrange("p k i e -> p (k i) e"),
                                               w12[:].rearrange("p k i -> p (k i)").unsqueeze(2)
                                               .to_broadcast([P, 2 * NT, NE]), ALU.mult))
                        link(dve.tensor_tensor(cw[:], ceq[:, 0], ceq[:, 1], ALU.add))
                        link(dve.tensor_copy(chl[:, :, 0:NE], cw[:]))
                        dve.tensor_tensor(chl[:, :, NE:], cw[:], chl[:, :, 0:NE].bitcast(F32),
                                          ALU.subtract).then_inc(c_ready, 1)

                    def dve_ffn(f, m0):
                        for j in range(NJ):
                            q, m = NJ * f + j, m0 + j
                            dve.wait_ge(silu_ready, q + 1)
                            dve.wait_ge(cb_made, q + 1)
                            dve.tensor_tensor(sc[:, q % RH], sg[:, q % RH], PS[:, BC[q % 2]], ALU.mult)\
                               .then_inc(scaled, 1)
                            dve.wait_ge(scaled, q + 1)
                            dve.wait_ge(up_made, q + 1)
                            if m >= RH:
                                dve.wait_ge(lo_ready, m + 1 - RH)
                            dve.tensor_tensor(hf[:, m % RH], sc[:, q % RH], PS[:, BU[q % 2]], ALU.mult)\
                               .then_inc(h_ready, 1)

                    def dve_residual(n):
                        dve.wait_ge(y_made, n + 1)
                        for k in range(2):
                            last = dve.tensor_tensor(
                                xr[:, 2 * k:2 * k + 2], xr[:, 2 * k:2 * k + 2],
                                PS[:, BY[k]].rearrange("p (i c) -> p i c", i=2), ALU.add)
                        last.then_inc(xr_ready, 1)

                    def dve_memory(m0):
                        for kc in range(KC):
                            dve.wait_ge(mexp_ready, kc + 1)
                            last = dve.scalar_tensor_tensor(sq_f[:, kc], mexp[:, kc], 1.0, mrelu[:, kc],
                                                            ALU.min, ALU.add)
                        last.then_inc(sq_ready, 1)
                        dve.wait_ge(sq_ready, 1)
                        dve.wait_ge(norm_made, 1)
                        link(dve.tensor_scalar(nrec[:], PS[:, BC[0]], MEM_EPS, None, ALU.max))
                        link(dve.reciprocal(nrec[:], nrec[:]))
                        link(dve.tensor_copy(rr[:], nrec[:]))
                        h = slice(NB * MH, 2 * NB * MH)
                        dve.tensor_tensor(rr[h], nrec[h], rr[h].bitcast(F32), ALU.subtract).then_inc(rr_ready, 1)
                        for m in range(NB * KC):
                            dve.wait_ge(rb_made, m + 1)
                            dve.wait_ge(lo_ready, m0 + m + 1 - RH)
                            dve.tensor_tensor(hf[:, (m0 + m) % RH], sq_f[:, m % KC], PS[:, BG[0] + m % 4],
                                              ALU.mult).then_inc(h_ready, 1)

                    dve_norm(0)
                    dve_router(0)
                    dve_ffn(0, 0)
                    dve_residual(0)
                    dve_norm(1)
                    dve_memory(NJ)
                    dve_residual(1)
                    dve_norm(2)
                    dve_router(1)
                    dve_ffn(1, NJ + NB * KC)
                    dve_residual(2)

                @block.tensor
                def _(pe):
                    for i in range(NT):
                        pe.wait_ge(xh_ready, i + 1)
                        for kc in range(KC):
                            mm = pe.transpose(bank16(BT)[:, kc * S + i * P:kc * S + (i + 1) * P],
                                              xh[:, i, kc * P:(kc + 1) * P], ident_h[:])
                    mm.then_inc(xhT_made, 1)
                    pe.wait_ge(xhT_ready, 1)
                    for i in range(NT):
                        for kc in range(KC):
                            mm = pe.matmul(PS[:, BB[0] + i, 0:QKV], xhT[:, kc, i * P:(i + 1) * P], wqkv_h[:, kc],
                                           start=(kc == 0), stop=(kc == KC - 1))
                        mm.then_inc(qkv_made, 1)
                    pe.wait_ge(k_rotated, 1)
                    for i in range(NT):
                        mm = pe.transpose(bank16(BA[0])[:, i * P:(i + 1) * P],
                                          ka[:, i].rearrange("p g d -> p (g d)"), ident_h[:])
                    mm.then_inc(kT_made, 1)
                    pe.wait_ge(q_rotated, 1)
                    pe.wait_ge(shift_cleared, 1)
                    for g in range(NG):
                        for i in range(NT):
                            mm = pe.transpose(
                                bank16((BT, BO)[g // 2])[:, (g % 2) * S + i * P:(g % 2) * S + (i + 1) * P],
                                qa[:, i, REP * g:REP * (g + 1)].rearrange("p r d -> p (r d)"), ident_h[:])
                        if g % 2:
                            mm.then_inc(qT1_made, 1)
                    pe.wait_ge(kT_ready, 1)
                    pe.wait_ge(kbd_v, 1)
                    pe.wait_ge(kbd_p, 1)
                    pe.wait_ge(qT1_ready, 2)
                    pe.wait_ge(v_ready, 1)

                    def scores_first(g, n):
                        i, r0, nr = U1[n]
                        u, w = N1 * g + n, (i + 1) * P
                        if u >= 2:
                            pe.wait_ge(max_taken, u - 1)
                        o = PS[:, BA[u % 2], 0:nr * w].rearrange("p (r w) -> p r w", r=nr)
                        pe.matmul(o, qT1[:, g, i * P:(i + 1) * P], kbd[:, g, r0:r0 + nr, 0:w],
                                  start=True, stop=False, skip_group_check=True)
                        pe.matmul(o[:, :, i * P:w], ident_b[:], mask_b[:].unsqueeze(1).to_broadcast([P, nr, P]),
                                  start=False, stop=True, skip_group_check=True).then_inc(scores1_made, 1)

                    def shifted(g):
                        pe.wait_ge(shift_ready, g + 1)
                        if g >= 1:
                            pe.wait_ge(qT2_ready, g)
                        for i in range(NT):
                            mm = pe.transpose(bank16(BT)[:, i * P:(i + 1) * P],
                                              qa[:, i, REP * g:REP * (g + 1)].rearrange("p r d -> p (r d)"),
                                              ident_h[:])
                        mm.then_inc(qT2_made, 1)

                    def scores_second(g, n):
                        j, r0, nr, nb = U2[n]
                        u, w = N2 * g + n, S - j * P
                        if n == 0:
                            pe.wait_ge(qT2_ready, g + 1)
                        if u >= 2:
                            pe.wait_ge(prob_ready, u - 1)
                        for k in range(nr):
                            o = PS[:, BB[u % 2] + k // nb, (k % nb) * w:(k % nb + 1) * w]
                            pe.matmul(o, kbd[:, g, r0 + k, j * P:(j + 1) * P], qT2[:, g % 2, j * P:S],
                                      start=True, stop=False, skip_group_check=True)
                            mm = pe.matmul(o[:, 0:P], mask_b[:], ident_b[:], start=False, stop=True,
                                           skip_group_check=True)
                        mm.then_inc(scores2_made, 1)

                    def weighted(g, n):
                        j, r0, nr, nb = U2[n]
                        u, w = N2 * g + n, S - j * P
                        if n == 0:
                            if g == 0:
                                pe.wait_ge(qT1_ready, 2)
                            else:
                                pe.wait_ge(o_ready, g)
                        pe.wait_ge(prob_ready, u + 1)
                        o = PS[:, BO, 0:NT * REP * (HD + 1)].rearrange("p (i r d) -> p i r d", i=NT, r=REP)
                        for k in range(nr):
                            for i in range(j, NT):
                                mm = pe.matmul(o[:, i, r0 + k],
                                               prob[:, u % NP_, k * w + (i - j) * P:k * w + (i - j + 1) * P],
                                               vaug[:, j, g], start=(n == 0 and k == 0 and i == 0), stop=True,
                                               skip_group_check=True)
                        mm.then_inc(prob_used, 1)
                        if n == N2 - 1:
                            pe.wait_ge(prob_used, u + 1)
                            pe.matmul(PS[:, BO, 511:512], ident_b[:, 0:P], ident_b[:, 0:1], start=False, stop=True,
                                      skip_group_check=True).then_inc(o_made, 1)

                    for g in range(NG + 1):
                        second = 0
                        for n in range(N1):
                            if g < NG:
                                scores_first(g, n)
                            if n == 1 and g >= 1:
                                shifted(g - 1)
                            if g >= 1 and n >= 2 and (n % 2 == 0 or n >= 9) and second < N2:
                                scores_second(g - 1, second)
                                if second:
                                    weighted(g - 1, second - 1)
                                second += 1
                        if g >= 1:
                            assert second == N2
                            weighted(g - 1, N2 - 1)

                    pe.wait_ge(o_ready, NG)
                    for i in range(NT):
                        for kc in range(KC):
                            mm = pe.transpose(bank16(BT)[:, kc * S + i * P:kc * S + (i + 1) * P],
                                              o16[:, i, kc * P:(kc + 1) * P], ident_h[:])
                    mm.then_inc(oT_made, 1)
                    pe.wait_ge(oT_ready, 1)
                    for i in range(NT):
                        for kc in range(KC):
                            mm = pe.matmul(PS[:, BB[0] + i, 0:D], oT[:, kc, i * P:(i + 1) * P], wo_h[:, kc],
                                           start=(kc == 0), stop=(kc == KC - 1))
                        mm.then_inc(att_made, 1)

                    def three(outs, pairs, sem_=None):
                        n = 0
                        for (sh, sl), (mh, ml) in pairs:
                            for st, mo in ((sh, mh), (sh, ml), (sl, mh)):
                                n += 1
                                mm = pe.matmul(outs, st, mo, start=(n == 1), stop=(n == 3 * len(pairs)))
                        return mm

                    def pe_xT(n):
                        for kc in range(KC):
                            for i in range(NT):
                                if kc == 0:
                                    pe.wait_ge(xn_ready, NT * n + i + 1)
                                mm = pe.transpose(PS[:, BG[kc], i * P:(i + 1) * P],
                                                  xn[:, i, kc * P:(kc + 1) * P], ident_f[:])
                            mm.then_inc(xT_made, 1)
                        pe.wait_ge(xT_hi_ready, KC * (n + 1))
                        pe.wait_ge(xT_lo_ready, KC * (n + 1))

                    xTs = lambda kc, a, z: (xT_hi[:, kc, a:z], xT_lo[:, kc, a:z])

                    def pe_router(f):
                        for i in range(NT):
                            n = 0
                            for kc in range(KC):
                                for st in xTs(kc, i * P, (i + 1) * P):
                                    for mo in (wr_hi, wr_lo):
                                        n += 1
                                        mm = pe.matmul(PS[:, BC[0], i * NE:(i + 1) * NE], st, mo[:, kc],
                                                       start=(n == 1), stop=(n == 4 * KC))
                        mm.then_inc(logits_made, 1)

                    def pe_up(f, j):
                        q = NJ * f + j
                        if j >= 2:
                            pe.wait_ge(silu_ready, q - 1)
                            pe.wait_ge(h_ready, f * (NJ + NB * KC) + j - 1)
                        cols = slice(j * P, (j + 1) * P)
                        three(PS[:, BG[q % 2]], [((gate_hi[:, kc, cols], gate_lo[:, kc, cols]), xTs(kc, 0, S))
                                                 for kc in range(KC)]).then_inc(gate_made, 1)
                        three(PS[:, BU[q % 2]], [((up_hi[:, kc, cols], up_lo[:, kc, cols]), xTs(kc, 0, S))
                                                 for kc in range(KC)]).then_inc(up_made, 1)

                    def pe_spread(f, j):
                        q = NJ * f + j
                        if j >= 2:
                            pe.wait_ge(scaled, q - 1)
                        pe.matmul(PS[:, BC[q % 2]], selc_r[:, j * P:(j + 1) * P], cT, start=True, stop=True)\
                          .then_inc(cb_made, 1)

                    def pe_accumulate(m, first, last, hi, lo):
                        pe.wait_ge(hi_ready, m + 1)
                        pe.wait_ge(lo_ready, m + 1)
                        for i in range(NT):
                            for k, (st, mo) in enumerate(((hhi, hi), (hhi, lo), (hlo, hi))):
                                mm = pe.matmul(PS[:, BY[i // 2], (i % 2) * D:(i % 2 + 1) * D],
                                               st[:, m % RH, i * P:(i + 1) * P], mo,
                                               start=(first and k == 0 and i % 2 == 0), stop=True,
                                               skip_group_check=True)
                        mm.then_inc(h_used, 1)
                        if last:
                            pe.wait_ge(h_used, m + 1)
                            pe.matmul(PS[0:1, BC[0], 0:1], ident_b[:, 0:1], ident_b[:, 0:1], start=True, stop=True)\
                              .then_inc(y_made, 1)

                    def pe_ffn(f, m0):
                        pe_router(f)
                        pe_up(f, 0)
                        pe_up(f, 1)
                        pe.wait_ge(c_ready, f + 1)
                        for i in range(NT):
                            mm = pe.transpose(PS[0:2 * NE, BC[1], i * P:(i + 1) * P],
                                              chl[:, i].bitcast(F32), ident_f[:])
                        mm.then_inc(cT_made, 1)
                        pe.wait_ge(cT_ready, f + 1)
                        pe_spread(f, 0)
                        pe_spread(f, 1)
                        for j in range(NJ):
                            if j + 2 < NJ:
                                pe_up(f, j + 2)
                                pe_spread(f, j + 2)
                            pe_accumulate(m0 + j, j == 0, j == NJ - 1, down_hi[:, j], down_lo[:, j])

                    def pe_memory(m0):
                        for mc in range(KC):
                            cols = slice(mc * P, (mc + 1) * P)
                            three(PS[:, BU[mc]], [((mwq_hi[:, kc, cols], mwq_lo[:, kc, cols]), xTs(kc, 0, S))
                                                  for kc in range(KC)]).then_inc(mq_made, 1)
                        pe.wait_ge(sq_hi_ready, 1)
                        pe.wait_ge(sq_lo_ready, 1)
                        three(PS[:, BC[0]], [((norm_hi[:, kc], norm_lo[:, kc]), (sq_hi[:, kc], sq_lo[:, kc]))
                                             for kc in range(KC)]).then_inc(norm_made, 1)
                        pe.wait_ge(rr_ready, 1)
                        for m in range(NB * KC + 1):
                            if m < NB * KC:
                                if m >= 4:
                                    pe.wait_ge(h_ready, m0 + m - 3)
                                pe.matmul(PS[:, BG[0] + m % 4], selr_r[:, m // KC, m % KC], rr[:],
                                          start=True, stop=True).then_inc(rb_made, 1)
                            if m >= 1:
                                u = m - 1
                                pe_accumulate(m0 + u, u == 0, u == NB * KC - 1,
                                              comb_hi[:, u % KC, u // KC], comb_lo[:, u % KC, u // KC])

                    pe_xT(0)
                    pe_ffn(0, 0)
                    pe_xT(1)
                    pe_memory(NJ)
                    pe_xT(2)
                    pe_ffn(1, NJ + NB * KC)
            clear()


def kernel(**inputs):
    import concourse.bacc as _bacc
    from concourse.bass_utils import run_bass_kernel_spmd as _run

    f = lambda a: np.ascontiguousarray(a, dtype=np.float32)
    g = {k: np.asarray(v) for k, v in inputs.items()}
    rows = lambda a, *shape: f(np.broadcast_to(a, (P, *shape)))

    inv = (1.0 / 10000.0 ** (np.arange(0, HD, 2, dtype=np.float32) / HD)).astype(np.float32)
    ang = np.outer(np.arange(S, dtype=np.float32), inv).astype(np.float32)
    by_tile = lambda a: f(a.reshape(NT, P, HD).transpose(1, 0, 2))
    cos = by_tile(np.concatenate([np.cos(ang), np.cos(ang)], 1))
    sin = by_tile(np.concatenate([-np.sin(ang), np.sin(ang)], 1))
    p = np.arange(P)
    ident = f(np.eye(P))
    mask = f(np.where(p[None, :] > p[:, None], MASKED, 0.0))
    headmask = f(p[:, None] // MD == np.arange(HP)[None, :])
    iota = rows(np.arange(NE), NE)
    selc = f(np.tile(np.arange(NE)[:, None] == np.arange(FT)[None, :] // FI, (2, 1)))
    row = np.arange(P) % (NB * MH)
    n_, kc_, c_ = np.ix_(np.arange(NB), np.arange(KC), p)
    selr = f(row[:, None, None, None] == (n_ * MH + kc_ * HP + c_ // MD)[None])

    qs, ks = g["L0_attn_a_q_norm_scale"], g["L0_attn_a_k_norm_scale"]
    swap = lambda a: np.concatenate([a[HD // 2:], a[:HD // 2]])
    scales = lambda q, k: rows(np.stack([q, k]), 2, HD)
    mem = g["L0_attn_b_memories"]
    mno = g["L0_attn_b_memory_norms"]
    bank = g["L0_attn_b_bank_weights"]
    arrays = {
        "x": f(g["L0_attn_a_x"]),
        "wqkv": f(np.concatenate([g["L0_attn_a_wq"], g["L0_attn_a_wk"], g["L0_attn_a_wv"]], 1)),
        "bqkv": rows(np.concatenate([g["L0_attn_a_bq"], g["L0_attn_a_bk"], g["L0_attn_a_bv"]]), QKV),
        "nscale": scales(qs, ks), "nscale_sw": scales(swap(qs), swap(ks)),
        "cos": cos, "sin": sin,
        "wo": f(g["L0_attn_a_wo"]), "bo": rows(g["L0_attn_a_bo"], D),
        "wr": f(g["L0_ffn_Wr"]),
        "wg": f(g["L0_ffn_Wg"].transpose(1, 0, 2).reshape(D, FT)),
        "wu": f(g["L0_ffn_Wu"].transpose(1, 0, 2).reshape(D, FT)),
        "wd": f(g["L0_ffn_Wd"].reshape(FT, D)),
        "mwq": f(g["L0_attn_b_Wq"].T), "mwo": f(g["L0_attn_b_Wo"].T),
        "mem": f(mem.reshape(NB, KC, HP, MD, MD).transpose(2, 4, 0, 1, 3).reshape(P, NB, KC, MD)),
        "mnorm": f(mno.reshape(NB, KC, P).transpose(2, 1, 0)),
        "mnorm_all": rows(mno.reshape(NB, MH * MD), NB, MH * MD),
        "bank": f(np.repeat(bank, MD, axis=0).reshape(KC, P, NB).transpose(1, 0, 2)),
        "ident": ident, "mask": mask, "headmask": headmask, "iota": iota, "selc": selc, "selr": selr,
    }
    nc = _bacc.Bacc("TRN2", target_bir_lowering=False, num_devices=1)
    args = {n: nc.dram_tensor(f"in_{n}", a.shape, F32, kind="ExternalInput").ap() for n, a in arrays.items()}
    out = nc.dram_tensor("out", (B, S, D), F32, kind="ExternalOutput").ap()
    build(nc, **args, out=out)
    r = _run(nc, [{f"in_{n}": a for n, a in arrays.items()}], core_ids=[0])
    return r.results[0]["out"]
```

```python
from contextlib import ExitStack

import numpy as np

import concourse.bass as bass
from concourse import mybir

ALU = mybir.AluOpType
ACT = mybir.ActivationFunctionType
AX = mybir.AxisListType
F32 = mybir.dt.float32
F32R = mybir.dt.float32r
F16 = mybir.dt.float16
BF16 = mybir.dt.bfloat16
U32 = mybir.dt.uint32

P = 128
B, S, D = 4, 512, 256
NT = S // P
KC = D // P
NH, NG, HD = 16, 4, 16
REP = NH // NG
QKV = D + 2 * NG * HD
NQK = NH + NG
QROW = 32
SHIFT = 16.0
NE, FI = 8, 176
FT = NE * FI
NJ = FT // P
MH, NB = 16, 4
MD = D // MH
HP = P // MD
LN_EPS, RMS_EPS, MEM_EPS = 1e-5, 1e-6, 1e-6
MASKED = -1e30
ATT_SCALE = HD ** -0.5
NS = 3


def score_units():
    return [(i, r, n) for i, n in ((3, 1), (2, 1), (1, 2), (0, 4)) for r in range(0, REP, n)]


UNITS = score_units()
NU = len(UNITS)


TURNED = [(1, NH, NQK)] + [(0, h, h + REP) for h in range(0, NH, REP)]


COST = {
    "a_stats": 3.0, "a_apply": 1.72, "a_turn": 1.75, "qkv": 1.25, "qkv_bias": 3.55, "square": 2.5,
    "mean_square": 1.5, "inv_rms": 1.0, "rms_scale": 1.27, "sines": 2.0, "rotate_keys": 1.0,
    "rotate_queries": 1.0, "keysT": 3.5, "queriesT": 1.0, "first": 0.65, "shiftedT": 1.03, "second": 0.5,
    "values": 0.2, "normalize": 0.6, "shift": 0.83, "outT": 1.5, "project": 0.6, "a_residual": 1.5,
    "carry": 1.24, "stats": 3.0, "apply": 2.5, "turn": 2.5, "router": 1.5, "gate": 1.3, "top2": 1.5,
    "up": 1.3, "combineT": 0.98, "spread": 0.2, "hidden": 0.0, "down": 1.3, "mem_q": 1.3, "mem_split": 2.5,
    "mem_norm": 1.3, "mem_inv": 6.0, "mem_rows": 0.3, "mem_scale": 0.0, "mem_out": 1.3, "residual": 1.0,
    "banks": 1.0, "norms": 1.0, "combine": 1.58, "split": 6.0, "ffn": (1.0, 0.9),
}


def attention_steps():
    steps = [("a_stats",), ("a_apply",), ("a_turn",)]
    steps += [("qkv", i) for i in range(NT)]
    steps += [("qkv_bias",), ("square",), ("mean_square",), ("inv_rms",), ("rms_scale",)]
    steps += [("sines", 0), ("sines", 1), ("rotate_keys",), ("keysT",)]
    steps += [("sines", n) for n in range(2, len(TURNED))]
    steps += [("rotate_queries",), ("queriesT", 0), ("queriesT", 1)]
    for g in range(NG + 1):
        for n in range(NU):
            if g < NG:
                steps.append(("first", g, n))
            if g >= 1:
                if n == 1:
                    steps.append(("shiftedT", g - 1))
                if n >= 1:
                    steps.append(("second", g - 1, n - 1))
                if n >= 2:
                    steps.append(("values", g - 1, n - 2))
        if g >= 1:
            steps += [("second", g - 1, NU - 1), ("values", g - 1, NU - 2),
                      ("values", g - 1, NU - 1), ("normalize", g - 1)]
        if g < NG:
            steps.append(("shift", g))
    steps.append(("outT",))
    steps += [("project", i) for i in range(NT)]
    return steps + [("a_residual",)]


def ffn_steps(f):
    s = [("router", f), ("gate", f, 0), ("top2", f), ("up", f, 0), ("gate", f, 1), ("combineT", f),
         ("spread", f, 0), ("hidden", f, 0)]
    for j in range(1, NJ):
        s += [("up", f, j), ("spread", f, j), ("hidden", f, j)]
        if j + 1 < NJ:
            s.append(("gate", f, j + 1))
        s.append(("down", f, j - 1))
    return s + [("down", f, NJ - 1)]


def tail_steps():
    s = [("carry",)]
    for n in range(NS):
        if n >= 1:
            s += [("stats", n), ("apply", n), ("turn", n)]
        if n == 1:
            s += [("mem_q", kc) for kc in range(KC)]
            s += [("mem_split",), ("mem_norm",), ("mem_inv",)]
            for m in range(NB * KC):
                s += [("mem_rows", m), ("mem_scale", m)]
                if m >= 2:
                    s.append(("mem_out", m - 2))
            s += [("mem_out", m) for m in (NB * KC - 2, NB * KC - 1)]
        else:
            s += ffn_steps(n // 2)
        s.append(("residual", n))
    return s


FIRST_NORM = [("stats", 0), ("apply", 0), ("turn", 0)]


FFN_STEPS = ("router", "gate", "top2", "up", "combineT", "spread", "hidden", "down")


def cost(step):
    return COST[step[0]] * (COST["ffn"][step[1]] if step[0] in FFN_STEPS else 1.0)


def merge(one, other):
    ta, tb = sum(cost(s) for s in one), sum(cost(s) for s in other)
    out, a, b, k = [], 0.0, 0.0, 0
    for step in one:
        out.append(step)
        a += cost(step)
        while k < len(other) and b / tb < a / ta:
            out.append(other[k])
            b += cost(other[k])
            k += 1
    return out + other[k:]


ALONE, TAIL = attention_steps(), tail_steps()
SET_UP = [("banks",), ("norms",)] + [("combine", n) for n in range(NB)] + [("split", w) for w in range(3)]
SCORES = ALONE.index(("first", 0, 0))
PROLOGUE = ([("presets",), ("weights16",), ALONE[0], ("tables",)] + ALONE[1:3] + [("selections",)]
            + ALONE[3:SCORES] + merge(ALONE[SCORES:], SET_UP) + FIRST_NORM)
LAST_UP = TAIL.index(("up", 1, NJ - 1))
STEADY = (merge(TAIL[:LAST_UP], ALONE) + FIRST_NORM[:2] + TAIL[LAST_UP:-2] + FIRST_NORM[2:] + TAIL[-2:])
EPILOGUE = TAIL
M0 = {("ffn", 0): 0, ("mem", 0): NJ, ("ffn", 1): NJ + NB * KC}
RH = 3


FIRST_PACK = {"ident": (P,), "wqkv": (KC, QKV), "bqkv": (QKV,), "mask": (P,), "nscale": (2, 2, HD),
              "turns": (2, NT, HD), "wo": (KC, D), "bo": (D,)}
ONCE_PACK = {"selr": (NB, KC, P), "mnorm_all": (NB, MH * MD)}
LATE_PACK = {"iota": (NE,), "headmask": (HP,), "wr": (KC, NE), "mwq": (KC, D), "mwo": (KC, D),
             "mem": (NB, KC, MD), "mnorm": (KC, NB), "bank": (KC, NB)}


def width(pack):
    return sum(int(np.prod(shape)) for shape in pack.values())


def build(nc, x, first_pack, once_pack, late_pack, selc, wg, wu, wd, out):
    x_v = x.rearrange("b (i p) c -> b p i c", p=P)
    out_v = out.rearrange("b (i p) c -> b p i c", p=P)
    with ExitStack() as ctx:
        staging = ctx.enter_context(ExitStack())

        def sb(name, shape, dt=F32, only=ctx):
            return only.enter_context(nc.sbuf_tensor(name, shape, dt))

        sems = []

        def sem(name):
            sems.append(ctx.enter_context(nc.semaphore(name)))
            return sems[-1]

        ident_f = sb("ident_f", [P, P])
        ident_h = sb("ident_h", [P, P], F16)
        ident_b = sb("ident_b", [P, P], BF16)
        mask_b = sb("mask_b", [P, P], BF16)
        iota_s = sb("iota_s", [P, NE])
        wqkv_h = sb("wqkv_h", [P, KC, QKV], F16)
        bqkv_h = sb("bqkv_h", [P, QKV], F16)
        rope = sb("rope", [P, 2, 2, NT, HD])
        wo_h = sb("wo_h", [P, KC, D], F16)
        bo_h = sb("bo_h", [P, D], F16)
        whi = sb("whi", [P, 3, KC * FT], F32R)
        wlo = sb("wlo", [P, 3, KC * FT], F32R)
        gate_hi, gate_lo = (w[:, 0, :].rearrange("p (k f) -> p k f", k=KC) for w in (whi, wlo))
        up_hi, up_lo = (w[:, 1, :].rearrange("p (k f) -> p k f", k=KC) for w in (whi, wlo))
        down_hi, down_lo = (w[:, 2, :].rearrange("p (j c) -> p j c", j=NJ) for w in (whi, wlo))
        wr_hl = sb("wr_hl", [P, KC, 2, NE], F32R)
        mwq_hi = sb("mwq_hi", [P, KC, D], F32R)
        mwq_lo = sb("mwq_lo", [P, KC, D], F32R)
        norm_hi = sb("norm_hi", [P, KC, 2 * NB * MH], F32R)
        norm_lo = sb("norm_lo", [P, KC, 2 * NB * MH], F32R)
        comb_hi = sb("comb_hi", [P, KC, NB, D], F32R)
        comb_lo = sb("comb_lo", [P, KC, NB, D], F32R)
        selc_r = sb("selc_r", [2 * NE, FT], F32R)
        selr_r = sb("selr_r", [P, NB, KC, P], F32R)
        mhalf = sb("mhalf", [P, NT])

        vaug = sb("vaug", [P, NT, NG, HD + 1], F16)
        qa = sb("qa", [P, NT, NH, QROW], F16)
        ka = sb("ka", [P, NT, NG, QROW], F16)
        kbd = sb("kbd", [P, NG, REP, S], F16)
        xin = sb("xin", [P, NT, D])
        a_stat = sb("a_stat", [P, NT, 6])
        a_mv = sb("a_mv", [P, NT, 2])
        a_veps = sb("a_veps", [P, NT])
        a_rstd = sb("a_rstd", [P, NT])
        xh = sb("xh", [P, NT, D], F16)
        xhT = sb("xhT", [P, KC, S], F16)
        qkv16 = sb("qkv16", [P, NT, QKV], F16)
        qk16 = sb("qk16", [P, NT, NQK * HD], F16)
        sq = sb("sq", [P, NT * NQK, HD])
        rota = sq
        ms = sb("ms", [P, NT * NQK])
        msv = sb("msv", [P, NT * NQK])
        lnv = sb("lnv", [P, NT * NQK])
        y0 = sb("y0", [P, NT * NQK])
        y1 = sb("y1", [P, NT * NQK])
        kT = sb("kT", [P, S], F16)
        qT = sb("qT", [P, NG + 2, S], F16)
        qT1, qT2 = qT[:, 0:NG], qT[:, NG:]
        rotb = qT[:].rearrange("p g s -> p (g s)").bitcast(F32)[:, 0:NT * NQK * HD]\
            .rearrange("p (h d) -> p h d", d=HD)
        smax = sb("smax", [P, NT, NH])
        NPR = 8
        prob = sb("prob", [P, NPR, S], F16)
        qkn = prob[:].rearrange("p n s -> p (n s)").bitcast(F32)[:, 0:NT * NQK * HD]\
            .rearrange("p (h d) -> p h d", d=HD)
        rsum = sb("rsum", [P, NT, REP])
        o16, oT = xh, xhT
        y16 = qkv16[:].rearrange("p i n -> p (i n)")[:, 0:NT * D].rearrange("p (i c) -> p i c", i=NT)

        n_stat = sb("n_stat", [P, NT, 6])
        n_mv = sb("n_mv", [P, NT, 2])
        n_veps = sb("n_veps", [P, NT])
        n_rstd = sb("n_rstd", [P, NT])
        xT_hi = sb("xT_hi", [P, KC, S], F32R)
        xT_lo = sb("xT_lo", [P, KC, S], F32R)
        xn0 = prob[:, 0:4].rearrange("p n s -> p (n s)").bitcast(F32).rearrange("p (i c) -> p i c", i=NT)

        st = lambda name, shape, dt=F32: sb(name, shape, dt, staging)
        wstage = st("wstage", [P, 2, KC * FT])
        late_s = st("late_s", [P, width(LATE_PACK)])

        def views(rows, pack):
            out, n = {}, 0
            for name, shape in pack.items():
                v = rows[:, n:n + int(np.prod(shape))]
                n += int(np.prod(shape))
                letters = "abc"[:len(shape)]
                out[name] = v if len(shape) == 1 else v.rearrange(
                    f"p ({' '.join(letters)}) -> p {' '.join(letters)}", **dict(zip(letters[1:], shape[1:])))
            return out

        first_rows = wstage[:, 1, 0:width(FIRST_PACK)]
        once_rows = prob[:].rearrange("p n s -> p (n s)").bitcast(F32)[:, 0:width(ONCE_PACK)]
        selc_f = qT[0:2 * NE].rearrange("p g s -> p (g s)").bitcast(F32)[:, 0:FT]
        first, once, late_v = views(first_rows, FIRST_PACK), views(once_rows, ONCE_PACK), views(late_s[:], LATE_PACK)
        mem_bd = st("mem_bd", [P, NB, KC, P])
        norm_f = st("norm_f", [P, KC, 2, NB, MH])
        mnsum = st("mnsum", [P, NB])
        bmax = st("bmax", [P, KC])
        bsum = st("bsum", [P, KC])
        bankw = st("bankw", [P, KC, NB])
        PS = ctx.enter_context(nc.psum_tensor("PS", [P, 8, 512], F32))

        def bank16(n):
            return PS[:, n, :].bitcast(F16)

        PA, PB, PO, PG, PU, PC, PY = 0, 1, 2, 3, 4, 5, (6, 7)

        first_loaded, once_loaded, late_loaded = sem("first_loaded"), sem("once_loaded"), sem("late_loaded")
        selc_loaded, staged = sem("selc_loaded"), [sem(f"staged{w}") for w in range(3)]
        ident_ready, weights16, bias_ready = sem("ident_ready"), sem("weights16"), sem("bias_ready")
        masks_ready, scales_ready, rope_ready = sem("masks_ready"), sem("scales_ready"), sem("rope_ready")
        queries_cleared, keys_cleared, keys_set = sem("queries_cleared"), sem("keys_cleared"), sem("keys_set")
        copies_cleared, pool_set, once_used = sem("copies_cleared"), sem("pool_set"), sem("once_used")
        bank_shifted, bank_exped, bank_ready = sem("bank_shifted"), sem("bank_exped"), sem("bank_ready")
        mem_placed, comb_made = sem("mem_placed"), sem("comb_made")
        comb_hi_ready, comb_lo_ready = sem("comb_hi_ready"), sem("comb_lo_ready")
        whi_ready, wlo_ready = sem("whi_ready"), sem("wlo_ready")
        x_loaded = sem("x_loaded")
        var_ready, rstd_ready = sem("var_ready"), sem("rstd_ready")
        xh_ready, xhT_made, xhT_ready = sem("xh_ready"), sem("xhT_made"), sem("xhT_ready")
        qkv_made, qkv_rounded = sem("qkv_made"), sem("qkv_rounded")
        qk_biased, v_ready, qk_squared = sem("qk_biased"), sem("v_ready"), sem("qk_squared")
        ms_ready, y0_ready, qk_normed = sem("ms_ready"), sem("y0_ready"), sem("qk_normed")
        sin_made, cos_made = sem("sin_made"), sem("cos_made")
        q_rotated, k_rotated, shift_cleared = sem("q_rotated"), sem("k_rotated"), sem("shift_cleared")
        kT_made, kT_ready = sem("kT_made"), sem("kT_ready")
        keys_placed = [sem(f"keys_placed{g}") for g in range(NG)]
        qT1_made, qT1_ready = sem("qT1_made"), sem("qT1_ready")
        first_made, max_taken, shift_ready = sem("first_made"), sem("max_taken"), sem("shift_ready")
        qT2_made, qT2_ready = sem("qT2_made"), sem("qT2_ready")
        second_made, prob_ready, prob_used = sem("second_made"), sem("prob_ready"), sem("prob_used")
        o_ready = sem("o_ready")
        oT_made, oT_ready, att_made, att_rounded = sem("oT_made"), sem("oT_ready"), sem("att_made"), sem("att_rounded")
        dve_step, act_step = sem("dve_step"), sem("act_step")
        carried = sem("carried")
        nvar_ready, nrstd_ready = sem("nvar_ready"), sem("nrstd_ready")
        attended, xn_ready, xT_made = sem("attended"), sem("xn_ready"), sem("xT_made")
        xT_hi_ready, xT_lo_ready = sem("xT_hi_ready"), sem("xT_lo_ready")
        logits_made, gap_ready, e2_ready = sem("logits_made"), sem("gap_ready"), sem("e2_ready")
        c_ready, cT_made, cT_ready = sem("c_ready"), sem("cT_made"), sem("cT_ready")
        gate_made, up_made, cb_made = sem("gate_made"), sem("up_made"), sem("cb_made")
        tanh_ready, silu_ready, scaled, h_ready = sem("tanh_ready"), sem("silu_ready"), sem("scaled"), sem("h_ready")
        hi_ready, lo_ready, h_used = sem("hi_ready"), sem("lo_ready"), sem("h_used")
        mq_made, mexp_ready, sq_ready = sem("mq_made"), sem("mexp_ready"), sem("sq_ready")
        sq_hi_ready, sq_lo_ready = sem("sq_hi_ready"), sem("sq_lo_ready")
        norm_made, rr_ready, rb_made = sem("norm_made"), sem("rr_ready"), sem("rb_made")
        xr_ready, xr_free = sem("xr_ready"), sem("xr_free")
        stored = ctx.enter_context(nc.semaphore("stored"))

        def counted(eng, signal):
            count = [0]

            def link(ins):
                count[0] += 1
                ins.then_inc(signal, 1)
                eng.wait_ge(signal, count[0])
            return link

        def heads(t, h0, h1):
            return t.rearrange("p (i h) d -> p i h d", i=NT)[:, :, h0:h1]

        def turn(n, q, nh):
            return rope[:, n, q].unsqueeze(2).to_broadcast([P, NT, nh, HD])

        def clear():
            nums = [s.num for s in sems]
            assert max(nums) - min(nums) == len(nums) - 1
            nc.sync.sem_clear(range(min(nums), max(nums) + 1))
            nc.all_engine_barrier()

        def sequences(schedule, load_from, store_to):
            has_tail = store_to is not None

            def norms(n):
                return n if n else (NS if has_tail else 1)

            with nc.Block() as block:

                @block.sync
                def _(sp):
                    if has_tail:
                        sp.wait_ge(stored, 16)
                        sp.sem_clear(stored)
                        sp.sem_inc(xr_free, 1)
                    if load_from is not None:
                        if has_tail:
                            sp.wait_ge(carried, 1)
                        sp.dma_start(xin[:], load_from).then_inc(x_loaded, 16)
                    if not has_tail:
                        sp.dma_start(first_rows, first_pack).then_inc(first_loaded, 16)
                        sp.dma_start(once_rows, once_pack).then_inc(once_loaded, 16)
                        sp.dma_start(selc_f, selc).then_inc(selc_loaded, 16)
                        sp.dma_start(late_s[:], late_pack).then_inc(late_loaded, 16)
                        for w, src in enumerate((wg, wu)):
                            if w == 1:
                                sp.wait_ge(ident_ready, 1)
                                sp.wait_ge(weights16, 2)
                                sp.wait_ge(masks_ready, 1)
                                sp.wait_ge(rope_ready, 1)
                            sp.dma_start(wstage[:, w].rearrange("p (k f) -> p k f", k=KC),
                                         src.rearrange("(k p) f -> p k f", p=P)).then_inc(staged[w], 16)
                        sp.wait_ge(copies_cleared, 1)
                    if load_from is not None:
                        sp.wait_ge(kT_ready, 1)
                        for g in range(NG):
                            for r in range(REP):
                                sp.dma_start(kbd[r * QROW:(r + 1) * QROW, g, r], kT[g * QROW:(g + 1) * QROW])\
                                  .then_inc(keys_placed[g], 16)
                    if not has_tail:
                        sp.wait_ge(wlo_ready, 1)
                        sp.dma_start(wstage[:, 0].rearrange("p (j c) -> p j c", j=NJ),
                                     wd.rearrange("(j p) c -> p j c", p=P)).then_inc(staged[2], 16)
                    else:
                        sp.wait_ge(xr_ready, NS)
                        sp.dma_start(store_to, xr[:]).then_inc(stored, 16)
                        if load_from is None:
                            sp.wait_ge(stored, 16)

                @block.tensor
                def _(pe):
                    def three(outs, pairs):
                        n = 0
                        for (sh, sl), (mh, ml) in pairs:
                            for s_, m_ in ((sh, mh), (sh, ml), (sl, mh)):
                                n += 1
                                mm = pe.matmul(outs, s_, m_, start=(n == 1), stop=(n == 3 * len(pairs)))
                        return mm

                    def xTs(kc, a, z):
                        return xT_hi[:, kc, a:z], xT_lo[:, kc, a:z]

                    def accumulate(m, first, hi, lo):
                        pe.wait_ge(hi_ready, m + 1)
                        pe.wait_ge(lo_ready, m + 1)
                        for i in range(NT):
                            for k, (s_, m_) in enumerate(((hhi, hi), (hhi, lo), (hlo, hi))):
                                mm = pe.matmul(PS[:, PY[i // 2], (i % 2) * D:(i % 2 + 1) * D],
                                               s_[:, m % RH, i * P:(i + 1) * P], m_,
                                               start=(first and k == 0 and i % 2 == 0), stop=True,
                                               skip_group_check=True)
                        mm.then_inc(h_used, 1)

                    for kind, *a in schedule:
                        if kind == "combine":
                            (n,) = a
                            pe.wait_ge(mem_placed, 1)
                            if n >= 2:
                                pe.wait_ge(comb_lo_ready, n - 1)
                            for kc in range(KC):
                                mm = pe.matmul(PS[:, PY[n % 2], kc * D:(kc + 1) * D], mem_bd[:, n, kc], late_v["mwo"][:, kc],
                                               start=True, stop=True)
                            mm.then_inc(comb_made, 1)
                        elif kind == "a_turn":
                            if not has_tail:
                                pe.wait_ge(ident_ready, 1)
                            for i in range(NT):
                                pe.wait_ge(xh_ready, i + 1)
                                for kc in range(KC):
                                    mm = pe.transpose(bank16(PA)[:, kc * S + i * P:kc * S + (i + 1) * P],
                                                      xh[:, i, kc * P:(kc + 1) * P], ident_h[:])
                            mm.then_inc(xhT_made, 1)
                        elif kind == "qkv":
                            (i,) = a
                            if i == 0:
                                pe.wait_ge(xhT_ready, 1)
                                if not has_tail:
                                    pe.wait_ge(weights16, 1)
                            if i >= 2:
                                pe.wait_ge(qkv_rounded, i - 1)
                            for kc in range(KC):
                                mm = pe.matmul(PS[:, (PB, PO)[i % 2], 0:QKV], xhT[:, kc, i * P:(i + 1) * P],
                                               wqkv_h[:, kc], start=(kc == 0), stop=(kc == KC - 1))
                            mm.then_inc(qkv_made, 1)
                        elif kind == "keysT":
                            pe.wait_ge(k_rotated, 1)
                            if not has_tail:
                                pe.wait_ge(keys_set, 1)
                                pe.wait_ge(masks_ready, 1)
                            for i in range(NT):
                                mm = pe.transpose(bank16(PA)[:, i * P:(i + 1) * P],
                                                  ka[:, i].rearrange("p g d -> p (g d)"), ident_h[:])
                            mm.then_inc(kT_made, 1)
                        elif kind == "queriesT":
                            (n,) = a
                            pe.wait_ge(q_rotated, 1)
                            pe.wait_ge(shift_cleared, 1)
                            for g in (2 * n, 2 * n + 1):
                                for i in range(NT):
                                    mm = pe.transpose(
                                        bank16((PB, PO)[n])[:, (g % 2) * S + i * P:(g % 2) * S + (i + 1) * P],
                                        qa[:, i, REP * g:REP * (g + 1)].rearrange("p r d -> p (r d)"), ident_h[:])
                            mm.then_inc(qT1_made, 1)
                        elif kind == "first":
                            g, n = a
                            i, r0, nr = UNITS[n]
                            u, w = NU * g + n, (i + 1) * P
                            if n == 0:
                                pe.wait_ge(keys_placed[g], 16 * REP)
                            if u == 0:
                                pe.wait_ge(qT1_ready, 2)
                            if u >= len(FIRST_BANKS):
                                pe.wait_ge(max_taken, u + 1 - len(FIRST_BANKS))
                            o = PS[:, FIRST_BANKS[u % len(FIRST_BANKS)], 0:nr * w].rearrange("p (r w) -> p r w", r=nr)
                            pe.matmul(o, qT1[:, g, i * P:(i + 1) * P], kbd[:, g, r0:r0 + nr, 0:w],
                                      start=True, stop=False, skip_group_check=True)
                            pe.matmul(o[:, :, i * P:w], ident_b[:], mask_b[:].unsqueeze(1).to_broadcast([P, nr, P]),
                                      start=False, stop=True, skip_group_check=True).then_inc(first_made, 1)
                        elif kind == "shiftedT":
                            (g,) = a
                            pe.wait_ge(shift_ready, g + 1)
                            if g >= 1:
                                pe.wait_ge(prob_ready, NU * g)
                            for i in range(NT):
                                mm = pe.transpose(bank16(SECOND_BANKS[NU * g % len(SECOND_BANKS)])[:, i * P:(i + 1) * P],
                                                  qa[:, i, REP * g:REP * (g + 1)].rearrange("p r d -> p (r d)"),
                                                  ident_h[:])
                            mm.then_inc(qT2_made, 1)
                        elif kind == "second":
                            g, n = a
                            i, r0, nr = UNITS[n]
                            j = NT - 1 - i
                            u, w = NU * g + n, S - j * P
                            if n == 0:
                                pe.wait_ge(qT2_ready, g + 1)
                            if u >= len(SECOND_BANKS):
                                pe.wait_ge(prob_ready, u + 1 - len(SECOND_BANKS))
                            for k in range(nr):
                                o = PS[:, SECOND_BANKS[u % len(SECOND_BANKS)], k * w:(k + 1) * w]
                                pe.matmul(o, kbd[:, g, r0 + k, j * P:(j + 1) * P], qT2[:, g % 2, j * P:S],
                                          start=True, stop=False, skip_group_check=True)
                                mm = pe.matmul(o[:, 0:P], mask_b[:], ident_b[:], start=False, stop=True,
                                               skip_group_check=True)
                            mm.then_inc(second_made, 1)
                        elif kind == "values":
                            g, n = a
                            i0, r0, nr = UNITS[n]
                            j = NT - 1 - i0
                            u, w = NU * g + n, S - j * P
                            if n == 0:
                                if g == 0:
                                    pe.wait_ge(v_ready, 1)
                                else:
                                    pe.wait_ge(o_ready, g)
                            pe.wait_ge(prob_ready, u + 1)
                            o = PS[:, PO, 0:NT * REP * (HD + 1)].rearrange("p (i r d) -> p i r d", i=NT, r=REP)
                            for k in range(nr):
                                for i in range(j, NT):
                                    mm = pe.matmul(o[:, i, r0 + k],
                                                   prob[:, u % NPR, k * w + (i - j) * P:k * w + (i - j + 1) * P],
                                                   vaug[:, j, g], start=(n == 0 and k == 0 and i == 0), stop=True,
                                                   skip_group_check=True)
                            mm.then_inc(prob_used, 1)
                        elif kind == "outT":
                            pe.wait_ge(o_ready, NG)
                            for i in range(NT):
                                for kc in range(KC):
                                    mm = pe.transpose(bank16(PA)[:, kc * S + i * P:kc * S + (i + 1) * P],
                                                      o16[:, i, kc * P:(kc + 1) * P], ident_h[:])
                            mm.then_inc(oT_made, 1)
                        elif kind == "project":
                            (i,) = a
                            if i == 0:
                                pe.wait_ge(oT_ready, 1)
                                if not has_tail:
                                    pe.wait_ge(weights16, 2)
                            if i >= 2:
                                pe.wait_ge(att_rounded, i - 1)
                            for kc in range(KC):
                                mm = pe.matmul(PS[:, (PB, PO)[i % 2], 0:D], oT[:, kc, i * P:(i + 1) * P], wo_h[:, kc],
                                               start=(kc == 0), stop=(kc == KC - 1))
                            mm.then_inc(att_made, 1)
                        elif kind == "turn":
                            (n,) = a
                            src = xn if n else xn0
                            for kc in range(KC):
                                if n == 0 and has_tail:
                                    pe.wait_ge((silu_ready, h_ready)[kc], (2 * NJ, 2 * NJ + NB * KC)[kc])
                                for i in range(NT):
                                    if kc == 0:
                                        pe.wait_ge(xn_ready, NT * (norms(n) - 1) + i + 1)
                                    mm = pe.transpose(PS[:, PG + kc, i * P:(i + 1) * P],
                                                      src[:, i, kc * P:(kc + 1) * P], ident_f[:])
                                mm.then_inc(xT_made, 1)
                        elif kind == "router":
                            (f,) = a
                            if f == 1:
                                pe.wait_ge(xT_hi_ready, KC * 2)
                                pe.wait_ge(xT_lo_ready, KC * 2)
                            for i in range(NT):
                                n = 0
                                for kc in range(KC):
                                    for s_ in xTs(kc, i * P, (i + 1) * P):
                                        n += 1
                                        mm = pe.matmul(PS[:, PC, i * 2 * NE:(i + 1) * 2 * NE], s_, wr_hl[:, kc],
                                                       start=(n == 1), stop=(n == 2 * KC))
                            mm.then_inc(logits_made, 1)
                        elif kind == "gate":
                            f, j = a
                            q = NJ * f + j
                            if j >= 1:
                                pe.wait_ge(silu_ready, q)
                            cols = slice(j * P, (j + 1) * P)
                            three(PS[:, PG], [((gate_hi[:, kc, cols], gate_lo[:, kc, cols]), xTs(kc, 0, S))
                                              for kc in range(KC)]).then_inc(gate_made, 1)
                        elif kind == "up":
                            f, j = a
                            if j >= 1:
                                pe.wait_ge(h_ready, M0["ffn", f] + j)
                            cols = slice(j * P, (j + 1) * P)
                            three(PS[:, PU], [((up_hi[:, kc, cols], up_lo[:, kc, cols]), xTs(kc, 0, S))
                                              for kc in range(KC)]).then_inc(up_made, 1)
                        elif kind == "combineT":
                            (f,) = a
                            pe.wait_ge(c_ready, f + 1)
                            for i in range(NT):
                                mm = pe.transpose(PS[0:2 * NE, PC, i * P:(i + 1) * P],
                                                  chl[:, i].bitcast(F32), ident_f[:])
                            mm.then_inc(cT_made, 1)
                        elif kind == "spread":
                            f, j = a
                            q = NJ * f + j
                            if j == 0:
                                pe.wait_ge(cT_ready, f + 1)
                            else:
                                pe.wait_ge(scaled, q)
                            pe.matmul(PS[:, PC], selc_r[:, j * P:(j + 1) * P], cT, start=True, stop=True)\
                              .then_inc(cb_made, 1)
                        elif kind == "down":
                            f, j = a
                            accumulate(M0["ffn", f] + j, j == 0, down_hi[:, j], down_lo[:, j])
                        elif kind == "mem_q":
                            (mc,) = a
                            pe.wait_ge(xT_hi_ready, KC)
                            pe.wait_ge(xT_lo_ready, KC)
                            cols = slice(mc * P, (mc + 1) * P)
                            three(PS[:, PG + mc], [((mwq_hi[:, kc, cols], mwq_lo[:, kc, cols]), xTs(kc, 0, S))
                                                   for kc in range(KC)]).then_inc(mq_made, 1)
                        elif kind == "mem_norm":
                            pe.wait_ge(sq_hi_ready, 1)
                            pe.wait_ge(sq_lo_ready, 1)
                            three(PS[:, PC], [((norm_hi[:, kc], norm_lo[:, kc]), (sq_hi[:, kc], sq_lo[:, kc]))
                                              for kc in range(KC)]).then_inc(norm_made, 1)
                        elif kind == "mem_rows":
                            (m,) = a
                            if m == 0:
                                pe.wait_ge(rr_ready, 1)
                            if m >= 3:
                                pe.wait_ge(h_ready, M0["mem", 0] + m - 2)
                            pe.matmul(PS[:, PG + m % 3], selr_r[:, m // KC, m % KC], rr[:], start=True, stop=True)\
                              .then_inc(rb_made, 1)
                        elif kind == "mem_out":
                            (m,) = a
                            accumulate(M0["mem", 0] + m, m == 0, comb_hi[:, m % KC, m // KC],
                                       comb_lo[:, m % KC, m // KC])

                @block.scalar
                def _(act):
                    link = counted(act, act_step)

                    def high(m):
                        act.wait_ge(h_ready, m + 1)
                        if m == M0["mem", 0]:
                            act.wait_ge(norm_made, 1)
                        if m >= RH:
                            act.wait_ge(h_used, m + 1 - RH)
                        act.activation(hhi[:, m % RH], hf[:, m % RH], ACT.Copy).then_inc(hi_ready, 1)

                    for kind, *a in schedule:
                        if kind == "weights16":
                            act.wait_ge(first_loaded, 16)
                            act.activation(wqkv_h[:], first["wqkv"], ACT.Copy).then_inc(weights16, 1)
                            act.activation(bqkv_h[:], first["bqkv"], ACT.Copy).then_inc(bias_ready, 1)
                            act.activation(bo_h[:], first["bo"], ACT.Copy)
                            act.activation(wo_h[:], first["wo"], ACT.Copy).then_inc(weights16, 1)
                        elif kind == "selections":
                            act.wait_ge(selc_loaded, 16)
                            act.activation(selc_r[:], selc_f, ACT.Copy, scale=0.5)
                            act.wait_ge(once_loaded, 16)
                            act.activation(selr_r[:], once["selr"], ACT.Copy).then_inc(once_used, 1)
                        elif kind == "banks":
                            act.wait_ge(bank_shifted, 1)
                            act.activation(bankw[:], late_v["bank"], ACT.Exp).then_inc(bank_exped, 1)
                        elif kind == "combine":
                            (n,) = a
                            act.wait_ge(comb_made, n + 1)
                            act.wait_ge(bank_ready, 1)
                            for kc in range(KC):
                                ins = act.activation(comb_hi[:, kc, n], PS[:, PY[n % 2], kc * D:(kc + 1) * D],
                                                     ACT.Copy, scale=bankw[:, kc, n:n + 1])
                            ins.then_inc(comb_hi_ready, 1)
                        elif kind == "split":
                            (w,) = a
                            act.wait_ge(staged[w], 16)
                            act.activation(whi[:, w], wstage[:, w % 2], ACT.Copy).then_inc(whi_ready, 1)
                        elif kind == "qkv":
                            (i,) = a
                            act.wait_ge(qkv_made, i + 1)
                            act.activation(qkv16[:, i], PS[:, (PB, PO)[i % 2], 0:QKV], ACT.Copy)\
                               .then_inc(qkv_rounded, 1)
                        elif kind == "square":
                            act.wait_ge(qk_biased, 1)
                            act.activation(sq[:].rearrange("p h d -> p (h d)"), qk16[:].rearrange("p i n -> p (i n)"),
                                           ACT.Square).then_inc(qk_squared, 1)
                        elif kind == "inv_rms":
                            act.wait_ge(ms_ready, 1)
                            link(act.activation(lnv[:], msv[:], ACT.Ln))
                            act.activation(y0[:], lnv[:], ACT.Exp, scale=-0.5).then_inc(y0_ready, 1)
                        elif kind == "queriesT":
                            (n,) = a
                            act.wait_ge(qT1_made, n + 1)
                            act.activation(qT1[:, 2 * n:2 * n + 2].rearrange("p g s -> p (g s)"),
                                           bank16((PB, PO)[n]), ACT.Copy).then_inc(qT1_ready, 1)
                        elif kind == "shiftedT":
                            (g,) = a
                            act.wait_ge(qT2_made, g + 1)
                            act.activation(qT2[:, g % 2], bank16(SECOND_BANKS[NU * g % len(SECOND_BANKS)])[:, 0:S],
                                           ACT.Copy).then_inc(qT2_ready, 1)
                        elif kind == "second":
                            g, n = a
                            i, r0, nr = UNITS[n]
                            u, w = NU * g + n, (i + 1) * P
                            act.wait_ge(second_made, u + 1)
                            if u >= NPR:
                                act.wait_ge(prob_used, u + 1 - NPR)
                            act.activation(prob[:, u % NPR, 0:nr * w],
                                           PS[:, SECOND_BANKS[u % len(SECOND_BANKS)], 0:nr * w],
                                           ACT.Exp, scale=ATT_SCALE).then_inc(prob_ready, 1)
                        elif kind == "project":
                            (i,) = a
                            act.wait_ge(att_made, i + 1)
                            act.activation(y16[:, i], PS[:, (PB, PO)[i % 2], 0:D], ACT.Copy).then_inc(att_rounded, 1)
                        elif kind == "turn":
                            (n,) = a
                            for kc in range(KC):
                                act.wait_ge(xT_made, KC * (norms(n) - 1) + kc + 1)
                                act.activation(xT_hi[:, kc], PS[:, PG + kc], ACT.Copy).then_inc(xT_hi_ready, 1)
                        elif kind == "top2":
                            (f,) = a
                            act.wait_ge(gap_ready, f + 1)
                            act.activation(e2[:], gap[:], ACT.Exp).then_inc(e2_ready, 1)
                        elif kind == "combineT":
                            (f,) = a
                            act.wait_ge(cT_made, f + 1)
                            act.activation(cT, PS[0:2 * NE, PC], ACT.Copy).then_inc(cT_ready, 1)
                        elif kind == "gate":
                            f, j = a
                            q = NJ * f + j
                            act.wait_ge(gate_made, q + 1)
                            if j >= 2:
                                act.wait_ge(scaled, q - 1)
                            act.activation(sg[:, q % 2], PS[:, PG], ACT.Tanh, scale=0.5).then_inc(tanh_ready, 1)
                        elif kind == "hidden":
                            f, j = a
                            high(M0["ffn", f] + j)
                        elif kind == "mem_q":
                            (kc,) = a
                            act.wait_ge(mq_made, kc + 1)
                            act.activation(mexp[:, kc], PS[:, PG + kc], ACT.Exp)
                            act.activation(mrelu[:, kc], PS[:, PG + kc], ACT.Relu).then_inc(mexp_ready, 1)
                        elif kind == "mem_split":
                            act.wait_ge(sq_ready, 1)
                            act.activation(sq_hi, sq_f[:], ACT.Copy).then_inc(sq_hi_ready, 1)
                        elif kind == "mem_scale":
                            (m,) = a
                            high(M0["mem", 0] + m)

                @block.vector
                def _(dve):
                    link = counted(dve, dve_step)

                    def statistics(src, stat, mv, veps):
                        for i in range(NT):
                            last = dve.bn_stats(stat[:, i], src[:, i])
                        link(last)
                        for i in range(NT):
                            last = dve.bn_aggr(mv[:, i], stat[:, i])
                        link(last)
                        return dve.tensor_scalar(veps[:], mv[:, :, 1], LN_EPS, None, ALU.add)

                    for kind, *a in schedule:
                        if kind == "presets":
                            dve.memset(qa[:].bitcast(U32), 0).then_inc(queries_cleared, 1)
                        elif kind == "weights16":
                            dve.wait_ge(first_loaded, 16)
                            dve.tensor_copy(ident_h[:], first["ident"]).then_inc(ident_ready, 1)
                            dve.tensor_scalar(first["nscale"][:, :, 0], first["nscale"][:, :, 0], ATT_SCALE, None,
                                              ALU.mult).then_inc(scales_ready, 1)
                            dve.tensor_copy(ident_f[:], first["ident"])
                            dve.tensor_copy(ident_b[:], first["ident"])
                            dve.tensor_copy(mask_b[:], first["mask"]).then_inc(masks_ready, 1)
                        elif kind == "selections":
                            dve.wait_ge(once_loaded, 16)
                            dve.tensor_reduce(mnsum[:], once["mnorm_all"], AX.X, ALU.add).then_inc(once_used, 1)
                        elif kind == "banks":
                            dve.wait_ge(late_loaded, 16)
                            dve.tensor_copy(iota_s[:], late_v["iota"])
                            link(dve.tensor_reduce(bmax[:], late_v["bank"], AX.X, ALU.max))
                            dve.tensor_tensor(late_v["bank"], late_v["bank"], bmax[:].unsqueeze(2).to_broadcast([P, KC, NB]),
                                              ALU.subtract).then_inc(bank_shifted, 1)
                            dve.wait_ge(once_used, 1)
                            link(dve.tensor_scalar(mnsum[:], mnsum[:], MEM_EPS, None, ALU.is_ge))
                            dve.wait_ge(bank_exped, 1)
                            link(dve.tensor_reduce(bsum[:], bankw[:], AX.X, ALU.add))
                            link(dve.reciprocal(bsum[:], bsum[:]))
                            link(dve.tensor_tensor(bankw[:], bankw[:], bsum[:].unsqueeze(2).to_broadcast([P, KC, NB]),
                                                   ALU.mult))
                            dve.tensor_tensor(bankw[:], bankw[:], mnsum[:].unsqueeze(1).to_broadcast([P, KC, NB]),
                                              ALU.mult).then_inc(bank_ready, 1)
                        elif kind == "combine":
                            (n,) = a
                            dve.wait_ge(bank_ready, 1)
                            dve.wait_ge(comb_hi_ready, n + 1)
                            for kc in range(KC):
                                ins = dve.scalar_tensor_tensor(
                                    comb_lo[:, kc, n], PS[:, PY[n % 2], kc * D:(kc + 1) * D], bankw[:, kc, n:n + 1],
                                    comb_hi[:, kc, n].bitcast(F32), ALU.mult, ALU.subtract)
                            ins.then_inc(comb_lo_ready, 1)
                        elif kind == "a_stats":
                            dve.wait_ge(x_loaded, 16)
                            statistics(xin, a_stat, a_mv, a_veps).then_inc(var_ready, 1)
                        elif kind == "a_apply":
                            dve.wait_ge(rstd_ready, 1)
                            for i in range(NT):
                                dve.tensor_scalar(xh[:, i], xin[:, i], a_mv[:, i, 0:1], a_rstd[:, i:i + 1],
                                                  ALU.subtract, ALU.mult).then_inc(xh_ready, 1)
                        elif kind == "a_turn":
                            dve.wait_ge(xhT_made, 1)
                            dve.tensor_copy(xhT[:].rearrange("p k s -> p (k s)"), bank16(PA)).then_inc(xhT_ready, 1)
                        elif kind == "qkv_bias":
                            dve.wait_ge(qkv_rounded, NT)
                            if not has_tail:
                                dve.wait_ge(bias_ready, 1)
                            dve.tensor_tensor(qk16[:], qkv16[:, :, 0:NQK * HD],
                                              bqkv_h[:, 0:NQK * HD].unsqueeze(1).to_broadcast([P, NT, NQK * HD]),
                                              ALU.add).then_inc(qk_biased, 1)
                        elif kind == "mean_square":
                            dve.wait_ge(qk_squared, 1)
                            link(dve.tensor_reduce(ms[:], sq[:], AX.X, ALU.add))
                            dve.tensor_scalar(msv[:], ms[:], 1.0 / HD, RMS_EPS, ALU.mult, ALU.add)\
                               .then_inc(ms_ready, 1)
                        elif kind == "inv_rms":
                            dve.wait_ge(ms_ready, 1)
                            dve.wait_ge(y0_ready, 1)
                            link(dve.scalar_tensor_tensor(y1[:], msv[:], -0.5, y0[:], ALU.mult, ALU.mult))
                            link(dve.tensor_tensor(y1[:], y1[:], y0[:], ALU.mult))
                            link(dve.scalar_tensor_tensor(y1[:], y1[:], 1.5, y0[:], ALU.add, ALU.mult))
                        elif kind == "rms_scale":
                            if not has_tail:
                                dve.wait_ge(once_used, 2)
                            dve.tensor_tensor(qkn, qk16[:].rearrange("p i (h d) -> p (i h) d", d=HD),
                                              y1[:].unsqueeze(2).to_broadcast([P, NT * NQK, HD]), ALU.mult)\
                               .then_inc(qk_normed, 1)
                        elif kind == "sines":
                            q, h0, h1 = TURNED[a[0]]
                            dve.wait_ge(qk_normed, 1)
                            if not has_tail:
                                dve.wait_ge(rope_ready, 1)
                            dve.tensor_tensor(heads(rota[:], h0, h1), heads(qkn, h0, h1),
                                              turn(0, q, h1 - h0), ALU.mult).then_inc(cos_made, 1)
                        elif kind == "rotate_keys":
                            dve.wait_ge(cos_made, 1)
                            dve.wait_ge(sin_made, 1)
                            if not has_tail:
                                dve.wait_ge(keys_cleared, 1)
                            dve.tensor_tensor(ka[:, :, :, 0:HD], heads(rota[:], NH, NQK), heads(rotb, NH, NQK),
                                              ALU.add).then_inc(k_rotated, 1)
                        elif kind == "rotate_queries":
                            dve.wait_ge(cos_made, len(TURNED))
                            dve.wait_ge(sin_made, len(TURNED))
                            if not has_tail:
                                dve.wait_ge(queries_cleared, 1)
                            dve.tensor_tensor(qa[:, :, :, 0:HD], heads(rota[:], 0, NH), heads(rotb, 0, NH),
                                              ALU.add).then_inc(q_rotated, 1)
                        elif kind == "keysT":
                            dve.wait_ge(kT_made, 1)
                            dve.tensor_copy(kT[:], bank16(PA)[:, 0:S]).then_inc(kT_ready, 1)
                        elif kind == "first":
                            g, n = a
                            i, r0, nr = UNITS[n]
                            u, w = NU * g + n, (i + 1) * P
                            dve.wait_ge(first_made, u + 1)
                            dve.tensor_reduce(
                                smax[:, i, REP * g + r0:REP * g + r0 + nr],
                                PS[:, FIRST_BANKS[u % len(FIRST_BANKS)], 0:nr * w].rearrange("p (r w) -> p r w", r=nr),
                                AX.X, ALU.max).then_inc(max_taken, 1)
                        elif kind == "shift":
                            (g,) = a
                            dve.wait_ge(max_taken, NU * (g + 1))
                            if g == 0:
                                dve.wait_ge(qT1_made, 2)
                            hs = slice(REP * g, REP * g + REP)
                            link(dve.tensor_scalar(qa[:, :, hs, HD], smax[:, :, hs], -1.0 / SHIFT, None, ALU.mult))
                            dve.scalar_tensor_tensor(qa[:, :, hs, HD + 1], smax[:, :, hs], -1.0 / SHIFT,
                                                     qa[:, :, hs, HD], ALU.mult, ALU.subtract).then_inc(shift_ready, 1)
                        elif kind == "normalize":
                            (g,) = a
                            dve.wait_ge(prob_used, NU * (g + 1))
                            o = PS[:, PO, 0:NT * REP * (HD + 1)].rearrange("p (i r d) -> p i r d", i=NT, r=REP)
                            link(dve.reciprocal(rsum[:], o[:, :, :, HD]))
                            dve.tensor_tensor(
                                o16[:, :, g * REP * HD:(g + 1) * REP * HD].rearrange("p i (r d) -> p i r d", r=REP),
                                o[:, :, :, 0:HD], rsum[:].unsqueeze(3).to_broadcast([P, NT, REP, HD]),
                                ALU.mult).then_inc(o_ready, 1)
                        elif kind == "outT":
                            dve.wait_ge(oT_made, 1)
                            dve.tensor_copy(oT[:].rearrange("p k s -> p (k s)"), bank16(PA)).then_inc(oT_ready, 1)
                        elif kind == "a_residual":
                            dve.wait_ge(att_rounded, NT)
                            link(dve.tensor_tensor(y16, y16, bo_h[:].unsqueeze(1).to_broadcast([P, NT, D]), ALU.add))
                            dve.tensor_tensor(xin[:], xin[:], y16, ALU.add).then_inc(attended, 1)
                        elif kind == "carry":
                            dve.wait_ge(xr_free, 1)
                            dve.tensor_copy(xr[:], xin[:]).then_inc(carried, 1)
                        elif kind == "stats":
                            (n,) = a
                            if n == 0:
                                dve.wait_ge(attended, 1)
                            else:
                                dve.wait_ge(xr_ready, n)
                            statistics(xr if n else xin, n_stat, n_mv, n_veps).then_inc(nvar_ready, 1)
                        elif kind == "apply":
                            (n,) = a
                            dve.wait_ge(nrstd_ready, norms(n))
                            for i in range(NT):
                                dve.tensor_scalar((xn if n else xn0)[:, i], (xr if n else xin)[:, i], n_mv[:, i, 0:1], n_rstd[:, i:i + 1],
                                                  ALU.subtract, ALU.mult).then_inc(xn_ready, 1)
                        elif kind == "turn":
                            (n,) = a
                            for kc in range(KC):
                                dve.wait_ge(xT_hi_ready, KC * (norms(n) - 1) + kc + 1)
                                dve.tensor_tensor(xT_lo[:, kc], PS[:, PG + kc], xT_hi[:, kc].bitcast(F32),
                                                  ALU.subtract).then_inc(xT_lo_ready, 1)
                        elif kind == "top2":
                            (f,) = a
                            dve.wait_ge(logits_made, f + 1)
                            link(dve.tensor_reduce(
                                lg[:], PS[:, PC, 0:NT * 2 * NE].rearrange("p (i h e) -> p i e h", i=NT, h=2),
                                AX.X, ALU.add))
                            for i in range(NT):
                                last = dve.max(top8[:, i], lg[:, i])
                            link(last)
                            dve.tensor_tensor(gap[:], top8[:, :, 1], top8[:, :, 0], ALU.subtract)\
                               .then_inc(gap_ready, 1)
                            for i in range(NT):
                                last = dve.max_index(tidx[:, i], top8[:, i], lg[:, i])
                            link(last)
                            link(dve.tensor_copy(tidf[:], tidx[:]))
                            for k in range(2):
                                last = dve.tensor_tensor(
                                    ceq[:, k], iota_s[:].unsqueeze(1).to_broadcast([P, NT, NE]),
                                    tidf[:, :, k:k + 1].to_broadcast([P, NT, NE]), ALU.is_equal)
                            dve.wait_ge(e2_ready, f + 1)
                            link(dve.tensor_scalar(w12[:, 1], e2[:], 1.0, None, ALU.add))
                            link(dve.reciprocal(w12[:, 0], w12[:, 1]))
                            link(dve.tensor_tensor(w12[:, 1], w12[:, 0], e2[:], ALU.mult))
                            link(dve.tensor_tensor(ceq[:].rearrange("p k i e -> p (k i) e"),
                                                   ceq[:].rearrange("p k i e -> p (k i) e"),
                                                   w12[:].rearrange("p k i -> p (k i)").unsqueeze(2)
                                                   .to_broadcast([P, 2 * NT, NE]), ALU.mult))
                            link(dve.tensor_tensor(cw[:], ceq[:, 0], ceq[:, 1], ALU.add))
                            link(dve.tensor_copy(chl[:, :, 0:NE], cw[:]))
                            dve.tensor_tensor(chl[:, :, NE:], cw[:], chl[:, :, 0:NE].bitcast(F32),
                                              ALU.subtract).then_inc(c_ready, 1)
                        elif kind == "gate":
                            f, j = a
                            q = NJ * f + j
                            dve.wait_ge(tanh_ready, q + 1)
                            dve.scalar_tensor_tensor(sg[:, q % 2], sg[:, q % 2], 1.0, PS[:, PG], ALU.add, ALU.mult)\
                               .then_inc(silu_ready, 1)
                        elif kind == "hidden":
                            f, j = a
                            q, m = NJ * f + j, M0["ffn", f] + j
                            dve.wait_ge(silu_ready, q + 1)
                            dve.wait_ge(cb_made, q + 1)
                            dve.tensor_tensor(sc[:, q % 2], sg[:, q % 2], PS[:, PC], ALU.mult).then_inc(scaled, 1)
                            dve.wait_ge(scaled, q + 1)
                            dve.wait_ge(up_made, q + 1)
                            if m >= RH:
                                dve.wait_ge(lo_ready, m + 1 - RH)
                            dve.tensor_tensor(hf[:, m % RH], sc[:, q % 2], PS[:, PU], ALU.mult).then_inc(h_ready, 1)
                        elif kind == "residual":
                            (n,) = a
                            dve.wait_ge(h_used, (NJ, NJ + NB * KC, 2 * NJ + NB * KC)[n])
                            for k in range(2):
                                last = dve.tensor_tensor(
                                    xr[:, 2 * k:2 * k + 2], xr[:, 2 * k:2 * k + 2],
                                    PS[:, PY[k]].rearrange("p (i c) -> p i c", i=2), ALU.add)
                            last.then_inc(xr_ready, 1)
                        elif kind == "mem_split":
                            for kc in range(KC):
                                dve.wait_ge(mexp_ready, kc + 1)
                                last = dve.scalar_tensor_tensor(sq_f[:, kc], mexp[:, kc], 1.0, mrelu[:, kc],
                                                                ALU.min, ALU.add)
                            last.then_inc(sq_ready, 1)
                        elif kind == "mem_inv":
                            dve.wait_ge(sq_ready, 1)
                            dve.wait_ge(norm_made, 1)
                            link(dve.tensor_scalar(nrec, PS[:, PC], MEM_EPS, None, ALU.max))
                            link(dve.reciprocal(nrec, nrec))
                            link(dve.tensor_copy(rr[:], nrec))
                            h = slice(NB * MH, 2 * NB * MH)
                            dve.tensor_tensor(rr[h], nrec[h], rr[h].bitcast(F32), ALU.subtract).then_inc(rr_ready, 1)
                        elif kind == "mem_scale":
                            (m,) = a
                            u = M0["mem", 0] + m
                            dve.wait_ge(rb_made, m + 1)
                            dve.wait_ge(lo_ready, u + 1 - RH)
                            dve.tensor_tensor(hf[:, u % RH], sq_f[:, m % KC], PS[:, PG + m % 3], ALU.mult)\
                               .then_inc(h_ready, 1)

                @block.gpsimd
                def _(pool):
                    def low(m):
                        pool.wait_ge(hi_ready, m + 1)
                        if m >= RH:
                            pool.wait_ge(h_used, m + 1 - RH)
                        pool.tensor_tensor(hlo[:, m % RH], hf[:, m % RH], hhi[:, m % RH].bitcast(F32),
                                           ALU.subtract).then_inc(lo_ready, 1)

                    for kind, *a in schedule:
                        if kind == "presets":
                            pool.memset(mhalf[:], -0.5)
                            pool.memset(ka[:].bitcast(U32), 0).then_inc(keys_cleared, 1)
                            pool.wait_ge(keys_cleared, 1)
                            pool.memset(ka[:, :, :, HD:HD + 2], SHIFT).then_inc(keys_set, 1)
                            pool.memset(vaug[:], 1.0)
                            pool.memset(kbd[:].bitcast(U32), 0).then_inc(copies_cleared, 1)
                        elif kind == "tables":
                            pool.wait_ge(first_loaded, 16)
                            pool.wait_ge(scales_ready, 1)
                            for n in range(2):
                                for q in range(2):
                                    last = pool.tensor_tensor(
                                        rope[:, n, q], first["turns"][:, n],
                                        first["nscale"][:, n, q].unsqueeze(1).to_broadcast([P, NT, HD]), ALU.mult)
                            last.then_inc(rope_ready, 1)
                        elif kind == "norms":
                            pool.wait_ge(late_loaded, 16)
                            pool.tensor_tensor(
                                mem_bd[:].rearrange("p n k (h d) -> p (n k) h d", h=HP),
                                late_v["mem"].rearrange("p n k d -> p (n k) d").unsqueeze(2)
                                .to_broadcast([P, NB * KC, HP, MD]),
                                late_v["headmask"].unsqueeze(1).unsqueeze(3).to_broadcast([P, NB * KC, HP, MD]),
                                ALU.mult).then_inc(mem_placed, 1)
                            pool.memset(norm_f[:], 0.0).then_inc(pool_set, 1)
                            pool.wait_ge(pool_set, 1)
                            for kc in range(KC):
                                for dup in range(2):
                                    last = pool.tensor_tensor(
                                        norm_f[:, kc, dup, :, kc * HP:(kc + 1) * HP],
                                        late_v["mnorm"][:, kc].unsqueeze(2).to_broadcast([P, NB, HP]),
                                        late_v["headmask"].unsqueeze(1).to_broadcast([P, NB, HP]), ALU.mult)
                            last.then_inc(pool_set, 1)
                            pool.wait_ge(pool_set, 2)
                            halves = ((norm_f[:].rearrange("p k u n h -> p k (u n h)"), norm_hi[:], norm_lo[:]),
                                      (late_v["wr"], wr_hl[:, :, 0], wr_hl[:, :, 1]), (late_v["mwq"], mwq_hi[:], mwq_lo[:]))
                            for f_, hi_, _ in halves:
                                last = pool.tensor_copy(hi_, f_)
                            last.then_inc(pool_set, 1)
                            pool.wait_ge(pool_set, 3)
                            for f_, hi_, lo_ in halves:
                                pool.tensor_tensor(lo_, f_, hi_.bitcast(F32), ALU.subtract)
                        elif kind == "split":
                            (w,) = a
                            pool.wait_ge(whi_ready, w + 1)
                            pool.wait_ge(staged[w], 16)
                            pool.tensor_tensor(wlo[:, w], wstage[:, w % 2], whi[:, w].bitcast(F32), ALU.subtract)\
                                .then_inc(wlo_ready, 1)
                        elif kind == "a_stats":
                            if not has_tail:
                                pool.wait_ge(queries_cleared, 1)
                            pool.memset(qa[:, :, :, HD:HD + 2], 0.0).then_inc(shift_cleared, 1)
                            pool.wait_ge(var_ready, 1)
                            pool.tensor_tensor(a_rstd[:], a_veps[:], mhalf[:], ALU.pow).then_inc(rstd_ready, 1)
                        elif kind == "qkv_bias":
                            pool.wait_ge(qkv_rounded, NT)
                            if not has_tail:
                                pool.wait_ge(bias_ready, 1)
                            pool.tensor_tensor(
                                vaug[:, :, :, 0:HD],
                                qkv16[:, :, D + NG * HD:].rearrange("p i (g d) -> p i g d", g=NG),
                                bqkv_h[:, D + NG * HD:].rearrange("p (g d) -> p g d", g=NG).unsqueeze(1)
                                .to_broadcast([P, NT, NG, HD]), ALU.add).then_inc(v_ready, 1)
                        elif kind == "sines":
                            q, h0, h1 = TURNED[a[0]]
                            pool.wait_ge(qk_normed, 1)
                            if not has_tail:
                                pool.wait_ge(once_used, 2)
                                pool.wait_ge(rope_ready, 1)
                            for c, z in ((0, HD // 2), (HD // 2, 0)):
                                last = pool.tensor_tensor(
                                    heads(rotb, h0, h1)[:, :, :, c:c + HD // 2],
                                    heads(qkn, h0, h1)[:, :, :, z:z + HD // 2],
                                    turn(1, q, h1 - h0)[:, :, :, c:c + HD // 2], ALU.mult)
                            last.then_inc(sin_made, 1)
                        elif kind == "stats":
                            (n,) = a
                            pool.wait_ge(nvar_ready, norms(n))
                            pool.tensor_tensor(n_rstd[:], n_veps[:], mhalf[:], ALU.pow).then_inc(nrstd_ready, 1)
                        elif kind == "hidden":
                            f, j = a
                            low(M0["ffn", f] + j)
                        elif kind == "mem_split":
                            pool.wait_ge(sq_hi_ready, 1)
                            pool.tensor_tensor(sq_lo, sq_f[:], sq_hi.bitcast(F32), ALU.subtract)\
                                .then_inc(sq_lo_ready, 1)
                        elif kind == "mem_scale":
                            (m,) = a
                            low(M0["mem", 0] + m)
            clear()

        FIRST_BANKS, SECOND_BANKS = (PA, PG), (PB, PU)
        sequences(PROLOGUE, x_v[0], None)

        staging.close()
        xr = sb("xr", [P, NT, D])
        lg = sb("lg", [P, NT, NE])
        top8 = sb("top8", [P, NT, 8])
        tidx = sb("tidx", [P, NT, 8], U32)
        tidf = sb("tidf", [P, NT, 8])
        gap = sb("gap", [P, NT])
        e2 = sb("e2", [P, NT])
        w12 = sb("w12", [P, 2, NT])
        ceq = sb("ceq", [P, 2, NT, NE])
        cw = sb("cw", [P, NT, NE])
        chl = sb("chl", [P, NT, 2 * NE], F32R)
        sg = sb("sg", [P, 2, S])
        xn = sg[:].rearrange("p a s -> p (a s)").rearrange("p (i c) -> p i c", i=NT)
        mexp = sg
        sc = sb("sc", [P, 2, S])
        mrelu = sc
        hf = sb("hf", [P, RH, S])
        hhi = sb("hhi", [P, RH, S], F32R)
        hlo = sb("hlo", [P, RH, S], F32R)
        sq_f = sb("sq_f", [P, KC, S])
        sq_hi, sq_lo = hhi[:, 0:KC], hlo[:, 0:KC]
        nrec = sc[:, 0]
        rr = sb("rr", [P, S], F32R)
        cT = rr[0:2 * NE]

        FIRST_BANKS, SECOND_BANKS = (PA,), (PB,)
        nc.sync.sem_inc(stored, 16)
        with nc.Fori(0, B - 1) as b:
            sequences(STEADY, x_v[bass.ds(b + 1, 1)].rearrange("a p i c -> (a p) i c"),
                      out_v[bass.ds(b, 1)].rearrange("a p i c -> (a p) i c"))
        sequences(EPILOGUE, None, out_v[B - 1])


def kernel(**inputs):
    import concourse.bacc as _bacc
    from concourse.bass_utils import run_bass_kernel_spmd as _run

    f = lambda a: np.ascontiguousarray(a, dtype=np.float32)
    g = {k: np.asarray(v) for k, v in inputs.items()}
    rows = lambda a, *shape: f(np.broadcast_to(a, (P, *shape)))

    inv = (1.0 / 10000.0 ** (np.arange(0, HD, 2, dtype=np.float32) / HD)).astype(np.float32)
    ang = np.outer(np.arange(S, dtype=np.float32), inv).astype(np.float32)
    by_tile = lambda a: f(a.reshape(NT, P, HD).transpose(1, 0, 2))
    cos = by_tile(np.concatenate([np.cos(ang), np.cos(ang)], 1))
    sin = by_tile(np.concatenate([-np.sin(ang), np.sin(ang)], 1))
    p = np.arange(P)
    ident = f(np.eye(P))
    mask = f(np.where(p[None, :] > p[:, None], MASKED, 0.0))
    headmask = f(p[:, None] // MD == np.arange(HP)[None, :])
    iota = rows(np.arange(NE), NE)
    selc = f(np.tile(np.arange(NE)[:, None] == np.arange(FT)[None, :] // FI, (2, 1)))
    row = np.arange(P) % (NB * MH)
    n_, kc_, c_ = np.ix_(np.arange(NB), np.arange(KC), p)
    selr = f(row[:, None, None, None] == (n_ * MH + kc_ * HP + c_ // MD)[None])

    qs, ks = g["L0_attn_a_q_norm_scale"], g["L0_attn_a_k_norm_scale"]
    swap = lambda a: np.concatenate([a[HD // 2:], a[:HD // 2]])
    scales = lambda q, k: rows(np.stack([q, k]), 2, HD)
    mem = g["L0_attn_b_memories"]
    mno = g["L0_attn_b_memory_norms"]
    bank = g["L0_attn_b_bank_weights"]
    by_row = lambda a: a.reshape(KC, P, -1).transpose(1, 0, 2)
    small = {
        "wqkv": by_row(np.concatenate([g["L0_attn_a_wq"], g["L0_attn_a_wk"], g["L0_attn_a_wv"]], 1)),
        "bqkv": rows(np.concatenate([g["L0_attn_a_bq"], g["L0_attn_a_bk"], g["L0_attn_a_bv"]]), QKV),
        "nscale": np.stack([scales(qs, ks), scales(swap(qs), swap(ks))], 1), "turns": np.stack([cos, sin], 1),
        "wo": by_row(g["L0_attn_a_wo"]), "bo": rows(g["L0_attn_a_bo"], D),
        "wr": by_row(g["L0_ffn_Wr"]), "mwq": by_row(g["L0_attn_b_Wq"].T), "mwo": by_row(g["L0_attn_b_Wo"].T),
        "mem": f(mem.reshape(NB, KC, HP, MD, MD).transpose(2, 4, 0, 1, 3).reshape(P, NB, KC, MD)),
        "mnorm": f(mno.reshape(NB, KC, P).transpose(2, 1, 0)),
        "mnorm_all": rows(mno.reshape(NB, MH * MD), NB, MH * MD),
        "bank": f(np.repeat(bank, MD, axis=0).reshape(KC, P, NB).transpose(1, 0, 2)),
        "ident": ident, "mask": mask, "headmask": headmask, "iota": iota, "selr": selr,
    }
    packed = lambda pack: f(np.concatenate([small[n].reshape(P, -1) for n in pack], 1))
    arrays = {
        "x": f(g["L0_attn_a_x"]),
        "first_pack": packed(FIRST_PACK), "once_pack": packed(ONCE_PACK), "late_pack": packed(LATE_PACK),
        "selc": selc,
        "wg": f(g["L0_ffn_Wg"].transpose(1, 0, 2).reshape(D, FT)),
        "wu": f(g["L0_ffn_Wu"].transpose(1, 0, 2).reshape(D, FT)),
        "wd": f(g["L0_ffn_Wd"].reshape(FT, D)),
    }
    nc = _bacc.Bacc("TRN2", target_bir_lowering=False, num_devices=1)
    args = {n: nc.dram_tensor(f"in_{n}", a.shape, F32, kind="ExternalInput").ap() for n, a in arrays.items()}
    out = nc.dram_tensor("out", (B, S, D), F32, kind="ExternalOutput").ap()
    build(nc, **args, out=out)
    r = _run(nc, [{f"in_{n}": a for n, a in arrays.items()}], core_ids=[0])
    return r.results[0]["out"]
```

```python
from contextlib import ExitStack

import numpy as np

import concourse.bass as bass
from concourse import mybir

ALU = mybir.AluOpType
ACT = mybir.ActivationFunctionType
AX = mybir.AxisListType
F32 = mybir.dt.float32
F32R = mybir.dt.float32r
F16 = mybir.dt.float16
BF16 = mybir.dt.bfloat16
U32 = mybir.dt.uint32

P = 128
B, S, D = 4, 512, 256
NT = S // P
KC = D // P
NH, NG, HD = 16, 4, 16
REP = NH // NG
QKV = D + 2 * NG * HD
NQK = NH + NG
QROW = 32
SHIFT = 16.0
NE, FI = 8, 176
FT = NE * FI
NJ = FT // P
MH, NB = 16, 4
MD = D // MH
HP = P // MD
LN_EPS, RMS_EPS, MEM_EPS = 1e-5, 1e-6, 1e-6
MASKED = -1e30
ATT_SCALE = HD ** -0.5
NS = 3


def score_units():
    return [(i, r, n) for i, n in ((3, 1), (2, 1), (1, 2), (0, 4)) for r in range(0, REP, n)]


UNITS = score_units()
NU = len(UNITS)
TURNED = [(1, NH, NQK)] + [(0, h, h + REP) for h in range(0, NH, REP)]
LAG = 2
M0 = {("ffn", 0): 0, ("mem", 0): NJ, ("ffn", 1): NJ + NB * KC}
LOW_BY_DVE = [NJ - 1] + [NJ + m for m in range(NB * KC) if m % 2] + [2 * NJ + NB * KC - 1]


def attention_steps():
    steps = [("a_stats",), ("a_apply",), ("a_turn",)]
    steps += [("qkv", i) for i in range(NT)]
    steps += [("qkv_bias",), ("square",), ("mean_square",), ("inv_rms",), ("rms_scale",)]
    steps += [("sines", 0), ("sines", 1), ("rotate_keys",), ("keysT",)]
    steps += [("sines", n) for n in range(2, len(TURNED))]
    steps += [("rotate_queries",), ("queriesT", 0), ("queriesT", 1)]
    for u in range(NG * NU + NU + 1 + LAG):
        g, n = divmod(u, NU)
        if g < NG:
            steps.append(("first", g, n))
            if n == NU - 1:
                steps.append(("shift", g))
        g, n = divmod(u - NU - 1, NU)
        if 0 <= g < NG:
            if n == 0:
                steps.append(("shiftedT", g))
            steps.append(("second", g, n))
        g, n = divmod(u - NU - 1 - LAG, NU)
        if 0 <= g < NG:
            steps.append(("values", g, n))
            if n == NU - 1:
                steps.append(("normalize", g))
    steps.append(("outT",))
    for i in range(NT):
        steps += [("project", i), ("a_residual", i)]
    return steps


def ffn_steps(f):
    s = [("router", f), ("gate", f, 0), ("logits", f), ("top2", f), ("silu", f, 0), ("up", f, 0), ("weights", f),
         ("gate", f, 1), ("combineT", f), ("silu", f, 1), ("spread", f, 0), ("hidden", f, 0)]
    s += [("carry",)] if f == 0 else []
    for j in range(1, NJ):
        s += [("spread", f, j), ("up", f, j), ("hidden", f, j)]
        if j + 1 < NJ:
            s += [("gate", f, j + 1), ("silu", f, j + 1)]
        if j < NJ - 2:
            s.append(("down", f, j - 1))
    return s + [("down", f, NJ - 3), ("low", M0["ffn", f] + NJ - 1), ("down", f, NJ - 2), ("down", f, NJ - 1)]


def tail_steps():
    s = []
    for n in range(NS):
        if n >= 1:
            s += [("stats", n), ("apply", n), ("turn", n)]
        if n == 1:
            s += [("mem_q", kc) for kc in range(KC)]
            s += [("mem_split", kc) for kc in range(KC)] + [("mem_low", kc) for kc in range(KC)]
            s += [("mem_norm",), ("mem_inv",)]
            for m in range(NB * KC):
                s += [("mem_rows", m), ("mem_scale", m)]
                if m and NJ + m - 1 in LOW_BY_DVE:
                    s.append(("low", NJ + m - 1))
                if m >= 2:
                    s.append(("mem_out", m - 2))
            s.append(("low", NJ + NB * KC - 1))
            s += [("mem_out", m) for m in (NB * KC - 2, NB * KC - 1)]
        else:
            s += ffn_steps(n // 2)
        s.append(("residual", n))
    return s


FIRST_NORM = [("stats", 0), ("apply", 0), ("turn", 0)]


def merge(one, beside, other):
    out, k = [], 0
    for step, n in zip(one, beside):
        out += [step] + other[k:k + n]
        k += n
    return out + other[k:]


BESIDE_TAIL = (0, 0, 1, 0, 1, 0, 0, 0, 0, 1, 1, 0, 1, 0, 1, 0, 0, 0, 1, 1, 0, 0, 0, 0, 1, 0, 0, 1, 0, 0, 1, 0, 0,
    1, 0, 0, 0, 0, 1, 1, 0, 0, 1, 0, 0, 0, 1, 1, 0, 0, 1, 0, 0, 1, 0, 0, 0, 0, 1, 0, 0, 0, 0, 0, 0,
    2, 1, 1, 1, 0, 0, 2, 0, 1, 7, 3, 1, 1, 3, 0, 2, 3, 2, 2, 2, 0, 0, 0, 1, 0, 2, 7, 4, 0, 2, 0, 2,
    0, 1, 0, 1, 0, 0, 2, 0, 2, 0, 0, 0, 0, 0, 2, 0, 4, 5, 8, 3, 0, 0, 1, 1, 2, 0, 0, 2, 2, 1, 2, 3,
    0, 2, 2, 0, 0, 1, 1, 3, 1, 1, 1, 0, 2, 1, 2, 1, 2, 2, 0, 2, 0, 2, 0, 1, 0, 3, 0, 1, 0, 1, 0, 2,
    0, 0, 3, 4, 1, 2, 0, 1, 1, 4, 0, 0, 0, 0, 0, 1, 1, 0, 1, 1, 3)
SET_UP_AT = (11, 12, 14, 22, 31, 47, 56, 83, 143)
ALONE, TAIL = attention_steps(), tail_steps()
SET_UP = [("banks",), ("norms",)] + [("combine", n) for n in range(NB)] + [("split", w) for w in range(3)]
SQUARE, SCORES = ALONE.index(("square",)), ALONE.index(("first", 0, 0))
BESIDE_SCORES = [SET_UP_AT.count(n) for n in range(len(ALONE) - SCORES)]
PROLOGUE = ([("presets",), ALONE[0], ("weights16",), ("tables",)] + ALONE[1:SQUARE + 1] + [("selections",)]
            + ALONE[SQUARE + 1:SCORES] + merge(ALONE[SCORES:], BESIDE_SCORES, SET_UP) + FIRST_NORM)
LAST_CHUNK = TAIL.index(("spread", 1, NJ - 1))
STEADY = (merge(TAIL[:LAST_CHUNK], BESIDE_TAIL, ALONE) + FIRST_NORM[:2] + TAIL[LAST_CHUNK:-2]
          + FIRST_NORM[2:] + TAIL[-2:])
EPILOGUE = TAIL
RH = 3
PA, PB, PO, PG, PU, PC, PY = 0, 1, 2, 3, 4, 5, (6, 7)
LENT_FROM = {("stats", 1): 1, ("mem_norm",): 2, ("stats", 2): 3}
LENT_TO = (("turn", 1), ("mem_rows", 0), ("turn", 2))


def place_scores(schedule):
    has_tail = ("carry",) in schedule
    banks = {"first": (PA, PG), "second": (PB, PU)}
    if not has_tail:
        banks = {"first": (PA, PG, PC), "second": (PB, PU, PY[1])}
    loan = None if has_tail else 0
    place, ended, last = {}, {}, {}
    recent = {"first": 0, "second": 0}
    for step in schedule:
        if step in LENT_FROM:
            loan = LENT_FROM[step]
            last[PG] = last[PU] = None
        elif step in LENT_TO:
            ended[step] = (last.get(PG), last.get(PU))
            loan = None
        elif step[0] in recent:
            n = (recent[step[0]] + 1) % len(banks[step[0]]) if loan is not None else 0
            bank = banks[step[0]][n]
            before = last.get(bank)
            place[step] = (bank, before, loan if n and before is None else None)
            last[bank], recent[step[0]] = NU * step[1] + step[2], n
        elif step[0] == "shiftedT":
            place[step] = (PB, last.get(PB), None)
            recent["second"] = 0
    return place, ended


FIRST_PACK = {"ident": (P,), "wqkv": (KC, QKV), "bqkv": (QKV,), "mask": (P,), "nscale": (2, 2, HD),
              "turns": (2, NT, HD), "wo": (KC, D), "bo": (D,)}
ONCE_PACK = {"selr": (NB, KC, P), "mnorm_all": (NB, MH * MD)}
LATE_PACK = {"iota": (NE,), "headmask": (HP,), "wr": (KC, NE), "mwq": (KC, D), "mwo": (KC, D),
             "mem": (NB, KC, MD), "mnorm": (KC, NB), "bank": (KC, NB)}


def width(pack):
    return sum(int(np.prod(shape)) for shape in pack.values())


def build(nc, x, first_pack, once_pack, late_pack, selc, wg, wu, wd, out):
    x_v = x.rearrange("b (i p) c -> b p i c", p=P)
    out_v = out.rearrange("b (i p) c -> b p i c", p=P)
    with ExitStack() as ctx:
        staging = ctx.enter_context(ExitStack())

        def sb(name, shape, dt=F32, only=ctx):
            return only.enter_context(nc.sbuf_tensor(name, shape, dt))

        sems = []

        def sem(name):
            sems.append(ctx.enter_context(nc.semaphore(name)))
            return sems[-1]

        ident_f = sb("ident_f", [P, P])
        ident_h = sb("ident_h", [P, P], F16)
        ident_b = sb("ident_b", [P, P], BF16)
        mask_b = sb("mask_b", [P, P], BF16)
        iota_s = sb("iota_s", [P, NE])
        wqkv_h = sb("wqkv_h", [P, KC, QKV], F16)
        bqkv_h = sb("bqkv_h", [P, QKV], F16)
        rope = sb("rope", [P, 2, 2, NT, HD])
        wo_h = sb("wo_h", [P, KC, D], F16)
        bo_h = sb("bo_h", [P, D], F16)
        whi = sb("whi", [P, 3, KC * FT], F32R)
        wlo = sb("wlo", [P, 3, KC * FT], F32R)
        gate_hi, gate_lo = (w[:, 0, :].rearrange("p (k f) -> p k f", k=KC) for w in (whi, wlo))
        up_hi, up_lo = (w[:, 1, :].rearrange("p (k f) -> p k f", k=KC) for w in (whi, wlo))
        down_hi, down_lo = (w[:, 2, :].rearrange("p (j c) -> p j c", j=NJ) for w in (whi, wlo))
        wr_hl = sb("wr_hl", [P, KC, 2 * NE], F32R)
        mwq_hi = sb("mwq_hi", [P, KC, D], F32R)
        mwq_lo = sb("mwq_lo", [P, KC, D], F32R)
        norm_hi = sb("norm_hi", [P, KC, 2 * NB * MH], F32R)
        norm_lo = sb("norm_lo", [P, KC, 2 * NB * MH], F32R)
        comb_hi = sb("comb_hi", [P, KC, NB, D], F32R)
        comb_lo = sb("comb_lo", [P, KC, NB, D], F32R)
        selc_r = sb("selc_r", [2 * NE, FT], F32R)
        selr_r = sb("selr_r", [P, NB, KC, P], F32R)
        mhalf = sb("mhalf", [P, NT])

        vaug = sb("vaug", [P, NT, NG, HD + 1], F16)
        qa = sb("qa", [P, NT, NH, QROW], F16)
        ka = sb("ka", [P, NT, NG, QROW], F16)
        kbd = sb("kbd", [P, NG, REP, S], F16)
        xin = sb("xin", [P, NT, D])
        xatt = sb("xatt", [P, NT, D])
        a_stat = sb("a_stat", [P, NT, 6])
        a_mv = sb("a_mv", [P, NT, 2])
        a_veps = sb("a_veps", [P, NT])
        a_rstd = sb("a_rstd", [P, NT])
        xh = sb("xh", [P, NT, D], F16)
        xhT = sb("xhT", [P, KC, S], F16)
        qkv16 = sb("qkv16", [P, NT, QKV], F16)
        qk16 = sb("qk16", [P, NT, NQK * HD], F16)
        sq = sb("sq", [P, NT * NQK, HD])
        rota = sq
        ms = sb("ms", [P, NT * NQK])
        msv = sb("msv", [P, NT * NQK])
        lnv = ms
        y0 = sb("y0", [P, NT * NQK])
        y1 = sb("y1", [P, NT * NQK])
        kT = sb("kT", [P, S], F16)
        qT = sb("qT", [P, NG + 2, S], F16)
        qT1, qT2 = qT[:, 0:NG], qT[:, NG:]
        rotb = qT[:].rearrange("p g s -> p (g s)").bitcast(F32)[:, 0:NT * NQK * HD]\
            .rearrange("p (h d) -> p h d", d=HD)
        smax = sb("smax", [P, NT, NH])
        NPR = 6
        prob = sb("prob", [P, NPR, S], F16)
        qkn = prob[:].rearrange("p n s -> p (n s)").bitcast(F32)[:, 0:NT * NQK * HD]\
            .rearrange("p (h d) -> p h d", d=HD)
        rsum = sb("rsum", [P, NT, REP])
        o16, oT = xh, xhT
        y16 = qkv16[:].rearrange("p i n -> p (i n)")[:, 0:NT * D].rearrange("p (i c) -> p i c", i=NT)

        n_stat = sb("n_stat", [P, NT, 6])
        n_mv = sb("n_mv", [P, NT, 2])
        n_veps = sb("n_veps", [P, NT])
        n_rstd = sb("n_rstd", [P, NT])
        xT_hi = sb("xT_hi", [P, KC, S], F32R)
        xT_lo = sb("xT_lo", [P, KC, S], F32R)
        xn0 = prob[:, 0:4].rearrange("p n s -> p (n s)").bitcast(F32).rearrange("p (i c) -> p i c", i=NT)

        st = lambda name, shape, dt=F32: sb(name, shape, dt, staging)
        wstage = st("wstage", [P, 2, KC * FT])
        late_s = st("late_s", [P, width(LATE_PACK)])
        once_s = st("once_s", [P, width(ONCE_PACK)])

        def views(rows, pack):
            out, n = {}, 0
            for name, shape in pack.items():
                v = rows[:, n:n + int(np.prod(shape))]
                n += int(np.prod(shape))
                letters = "abc"[:len(shape)]
                out[name] = v if len(shape) == 1 else v.rearrange(
                    f"p ({' '.join(letters)}) -> p {' '.join(letters)}", **dict(zip(letters[1:], shape[1:])))
            return out

        first_rows = wstage[:, 1, 0:width(FIRST_PACK)]
        once_rows = once_s[:]
        selc_f = qT[0:2 * NE].rearrange("p g s -> p (g s)").bitcast(F32)[:, 0:FT]
        first, once = views(first_rows, FIRST_PACK), views(once_rows, ONCE_PACK)
        late_v = views(late_s[:], LATE_PACK)
        mem_bd = once_s[:, 0:NB * KC * P].rearrange("p (n k c) -> p n k c", n=NB, k=KC)
        norm_f = st("norm_f", [P, KC, 2, NB, MH])
        mnsum = st("mnsum", [P, NB])
        bmax = st("bmax", [P, KC])
        bsum = st("bsum", [P, KC])
        bankw = st("bankw", [P, KC, NB])
        PS = ctx.enter_context(nc.psum_tensor("PS", [P, 8, 512], F32))

        def bank16(n):
            return PS[:, n, :].bitcast(F16)

        first_loaded, once_loaded, late_loaded = sem("first_loaded"), sem("once_loaded"), sem("late_loaded")
        selc_loaded, staged = sem("selc_loaded"), [sem(f"staged{w}") for w in range(3)]
        ident_ready, weights16, bias_ready = sem("ident_ready"), sem("weights16"), sem("bias_ready")
        masks_ready, scales_ready, rope_ready = sem("masks_ready"), sem("scales_ready"), sem("rope_ready")
        queries_cleared, keys_cleared, keys_set = sem("queries_cleared"), sem("keys_cleared"), sem("keys_set")
        copies_cleared, pool_set, once_used = sem("copies_cleared"), sem("pool_set"), sem("once_used")
        bank_shifted, bank_exped, bank_ready = sem("bank_shifted"), sem("bank_exped"), sem("bank_ready")
        mem_placed, comb_made = sem("mem_placed"), sem("comb_made")
        comb_hi_ready, comb_lo_ready = sem("comb_hi_ready"), sem("comb_lo_ready")
        whi_ready, wlo_ready = sem("whi_ready"), sem("wlo_ready")
        x_loaded = sem("x_loaded")
        var_ready, rstd_ready = sem("var_ready"), sem("rstd_ready")
        xh_ready, xhT_made, xhT_ready = sem("xh_ready"), sem("xhT_made"), sem("xhT_ready")
        qkv_made, qkv_rounded = sem("qkv_made"), sem("qkv_rounded")
        qk_biased, v_ready, qk_squared = sem("qk_biased"), sem("v_ready"), sem("qk_squared")
        ms_ready, y0_ready, qk_normed = sem("ms_ready"), sem("y0_ready"), sem("qk_normed")
        sin_made, cos_made = sem("sin_made"), sem("cos_made")
        q_rotated, k_rotated, shift_cleared = sem("q_rotated"), sem("k_rotated"), sem("shift_cleared")
        kT_made, kT_ready = sem("kT_made"), sem("kT_ready")
        keys_placed = [sem(f"keys_placed{g}") for g in range(NG)]
        qT1_made, qT1_ready = sem("qT1_made"), sem("qT1_ready")
        first_made, max_taken, shift_ready = sem("first_made"), sem("max_taken"), sem("shift_ready")
        qT2_made, qT2_ready = sem("qT2_made"), sem("qT2_ready")
        second_made, prob_ready, prob_used = sem("second_made"), sem("prob_ready"), sem("prob_used")
        o_ready = sem("o_ready")
        oT_made, oT_ready, att_made, att_rounded = sem("oT_made"), sem("oT_ready"), sem("att_made"), sem("att_rounded")
        dve_step, act_step = sem("dve_step"), sem("act_step")
        carried = sem("carried")
        nvar_ready, nrstd_ready = sem("nvar_ready"), sem("nrstd_ready")
        attended, xn_ready, xT_made = sem("attended"), sem("xn_ready"), sem("xT_made")
        xT_hi_ready, xT_lo_ready = sem("xT_hi_ready"), sem("xT_lo_ready")
        routed, lgT_ready = sem("routed"), sem("lgT_ready")
        logits_made, gap_ready, e2_ready = sem("logits_made"), sem("gap_ready"), sem("e2_ready")
        c_ready, cT_made, cT_ready = sem("c_ready"), sem("cT_made"), sem("cT_ready")
        gate_made, up_made, cb_made = sem("gate_made"), sem("up_made"), sem("cb_made")
        tanh_ready, silu_ready, scaled, h_ready = sem("tanh_ready"), sem("silu_ready"), sem("scaled"), sem("h_ready")
        hi_ready, h_used = sem("hi_ready"), sem("h_used")
        lo_by_pool, lo_by_dve = sem("lo_by_pool"), sem("lo_by_dve")
        mq_made, mexp_ready, sq_ready = sem("mq_made"), sem("mexp_ready"), sem("sq_ready")
        sq_hi_ready, sq_lo_ready = sem("sq_hi_ready"), sem("sq_lo_ready")
        norm_made, rr_ready, rb_made = sem("norm_made"), sem("rr_ready"), sem("rb_made")
        xr_ready, xr_counted, xr_free = sem("xr_ready"), sem("xr_counted"), sem("xr_free")
        y_half_made = sem("y_half_made")
        stored = ctx.enter_context(nc.semaphore("stored"))

        def counted(eng, signal):
            count = [0]

            def link(ins):
                count[0] += 1
                ins.then_inc(signal, 1)
                eng.wait_ge(signal, count[0])
            return link

        def wait_for_low(eng, m):
            by_dve = sum(n in LOW_BY_DVE for n in range(m + 1))
            if m in LOW_BY_DVE:
                eng.wait_ge(lo_by_dve, by_dve)
            else:
                eng.wait_ge(lo_by_pool, m + 1 - by_dve)

        def heads(t, h0, h1):
            return t.rearrange("p (i h) d -> p i h d", i=NT)[:, :, h0:h1]

        def turn(n, q, nh):
            return rope[:, n, q].unsqueeze(2).to_broadcast([P, NT, nh, HD])

        def clear():
            nums = [s.num for s in sems]
            assert max(nums) - min(nums) == len(nums) - 1
            nc.sync.sem_clear(range(min(nums), max(nums) + 1))
            nc.all_engine_barrier()

        def sequences(schedule, load_from, store_to):
            has_tail = store_to is not None
            place, ended = place_scores(schedule)

            def norms(n):
                return n if n else (NS if has_tail else 1)

            with nc.Block() as block:

                @block.sync
                def _(sp):
                    if load_from is not None:
                        sp.dma_start(xin[:], load_from).then_inc(x_loaded, 16)
                    if has_tail:
                        sp.wait_ge(stored, 16)
                        sp.sem_clear(stored)
                        sp.sem_inc(xr_free, 1)
                    if not has_tail:
                        sp.dma_start(first_rows, first_pack).then_inc(first_loaded, 16)
                        sp.dma_start(once_rows, once_pack).then_inc(once_loaded, 16)
                        sp.dma_start(selc_f, selc).then_inc(selc_loaded, 16)
                        sp.dma_start(late_s[:], late_pack).then_inc(late_loaded, 16)
                        for w, src in enumerate((wg, wu)):
                            if w == 1:
                                sp.wait_ge(ident_ready, 1)
                                sp.wait_ge(weights16, 2)
                                sp.wait_ge(masks_ready, 1)
                                sp.wait_ge(rope_ready, 1)
                            sp.dma_start(wstage[:, w].rearrange("p (k f) -> p k f", k=KC),
                                         src.rearrange("(k p) f -> p k f", p=P)).then_inc(staged[w], 16)
                        sp.wait_ge(copies_cleared, 1)
                    if load_from is not None:
                        sp.wait_ge(kT_ready, 1)
                        for g in range(NG):
                            for r in range(REP):
                                sp.dma_start(kbd[r * QROW:(r + 1) * QROW, g, r], kT[g * QROW:(g + 1) * QROW])\
                                  .then_inc(keys_placed[g], 16)
                    if not has_tail:
                        sp.wait_ge(wlo_ready, 1)
                        sp.dma_start(wstage[:, 0].rearrange("p (j c) -> p j c", j=NJ),
                                     wd.rearrange("(j p) c -> p j c", p=P)).then_inc(staged[2], 16)
                    else:
                        sp.wait_ge(xr_ready, 2 * NS)
                        sp.dma_start(store_to, xr[:]).then_inc(stored, 16)
                        if load_from is None:
                            sp.wait_ge(stored, 16)

                @block.tensor
                def _(pe):
                    def three(outs, pairs, ready=()):
                        n = 0
                        for k, ((sh, sl), (mh, ml)) in enumerate(pairs):
                            for signal, base in ready:
                                pe.wait_ge(signal, base + k + 1)
                            for s_, m_ in ((sh, mh), (sh, ml), (sl, mh)):
                                n += 1
                                mm = pe.matmul(outs, s_, m_, start=(n == 1), stop=(n == 3 * len(pairs)))
                        return mm

                    def xTs(kc, a, z):
                        return xT_hi[:, kc, a:z], xT_lo[:, kc, a:z]

                    def accumulate(m, first, hi, lo):
                        pe.wait_ge(hi_ready, m + 1)
                        wait_for_low(pe, m)
                        for i in range(NT):
                            for k, (s_, m_) in enumerate(((hhi, hi), (hhi, lo), (hlo, hi))):
                                mm = pe.matmul(PS[:, PY[i // 2], (i % 2) * D:(i % 2 + 1) * D],
                                               s_[:, m % RH, i * P:(i + 1) * P], m_,
                                               start=(first and k == 0 and i % 2 == 0), stop=True,
                                               skip_group_check=True)
                            if i == NT // 2 - 1 and m in (NJ - 1, NJ + NB * KC - 1, 2 * NJ + NB * KC - 1):
                                mm.then_inc(y_half_made, 1)
                        mm.then_inc(h_used, 1)

                    def wait_for_loan(loan):
                        if loan == 1:
                            pe.wait_ge(silu_ready, NJ)
                            pe.wait_ge(h_ready, NJ)
                        elif loan == 2:
                            pe.wait_ge(mexp_ready, KC)
                        elif loan == 3:
                            pe.wait_ge(h_ready, NJ + NB * KC)

                    def wait_for_return(step):
                        first, second = ended.get(step, (None, None))
                        if first is not None:
                            pe.wait_ge(max_taken, first + 1)
                        if second is not None:
                            pe.wait_ge(prob_ready, second + 1)

                    for kind, *a in schedule:
                        if kind == "combine":
                            (n,) = a
                            pe.wait_ge(mem_placed, 1)
                            if n >= 1:
                                pe.wait_ge(comb_lo_ready, n)
                            for kc in range(KC):
                                mm = pe.matmul(PS[:, PY[0], kc * D:(kc + 1) * D], mem_bd[:, n, kc],
                                               late_v["mwo"][:, kc],
                                               start=True, stop=True)
                            mm.then_inc(comb_made, 1)
                        elif kind == "a_turn":
                            if not has_tail:
                                pe.wait_ge(ident_ready, 1)
                            for i in range(NT):
                                pe.wait_ge(xh_ready, i + 1)
                                for kc in range(KC):
                                    mm = pe.transpose(bank16(PA)[:, kc * S + i * P:kc * S + (i + 1) * P],
                                                      xh[:, i, kc * P:(kc + 1) * P], ident_h[:])
                            mm.then_inc(xhT_made, 1)
                        elif kind == "qkv":
                            (i,) = a
                            if i == 0:
                                pe.wait_ge(xhT_ready, 1)
                                if not has_tail:
                                    pe.wait_ge(weights16, 1)
                            if i >= 2:
                                pe.wait_ge(qkv_rounded, i - 1)
                            for kc in range(KC):
                                mm = pe.matmul(PS[:, (PB, PO)[i % 2], 0:QKV], xhT[:, kc, i * P:(i + 1) * P],
                                               wqkv_h[:, kc], start=(kc == 0), stop=(kc == KC - 1))
                            mm.then_inc(qkv_made, 1)
                        elif kind == "keysT":
                            pe.wait_ge(k_rotated, 1)
                            if not has_tail:
                                pe.wait_ge(keys_set, 1)
                                pe.wait_ge(masks_ready, 1)
                            for i in range(NT):
                                mm = pe.transpose(bank16(PA)[:, i * P:(i + 1) * P],
                                                  ka[:, i].rearrange("p g d -> p (g d)"), ident_h[:])
                            mm.then_inc(kT_made, 1)
                        elif kind == "queriesT":
                            (n,) = a
                            pe.wait_ge(q_rotated, 1)
                            pe.wait_ge(shift_cleared, 1)
                            for g in (2 * n, 2 * n + 1):
                                for i in range(NT):
                                    mm = pe.transpose(
                                        bank16((PB, PO)[n])[:, (g % 2) * S + i * P:(g % 2) * S + (i + 1) * P],
                                        qa[:, i, REP * g:REP * (g + 1)].rearrange("p r d -> p (r d)"), ident_h[:])
                            mm.then_inc(qT1_made, 1)
                        elif kind == "first":
                            g, n = a
                            i, r0, nr = UNITS[n]
                            u, w = NU * g + n, (i + 1) * P
                            if n == 0:
                                pe.wait_ge(keys_placed[g], 16 * REP)
                            if u == 0:
                                pe.wait_ge(qT1_ready, 2)
                            bank, before, loan = place["first", g, n]
                            wait_for_loan(loan)
                            if before is not None:
                                pe.wait_ge(max_taken, before + 1)
                            o = PS[:, bank, 0:nr * w].rearrange("p (r w) -> p r w", r=nr)
                            pe.matmul(o, qT1[:, g, i * P:(i + 1) * P], kbd[:, g, r0:r0 + nr, 0:w],
                                      start=True, stop=False, skip_group_check=True)
                            pe.matmul(o[:, :, i * P:w], ident_b[:], mask_b[:].unsqueeze(1).to_broadcast([P, nr, P]),
                                      start=False, stop=True, skip_group_check=True).then_inc(first_made, 1)
                        elif kind == "shiftedT":
                            (g,) = a
                            pe.wait_ge(shift_ready, g + 1)
                            bank, before, _ = place["shiftedT", g]
                            if before is not None:
                                pe.wait_ge(prob_ready, before + 1)
                            for i in range(NT):
                                mm = pe.transpose(bank16(bank)[:, i * P:(i + 1) * P],
                                                  qa[:, i, REP * g:REP * (g + 1)].rearrange("p r d -> p (r d)"),
                                                  ident_h[:])
                            mm.then_inc(qT2_made, 1)
                        elif kind == "second":
                            g, n = a
                            i, r0, nr = UNITS[n]
                            j = NT - 1 - i
                            u, w = NU * g + n, S - j * P
                            if n == 0:
                                pe.wait_ge(qT2_ready, g + 1)
                            bank, before, loan = place["second", g, n]
                            wait_for_loan(loan)
                            if before is not None:
                                pe.wait_ge(prob_ready, before + 1)
                            for k in range(nr):
                                o = PS[:, bank, k * w:(k + 1) * w]
                                pe.matmul(o, kbd[:, g, r0 + k, j * P:(j + 1) * P], qT2[:, g % 2, j * P:S],
                                          start=True, stop=False, skip_group_check=True)
                                mm = pe.matmul(o[:, 0:P], mask_b[:], ident_b[:], start=False, stop=True,
                                               skip_group_check=True)
                            mm.then_inc(second_made, 1)
                        elif kind == "values":
                            g, n = a
                            i0, r0, nr = UNITS[n]
                            j = NT - 1 - i0
                            u, w = NU * g + n, S - j * P
                            if n == 0:
                                if g == 0:
                                    pe.wait_ge(v_ready, 1)
                                else:
                                    pe.wait_ge(o_ready, g)
                            pe.wait_ge(prob_ready, u + 1)
                            o = PS[:, PO, 0:NT * REP * (HD + 1)].rearrange("p (i r d) -> p i r d", i=NT, r=REP)
                            for k in range(nr):
                                for i in range(j, NT):
                                    mm = pe.matmul(o[:, i, r0 + k],
                                                   prob[:, u % NPR, k * w + (i - j) * P:k * w + (i - j + 1) * P],
                                                   vaug[:, j, g], start=(n == 0 and k == 0 and i == 0), stop=True,
                                                   skip_group_check=True)
                            mm.then_inc(prob_used, 1)
                        elif kind == "outT":
                            pe.wait_ge(o_ready, NG)
                            for i in range(NT):
                                for kc in range(KC):
                                    mm = pe.transpose(bank16(PA)[:, kc * S + i * P:kc * S + (i + 1) * P],
                                                      o16[:, i, kc * P:(kc + 1) * P], ident_h[:])
                            mm.then_inc(oT_made, 1)
                        elif kind == "project":
                            (i,) = a
                            if i == 0:
                                pe.wait_ge(oT_ready, 1)
                                if not has_tail:
                                    pe.wait_ge(weights16, 2)
                            if i >= 2:
                                pe.wait_ge(att_rounded, i - 1)
                            for kc in range(KC):
                                mm = pe.matmul(PS[:, (PB, PO)[i % 2], 0:D], oT[:, kc, i * P:(i + 1) * P], wo_h[:, kc],
                                               start=(kc == 0), stop=(kc == KC - 1))
                            mm.then_inc(att_made, 1)
                        elif kind == "turn":
                            (n,) = a
                            src = xn if n else xn0
                            wait_for_return(("turn", n))
                            for kc in range(KC):
                                if n == 0 and has_tail:
                                    pe.wait_ge((silu_ready, h_ready)[kc], (2 * NJ, 2 * NJ + NB * KC)[kc])
                                for i in range(NT):
                                    if kc == 0:
                                        pe.wait_ge(xn_ready, NT * (norms(n) - 1) + i + 1)
                                    mm = pe.transpose(PS[:, PG + kc, i * P:(i + 1) * P],
                                                      src[:, i, kc * P:(kc + 1) * P], ident_f[:])
                                mm.then_inc(xT_made, 1)
                        elif kind == "router":
                            (f,) = a
                            if f == 1:
                                pe.wait_ge(xT_hi_ready, KC * 2)
                                pe.wait_ge(xT_lo_ready, KC * 2)
                            n = 0
                            for kc in range(KC):
                                for m_ in xTs(kc, 0, S):
                                    n += 1
                                    mm = pe.matmul(PS[0:2 * NE, PC], wr_hl[:, kc], m_,
                                                   start=(n == 1), stop=(n == 2 * KC))
                            mm.then_inc(routed, 1)
                        elif kind == "logits":
                            (f,) = a
                            pe.wait_ge(lgT_ready, f + 1)
                            for i in range(NT):
                                mm = pe.transpose(PS[:, PC, i * 2 * NE:(i + 1) * 2 * NE], lgT[:, i * P:(i + 1) * P],
                                                  ident_f[0:2 * NE, 0:2 * NE])
                            mm.then_inc(logits_made, 1)
                        elif kind == "gate":
                            f, j = a
                            q = NJ * f + j
                            if j >= 1:
                                pe.wait_ge(silu_ready, q)
                            cols = slice(j * P, (j + 1) * P)
                            three(PS[:, PG], [((gate_hi[:, kc, cols], gate_lo[:, kc, cols]), xTs(kc, 0, S))
                                              for kc in range(KC)]).then_inc(gate_made, 1)
                        elif kind == "up":
                            f, j = a
                            if j >= 1:
                                pe.wait_ge(h_ready, M0["ffn", f] + j)
                            cols = slice(j * P, (j + 1) * P)
                            three(PS[:, PU], [((up_hi[:, kc, cols], up_lo[:, kc, cols]), xTs(kc, 0, S))
                                              for kc in range(KC)]).then_inc(up_made, 1)
                        elif kind == "combineT":
                            (f,) = a
                            pe.wait_ge(c_ready, f + 1)
                            for i in range(NT):
                                mm = pe.transpose(PS[0:2 * NE, PC, i * P:(i + 1) * P],
                                                  chl[:, i].bitcast(F32), ident_f[:])
                            mm.then_inc(cT_made, 1)
                        elif kind == "spread":
                            f, j = a
                            q = NJ * f + j
                            if j == 0:
                                pe.wait_ge(cT_ready, f + 1)
                            else:
                                pe.wait_ge(scaled, q)
                            pe.matmul(PS[:, PC], selc_r[:, j * P:(j + 1) * P], cT, start=True, stop=True)\
                              .then_inc(cb_made, 1)
                        elif kind == "down":
                            f, j = a
                            accumulate(M0["ffn", f] + j, j == 0, down_hi[:, j], down_lo[:, j])
                        elif kind == "mem_q":
                            (mc,) = a
                            cols = slice(mc * P, (mc + 1) * P)
                            three(PS[:, PG + mc], [((mwq_hi[:, kc, cols], mwq_lo[:, kc, cols]), xTs(kc, 0, S))
                                                   for kc in range(KC)],
                                  ((xT_hi_ready, 0), (xT_lo_ready, 0)) if mc == 0 else ()).then_inc(mq_made, 1)
                        elif kind == "mem_norm":
                            three(PS[:, PC], [((norm_hi[:, kc], norm_lo[:, kc]), (sq_hi[:, kc], sq_lo[:, kc]))
                                              for kc in range(KC)],
                                  ((sq_hi_ready, 0), (sq_lo_ready, 0))).then_inc(norm_made, 1)
                        elif kind == "mem_rows":
                            (m,) = a
                            wait_for_return(("mem_rows", m))
                            if m == 0:
                                pe.wait_ge(rr_ready, 1)
                            if m >= 3:
                                pe.wait_ge(h_ready, M0["mem", 0] + m - 2)
                            pe.matmul(PS[:, PG + m % 3], selr_r[:, m // KC, m % KC], rr[:], start=True, stop=True)\
                              .then_inc(rb_made, 1)
                        elif kind == "mem_out":
                            (m,) = a
                            accumulate(M0["mem", 0] + m, m == 0, comb_hi[:, m % KC, m // KC],
                                       comb_lo[:, m % KC, m // KC])

                @block.scalar
                def _(act):
                    link = counted(act, act_step)

                    def high(m):
                        act.wait_ge(h_ready, m + 1)
                        if m == M0["mem", 0]:
                            act.wait_ge(norm_made, 1)
                        if m >= RH:
                            act.wait_ge(h_used, m + 1 - RH)
                        act.activation(hhi[:, m % RH], hf[:, m % RH], ACT.Copy).then_inc(hi_ready, 1)

                    for kind, *a in schedule:
                        if kind == "weights16":
                            act.wait_ge(first_loaded, 16)
                            act.activation(wqkv_h[:], first["wqkv"], ACT.Copy).then_inc(weights16, 1)
                            act.activation(bqkv_h[:], first["bqkv"], ACT.Copy).then_inc(bias_ready, 1)
                            act.activation(bo_h[:], first["bo"], ACT.Copy)
                            act.activation(wo_h[:], first["wo"], ACT.Copy).then_inc(weights16, 1)
                        elif kind == "selections":
                            act.wait_ge(selc_loaded, 16)
                            act.activation(selc_r[:], selc_f, ACT.Copy, scale=0.5)
                            act.wait_ge(once_loaded, 16)
                            act.activation(selr_r[:], once["selr"], ACT.Copy).then_inc(once_used, 1)
                        elif kind == "banks":
                            act.wait_ge(bank_shifted, 1)
                            act.activation(bankw[:], late_v["bank"], ACT.Exp).then_inc(bank_exped, 1)
                        elif kind == "combine":
                            (n,) = a
                            act.wait_ge(comb_made, n + 1)
                            act.wait_ge(bank_ready, 1)
                            for kc in range(KC):
                                ins = act.activation(comb_hi[:, kc, n], PS[:, PY[0], kc * D:(kc + 1) * D],
                                                     ACT.Copy, scale=bankw[:, kc, n:n + 1])
                            ins.then_inc(comb_hi_ready, 1)
                        elif kind == "split":
                            (w,) = a
                            act.wait_ge(staged[w], 16)
                            act.activation(whi[:, w], wstage[:, w % 2], ACT.Copy).then_inc(whi_ready, 1)
                        elif kind == "qkv":
                            (i,) = a
                            act.wait_ge(qkv_made, i + 1)
                            act.activation(qkv16[:, i], PS[:, (PB, PO)[i % 2], 0:QKV], ACT.Copy)\
                               .then_inc(qkv_rounded, 1)
                        elif kind == "square":
                            act.wait_ge(qk_biased, 1)
                            act.activation(sq[:].rearrange("p h d -> p (h d)"), qk16[:].rearrange("p i n -> p (i n)"),
                                           ACT.Square).then_inc(qk_squared, 1)
                        elif kind == "inv_rms":
                            act.wait_ge(ms_ready, 1)
                            link(act.activation(lnv[:], msv[:], ACT.Ln))
                            act.activation(y0[:], lnv[:], ACT.Exp, scale=-0.5).then_inc(y0_ready, 1)
                        elif kind == "queriesT":
                            (n,) = a
                            act.wait_ge(qT1_made, n + 1)
                            act.activation(qT1[:, 2 * n:2 * n + 2].rearrange("p g s -> p (g s)"),
                                           bank16((PB, PO)[n]), ACT.Copy).then_inc(qT1_ready, 1)
                        elif kind == "shiftedT":
                            (g,) = a
                            act.wait_ge(qT2_made, g + 1)
                            act.activation(qT2[:, g % 2], bank16(place["shiftedT", g][0])[:, 0:S],
                                           ACT.Copy).then_inc(qT2_ready, 1)
                        elif kind == "second":
                            g, n = a
                            i, r0, nr = UNITS[n]
                            u, w = NU * g + n, (i + 1) * P
                            act.wait_ge(second_made, u + 1)
                            if u >= NPR:
                                act.wait_ge(prob_used, u + 1 - NPR)
                            act.activation(prob[:, u % NPR, 0:nr * w],
                                           PS[:, place["second", g, n][0], 0:nr * w],
                                           ACT.Exp, scale=ATT_SCALE).then_inc(prob_ready, 1)
                        elif kind == "project":
                            (i,) = a
                            act.wait_ge(att_made, i + 1)
                            act.activation(y16[:, i], PS[:, (PB, PO)[i % 2], 0:D], ACT.Copy).then_inc(att_rounded, 1)
                        elif kind == "turn":
                            (n,) = a
                            for kc in range(KC):
                                act.wait_ge(xT_made, KC * (norms(n) - 1) + kc + 1)
                                act.activation(xT_hi[:, kc], PS[:, PG + kc], ACT.Copy).then_inc(xT_hi_ready, 1)
                        elif kind == "router":
                            (f,) = a
                            act.wait_ge(routed, f + 1)
                            act.activation(lgT, PS[0:2 * NE, PC], ACT.Copy).then_inc(lgT_ready, 1)
                        elif kind == "top2":
                            (f,) = a
                            act.wait_ge(gap_ready, f + 1)
                            act.activation(e2[:], gap[:], ACT.Exp).then_inc(e2_ready, 1)
                        elif kind == "combineT":
                            (f,) = a
                            act.wait_ge(cT_made, f + 1)
                            act.activation(cT, PS[0:2 * NE, PC], ACT.Copy).then_inc(cT_ready, 1)
                        elif kind == "gate":
                            f, j = a
                            q = NJ * f + j
                            act.wait_ge(gate_made, q + 1)
                            if j >= 2:
                                act.wait_ge(scaled, q - 1)
                            act.activation(sg[:, q % 2], PS[:, PG], ACT.Tanh, scale=0.5).then_inc(tanh_ready, 1)
                        elif kind == "hidden":
                            f, j = a
                            high(M0["ffn", f] + j)
                        elif kind == "mem_q":
                            (kc,) = a
                            act.wait_ge(mq_made, kc + 1)
                            act.activation(mexp[:, kc], PS[:, PG + kc], ACT.Exp)
                            act.activation(mrelu[:, kc], PS[:, PG + kc], ACT.Relu).then_inc(mexp_ready, 1)
                        elif kind == "mem_split":
                            (kc,) = a
                            act.wait_ge(sq_ready, kc + 1)
                            act.activation(sq_hi[:, kc], sq_f[:, kc], ACT.Copy).then_inc(sq_hi_ready, 1)
                        elif kind == "mem_scale":
                            (m,) = a
                            high(M0["mem", 0] + m)

                @block.vector
                def _(dve):
                    link = counted(dve, dve_step)

                    def statistics(src, stat, mv, veps):
                        if src is not None:
                            for i in range(NT):
                                last = dve.bn_stats(stat[:, i], src[:, i])
                            link(last)
                        for i in range(NT):
                            last = dve.bn_aggr(mv[:, i], stat[:, i])
                        link(last)
                        return dve.tensor_scalar(veps[:], mv[:, :, 1], LN_EPS, None, ALU.add)

                    for kind, *a in schedule:
                        if kind == "presets":
                            dve.memset(qa[:].bitcast(U32), 0).then_inc(queries_cleared, 1)
                        elif kind == "weights16":
                            dve.wait_ge(first_loaded, 16)
                            dve.tensor_copy(ident_h[:], first["ident"]).then_inc(ident_ready, 1)
                            dve.tensor_scalar(first["nscale"][:, :, 0], first["nscale"][:, :, 0], ATT_SCALE, None,
                                              ALU.mult).then_inc(scales_ready, 1)
                            dve.tensor_copy(ident_f[:], first["ident"])
                            dve.tensor_copy(ident_b[:], first["ident"])
                            dve.tensor_copy(mask_b[:], first["mask"]).then_inc(masks_ready, 1)
                        elif kind == "selections":
                            dve.wait_ge(once_loaded, 16)
                            dve.tensor_reduce(mnsum[:], once["mnorm_all"], AX.X, ALU.add).then_inc(once_used, 1)
                        elif kind == "banks":
                            dve.wait_ge(late_loaded, 16)
                            dve.tensor_copy(iota_s[:], late_v["iota"])
                            link(dve.tensor_reduce(bmax[:], late_v["bank"], AX.X, ALU.max))
                            dve.tensor_tensor(late_v["bank"], late_v["bank"],
                                              bmax[:].unsqueeze(2).to_broadcast([P, KC, NB]), ALU.subtract).then_inc(bank_shifted, 1)
                            dve.wait_ge(once_used, 1)
                            link(dve.tensor_scalar(mnsum[:], mnsum[:], MEM_EPS, None, ALU.is_ge))
                            dve.wait_ge(bank_exped, 1)
                            link(dve.tensor_reduce(bsum[:], bankw[:], AX.X, ALU.add))
                            link(dve.reciprocal(bsum[:], bsum[:]))
                            link(dve.tensor_tensor(bankw[:], bankw[:], bsum[:].unsqueeze(2).to_broadcast([P, KC, NB]),
                                                   ALU.mult))
                            dve.tensor_tensor(bankw[:], bankw[:], mnsum[:].unsqueeze(1).to_broadcast([P, KC, NB]),
                                              ALU.mult).then_inc(bank_ready, 1)
                        elif kind == "combine":
                            (n,) = a
                            dve.wait_ge(bank_ready, 1)
                            dve.wait_ge(comb_hi_ready, n + 1)
                            for kc in range(KC):
                                ins = dve.scalar_tensor_tensor(
                                    comb_lo[:, kc, n], PS[:, PY[0], kc * D:(kc + 1) * D], bankw[:, kc, n:n + 1],
                                    comb_hi[:, kc, n].bitcast(F32), ALU.mult, ALU.subtract)
                            ins.then_inc(comb_lo_ready, 1)
                        elif kind == "a_stats":
                            dve.wait_ge(x_loaded, 16)
                            statistics(xin, a_stat, a_mv, a_veps).then_inc(var_ready, 1)
                        elif kind == "a_apply":
                            dve.wait_ge(rstd_ready, 1)
                            for i in range(NT):
                                dve.tensor_scalar(xh[:, i], xin[:, i], a_mv[:, i, 0:1], a_rstd[:, i:i + 1],
                                                  ALU.subtract, ALU.mult).then_inc(xh_ready, 1)
                        elif kind == "a_turn":
                            dve.wait_ge(xhT_made, 1)
                            dve.tensor_copy(xhT[:].rearrange("p k s -> p (k s)"), bank16(PA)).then_inc(xhT_ready, 1)
                        elif kind == "qkv_bias":
                            dve.wait_ge(qkv_rounded, NT)
                            if not has_tail:
                                dve.wait_ge(bias_ready, 1)
                            dve.tensor_tensor(qk16[:], qkv16[:, :, 0:NQK * HD],
                                              bqkv_h[:, 0:NQK * HD].unsqueeze(1).to_broadcast([P, NT, NQK * HD]),
                                              ALU.add).then_inc(qk_biased, 1)
                        elif kind == "mean_square":
                            dve.wait_ge(qk_squared, 1)
                            link(dve.tensor_reduce(ms[:], sq[:], AX.X, ALU.add))
                            dve.tensor_scalar(msv[:], ms[:], 1.0 / HD, RMS_EPS, ALU.mult, ALU.add)\
                               .then_inc(ms_ready, 1)
                        elif kind == "inv_rms":
                            dve.wait_ge(ms_ready, 1)
                            dve.wait_ge(y0_ready, 1)
                            link(dve.scalar_tensor_tensor(y1[:], msv[:], -0.5, y0[:], ALU.mult, ALU.mult))
                            link(dve.tensor_tensor(y1[:], y1[:], y0[:], ALU.mult))
                            link(dve.scalar_tensor_tensor(y1[:], y1[:], 1.5, y0[:], ALU.add, ALU.mult))
                        elif kind == "rms_scale":
                            dve.tensor_tensor(qkn, qk16[:].rearrange("p i (h d) -> p (i h) d", d=HD),
                                              y1[:].unsqueeze(2).to_broadcast([P, NT * NQK, HD]), ALU.mult)\
                               .then_inc(qk_normed, 1)
                        elif kind == "sines":
                            q, h0, h1 = TURNED[a[0]]
                            dve.wait_ge(qk_normed, 1)
                            if not has_tail:
                                dve.wait_ge(rope_ready, 1)
                            dve.tensor_tensor(heads(rota[:], h0, h1), heads(qkn, h0, h1),
                                              turn(0, q, h1 - h0), ALU.mult).then_inc(cos_made, 1)
                        elif kind == "rotate_keys":
                            dve.wait_ge(cos_made, 1)
                            dve.wait_ge(sin_made, 1)
                            if not has_tail:
                                dve.wait_ge(keys_cleared, 1)
                            dve.tensor_tensor(ka[:, :, :, 0:HD], heads(rota[:], NH, NQK), heads(rotb, NH, NQK),
                                              ALU.add).then_inc(k_rotated, 1)
                        elif kind == "rotate_queries":
                            dve.wait_ge(cos_made, len(TURNED))
                            dve.wait_ge(sin_made, len(TURNED))
                            if not has_tail:
                                dve.wait_ge(queries_cleared, 1)
                            dve.tensor_tensor(qa[:, :, :, 0:HD], heads(rota[:], 0, NH), heads(rotb, 0, NH),
                                              ALU.add).then_inc(q_rotated, 1)
                        elif kind == "keysT":
                            dve.wait_ge(kT_made, 1)
                            dve.tensor_copy(kT[:], bank16(PA)[:, 0:S]).then_inc(kT_ready, 1)
                        elif kind == "first":
                            g, n = a
                            i, r0, nr = UNITS[n]
                            u, w = NU * g + n, (i + 1) * P
                            dve.wait_ge(first_made, u + 1)
                            dve.tensor_reduce(
                                smax[:, i, REP * g + r0:REP * g + r0 + nr],
                                PS[:, place["first", g, n][0], 0:nr * w].rearrange("p (r w) -> p r w", r=nr),
                                AX.X, ALU.max).then_inc(max_taken, 1)
                        elif kind == "shift":
                            (g,) = a
                            dve.wait_ge(max_taken, NU * (g + 1))
                            if g == 0:
                                dve.wait_ge(qT1_made, 2)
                            hs = slice(REP * g, REP * g + REP)
                            link(dve.tensor_scalar(qa[:, :, hs, HD], smax[:, :, hs], -1.0 / SHIFT, None, ALU.mult))
                            dve.scalar_tensor_tensor(qa[:, :, hs, HD + 1], smax[:, :, hs], -1.0 / SHIFT,
                                                     qa[:, :, hs, HD], ALU.mult, ALU.subtract).then_inc(shift_ready, 1)
                        elif kind == "normalize":
                            (g,) = a
                            dve.wait_ge(prob_used, NU * (g + 1))
                            o = PS[:, PO, 0:NT * REP * (HD + 1)].rearrange("p (i r d) -> p i r d", i=NT, r=REP)
                            link(dve.reciprocal(rsum[:], o[:, :, :, HD]))
                            dve.tensor_tensor(
                                o16[:, :, g * REP * HD:(g + 1) * REP * HD].rearrange("p i (r d) -> p i r d", r=REP),
                                o[:, :, :, 0:HD], rsum[:].unsqueeze(3).to_broadcast([P, NT, REP, HD]),
                                ALU.mult).then_inc(o_ready, 1)
                        elif kind == "outT":
                            dve.wait_ge(oT_made, 1)
                            dve.tensor_copy(oT[:].rearrange("p k s -> p (k s)"), bank16(PA)).then_inc(oT_ready, 1)
                        elif kind == "a_residual":
                            (i,) = a
                            if has_tail and i == 0:
                                dve.wait_ge(carried, 1)
                            dve.wait_ge(att_rounded, i + 1)
                            link(dve.tensor_tensor(y16[:, i], y16[:, i], bo_h[:], ALU.add))
                            dve.tensor_tensor(xatt[:, i], xin[:, i], y16[:, i], ALU.add).then_inc(attended, 1)
                        elif kind == "carry":
                            dve.wait_ge(xr_free, 1)
                            dve.tensor_copy(xr[:], xatt[:]).then_inc(carried, 1)
                        elif kind == "stats":
                            (n,) = a
                            if n == 0:
                                dve.wait_ge(attended, NT)
                            else:
                                dve.wait_ge(xr_counted, n)
                            statistics(None if n else xatt, n_stat, n_mv, n_veps).then_inc(nvar_ready, 1)
                        elif kind == "apply":
                            (n,) = a
                            dve.wait_ge(nrstd_ready, norms(n))
                            for i in range(NT):
                                dve.tensor_scalar((xn if n else xn0)[:, i], (xr if n else xatt)[:, i],
                                                  n_mv[:, i, 0:1], n_rstd[:, i:i + 1], ALU.subtract, ALU.mult)\
                                   .then_inc(xn_ready, 1)
                        elif kind == "turn":
                            (n,) = a
                            for kc in range(KC):
                                dve.wait_ge(xT_hi_ready, KC * (norms(n) - 1) + kc + 1)
                                dve.tensor_tensor(xT_lo[:, kc], PS[:, PG + kc], xT_hi[:, kc].bitcast(F32),
                                                  ALU.subtract).then_inc(xT_lo_ready, 1)
                        elif kind == "top2":
                            (f,) = a
                            dve.wait_ge(logits_made, f + 1)
                            link(dve.tensor_reduce(
                                lg[:], PS[:, PC, 0:NT * 2 * NE].rearrange("p (i h e) -> p i e h", i=NT, h=2),
                                AX.X, ALU.add))
                            for i in range(NT):
                                last = dve.max(top8[:, i], lg[:, i])
                            link(last)
                            dve.tensor_tensor(gap[:], top8[:, :, 1], top8[:, :, 0], ALU.subtract)\
                               .then_inc(gap_ready, 1)
                        elif kind == "weights":
                            (f,) = a
                            dve.wait_ge(gap_ready, f + 1)
                            for i in range(NT):
                                last = dve.max_index(tidx[:, i], top8[:, i], lg[:, i])
                            link(last)
                            link(dve.tensor_copy(tidf[:], tidx[:]))
                            for k in range(2):
                                last = dve.tensor_tensor(
                                    ceq[:, k], iota_s[:].unsqueeze(1).to_broadcast([P, NT, NE]),
                                    tidf[:, :, k:k + 1].to_broadcast([P, NT, NE]), ALU.is_equal)
                            dve.wait_ge(e2_ready, f + 1)
                            link(dve.tensor_scalar(w12[:, 1], e2[:], 1.0, None, ALU.add))
                            link(dve.reciprocal(w12[:, 0], w12[:, 1]))
                            link(dve.tensor_tensor(w12[:, 1], w12[:, 0], e2[:], ALU.mult))
                            link(dve.tensor_tensor(ceq[:].rearrange("p k i e -> p (k i) e"),
                                                   ceq[:].rearrange("p k i e -> p (k i) e"),
                                                   w12[:].rearrange("p k i -> p (k i)").unsqueeze(2)
                                                   .to_broadcast([P, 2 * NT, NE]), ALU.mult))
                            link(dve.tensor_tensor(cw[:], ceq[:, 0], ceq[:, 1], ALU.add))
                            link(dve.tensor_copy(chl[:, :, 0:NE], cw[:]))
                            dve.tensor_tensor(chl[:, :, NE:], cw[:], chl[:, :, 0:NE].bitcast(F32),
                                              ALU.subtract).then_inc(c_ready, 1)
                        elif kind == "silu":
                            f, j = a
                            q = NJ * f + j
                            dve.wait_ge(tanh_ready, q + 1)
                            dve.scalar_tensor_tensor(sg[:, q % 2], sg[:, q % 2], 1.0, PS[:, PG], ALU.add, ALU.mult)\
                               .then_inc(silu_ready, 1)
                        elif kind == "hidden":
                            f, j = a
                            q, m = NJ * f + j, M0["ffn", f] + j
                            dve.wait_ge(silu_ready, q + 1)
                            dve.wait_ge(cb_made, q + 1)
                            dve.tensor_tensor(sc[:, q % 2], sg[:, q % 2], PS[:, PC], ALU.mult).then_inc(scaled, 1)
                            dve.wait_ge(scaled, q + 1)
                            dve.wait_ge(up_made, q + 1)
                            if m >= RH:
                                wait_for_low(dve, m - RH)
                            dve.tensor_tensor(hf[:, m % RH], sc[:, q % 2], PS[:, PU], ALU.mult).then_inc(h_ready, 1)
                        elif kind == "residual":
                            (n,) = a
                            for k in range(2):
                                if k == 0:
                                    dve.wait_ge(y_half_made, n + 1)
                                else:
                                    dve.wait_ge(h_used, (NJ, NJ + NB * KC, 2 * NJ + NB * KC)[n])
                                dve.tensor_tensor(
                                    xr[:, 2 * k:2 * k + 2], xr[:, 2 * k:2 * k + 2],
                                    PS[:, PY[k]].rearrange("p (i c) -> p i c", i=2), ALU.add).then_inc(xr_ready, 1)
                                if n < NS - 1:
                                    dve.wait_ge(xr_ready, 2 * n + k + 1)
                                    for i in (2 * k, 2 * k + 1):
                                        last = dve.bn_stats(n_stat[:, i], xr[:, i])
                            if n < NS - 1:
                                last.then_inc(xr_counted, 1)
                        elif kind == "mem_split":
                            (kc,) = a
                            dve.wait_ge(mexp_ready, kc + 1)
                            dve.scalar_tensor_tensor(sq_f[:, kc], mexp[:, kc], 1.0, mrelu[:, kc],
                                                     ALU.min, ALU.add).then_inc(sq_ready, 1)
                        elif kind == "mem_low":
                            (kc,) = a
                            dve.wait_ge(sq_hi_ready, kc + 1)
                            dve.tensor_tensor(sq_lo[:, kc], sq_f[:, kc], sq_hi[:, kc].bitcast(F32), ALU.subtract)\
                               .then_inc(sq_lo_ready, 1)
                        elif kind == "low":
                            (m,) = a
                            dve.wait_ge(hi_ready, m + 1)
                            if m >= RH:
                                dve.wait_ge(h_used, m + 1 - RH)
                            dve.tensor_tensor(hlo[:, m % RH], hf[:, m % RH], hhi[:, m % RH].bitcast(F32),
                                              ALU.subtract).then_inc(lo_by_dve, 1)
                        elif kind == "mem_inv":
                            dve.wait_ge(sq_ready, KC)
                            dve.wait_ge(norm_made, 1)
                            link(dve.tensor_scalar(nrec, PS[:, PC], MEM_EPS, None, ALU.max))
                            link(dve.reciprocal(nrec, nrec))
                            link(dve.tensor_copy(rr[:], nrec))
                            h = slice(NB * MH, 2 * NB * MH)
                            dve.tensor_tensor(rr[h], nrec[h], rr[h].bitcast(F32), ALU.subtract).then_inc(rr_ready, 1)
                        elif kind == "mem_scale":
                            (m,) = a
                            u = M0["mem", 0] + m
                            dve.wait_ge(rb_made, m + 1)
                            wait_for_low(dve, u - RH)
                            dve.tensor_tensor(hf[:, u % RH], sq_f[:, m % KC], PS[:, PG + m % 3], ALU.mult)\
                               .then_inc(h_ready, 1)

                @block.gpsimd
                def _(pool):
                    def low(m):
                        if m in LOW_BY_DVE:
                            return
                        pool.wait_ge(hi_ready, m + 1)
                        if m >= RH:
                            pool.wait_ge(h_used, m + 1 - RH)
                        pool.tensor_tensor(hlo[:, m % RH], hf[:, m % RH], hhi[:, m % RH].bitcast(F32),
                                           ALU.subtract).then_inc(lo_by_pool, 1)

                    for kind, *a in schedule:
                        if kind == "presets":
                            pool.memset(mhalf[:], -0.5)
                            pool.memset(ka[:].bitcast(U32), 0).then_inc(keys_cleared, 1)
                            pool.wait_ge(keys_cleared, 1)
                            pool.memset(ka[:, :, :, HD:HD + 2], SHIFT).then_inc(keys_set, 1)
                            pool.memset(vaug[:], 1.0)
                            pool.memset(kbd[:].bitcast(U32), 0).then_inc(copies_cleared, 1)
                        elif kind == "tables":
                            pool.wait_ge(first_loaded, 16)
                            pool.wait_ge(scales_ready, 1)
                            for n in range(2):
                                for q in range(2):
                                    last = pool.tensor_tensor(
                                        rope[:, n, q], first["turns"][:, n],
                                        first["nscale"][:, n, q].unsqueeze(1).to_broadcast([P, NT, HD]), ALU.mult)
                            last.then_inc(rope_ready, 1)
                        elif kind == "norms":
                            pool.wait_ge(late_loaded, 16)
                            pool.wait_ge(once_used, 2)
                            pool.tensor_tensor(
                                mem_bd.rearrange("p n k (h d) -> p (n k) h d", h=HP),
                                late_v["mem"].rearrange("p n k d -> p (n k) d").unsqueeze(2)
                                .to_broadcast([P, NB * KC, HP, MD]),
                                late_v["headmask"].unsqueeze(1).unsqueeze(3).to_broadcast([P, NB * KC, HP, MD]),
                                ALU.mult).then_inc(mem_placed, 1)
                            pool.memset(norm_f[:], 0.0).then_inc(pool_set, 1)
                            pool.wait_ge(pool_set, 1)
                            for kc in range(KC):
                                for dup in range(2):
                                    last = pool.tensor_tensor(
                                        norm_f[:, kc, dup, :, kc * HP:(kc + 1) * HP],
                                        late_v["mnorm"][:, kc].unsqueeze(2).to_broadcast([P, NB, HP]),
                                        late_v["headmask"].unsqueeze(1).to_broadcast([P, NB, HP]), ALU.mult)
                            last.then_inc(pool_set, 1)
                            pool.wait_ge(pool_set, 2)
                            halves = ((norm_f[:].rearrange("p k u n h -> p k (u n h)"), norm_hi[:], norm_lo[:]),
                                      (late_v["wr"], wr_hl[:, :, 0:NE], wr_hl[:, :, NE:]), (late_v["mwq"], mwq_hi[:], mwq_lo[:]))
                            for f_, hi_, _ in halves:
                                last = pool.tensor_copy(hi_, f_)
                            last.then_inc(pool_set, 1)
                            pool.wait_ge(pool_set, 3)
                            for f_, hi_, lo_ in halves:
                                pool.tensor_tensor(lo_, f_, hi_.bitcast(F32), ALU.subtract)
                        elif kind == "split":
                            (w,) = a
                            pool.wait_ge(whi_ready, w + 1)
                            pool.wait_ge(staged[w], 16)
                            pool.tensor_tensor(wlo[:, w], wstage[:, w % 2], whi[:, w].bitcast(F32), ALU.subtract)\
                                .then_inc(wlo_ready, 1)
                        elif kind == "a_stats":
                            if not has_tail:
                                pool.wait_ge(queries_cleared, 1)
                            pool.memset(qa[:, :, :, HD:HD + 2], 0.0).then_inc(shift_cleared, 1)
                            pool.wait_ge(var_ready, 1)
                            pool.tensor_tensor(a_rstd[:], a_veps[:], mhalf[:], ALU.pow).then_inc(rstd_ready, 1)
                        elif kind == "qkv_bias":
                            pool.wait_ge(qkv_rounded, NT)
                            if not has_tail:
                                pool.wait_ge(bias_ready, 1)
                            pool.tensor_tensor(
                                vaug[:, :, :, 0:HD],
                                qkv16[:, :, D + NG * HD:].rearrange("p i (g d) -> p i g d", g=NG),
                                bqkv_h[:, D + NG * HD:].rearrange("p (g d) -> p g d", g=NG).unsqueeze(1)
                                .to_broadcast([P, NT, NG, HD]), ALU.add).then_inc(v_ready, 1)
                        elif kind == "sines":
                            q, h0, h1 = TURNED[a[0]]
                            pool.wait_ge(qk_normed, 1)
                            if not has_tail:
                                pool.wait_ge(once_used, 2)
                                pool.wait_ge(rope_ready, 1)
                            for c, z in ((0, HD // 2), (HD // 2, 0)):
                                last = pool.tensor_tensor(
                                    heads(rotb, h0, h1)[:, :, :, c:c + HD // 2],
                                    heads(qkn, h0, h1)[:, :, :, z:z + HD // 2],
                                    turn(1, q, h1 - h0)[:, :, :, c:c + HD // 2], ALU.mult)
                            last.then_inc(sin_made, 1)
                        elif kind == "stats":
                            (n,) = a
                            pool.wait_ge(nvar_ready, norms(n))
                            pool.tensor_tensor(n_rstd[:], n_veps[:], mhalf[:], ALU.pow).then_inc(nrstd_ready, 1)
                        elif kind == "hidden":
                            f, j = a
                            low(M0["ffn", f] + j)
                        elif kind == "mem_scale":
                            (m,) = a
                            low(M0["mem", 0] + m)
            clear()

        sequences(PROLOGUE, x_v[0], None)

        staging.close()
        xr = sb("xr", [P, NT, D])
        lg = sb("lg", [P, NT, NE])
        top8 = sb("top8", [P, NT, 8])
        tidx = sb("tidx", [P, NT, 8], U32)
        tidf = sb("tidf", [P, NT, 8])
        gap = sb("gap", [P, NT])
        e2 = sb("e2", [P, NT])
        w12 = sb("w12", [P, 2, NT])
        ceq = sb("ceq", [P, 2, NT, NE])
        cw = lg
        chl = sb("chl", [P, NT, 2 * NE], F32R)
        sg = sb("sg", [P, 2, S])
        xn = sg[:].rearrange("p a s -> p (a s)").rearrange("p (i c) -> p i c", i=NT)
        mexp = sg
        sc = sb("sc", [P, 2, S])
        mrelu = sc
        hf = sb("hf", [P, RH, S])
        hhi = sb("hhi", [P, RH, S], F32R)
        hlo = sb("hlo", [P, RH, S], F32R)
        sq_f = sb("sq_f", [P, KC, S])
        sq_hi, sq_lo = hhi[:, 0:KC], hlo[:, 0:KC]
        nrec = sc[:, 0]
        rr = sb("rr", [P, S], F32R)
        cT = rr[0:2 * NE]
        lgT = sc[0:2 * NE, 1]

        nc.sync.sem_inc(stored, 16)
        with nc.Fori(0, B - 1) as b:
            sequences(STEADY, x_v[bass.ds(b + 1, 1)].rearrange("a p i c -> (a p) i c"),
                      out_v[bass.ds(b, 1)].rearrange("a p i c -> (a p) i c"))
        sequences(EPILOGUE, None, out_v[B - 1])


def kernel(**inputs):
    import concourse.bacc as _bacc
    from concourse.bass_utils import run_bass_kernel_spmd as _run

    f = lambda a: np.ascontiguousarray(a, dtype=np.float32)
    g = {k: np.asarray(v) for k, v in inputs.items()}
    rows = lambda a, *shape: f(np.broadcast_to(a, (P, *shape)))

    inv = (1.0 / 10000.0 ** (np.arange(0, HD, 2, dtype=np.float32) / HD)).astype(np.float32)
    ang = np.outer(np.arange(S, dtype=np.float32), inv).astype(np.float32)
    by_tile = lambda a: f(a.reshape(NT, P, HD).transpose(1, 0, 2))
    cos = by_tile(np.concatenate([np.cos(ang), np.cos(ang)], 1))
    sin = by_tile(np.concatenate([-np.sin(ang), np.sin(ang)], 1))
    p = np.arange(P)
    ident = f(np.eye(P))
    mask = f(np.where(p[None, :] > p[:, None], MASKED, 0.0))
    headmask = f(p[:, None] // MD == np.arange(HP)[None, :])
    iota = rows(np.arange(NE), NE)
    selc = f(np.tile(np.arange(NE)[:, None] == np.arange(FT)[None, :] // FI, (2, 1)))
    row = np.arange(P) % (NB * MH)
    n_, kc_, c_ = np.ix_(np.arange(NB), np.arange(KC), p)
    selr = f(row[:, None, None, None] == (n_ * MH + kc_ * HP + c_ // MD)[None])

    qs, ks = g["L0_attn_a_q_norm_scale"], g["L0_attn_a_k_norm_scale"]
    swap = lambda a: np.concatenate([a[HD // 2:], a[:HD // 2]])
    scales = lambda q, k: rows(np.stack([q, k]), 2, HD)
    mem = g["L0_attn_b_memories"]
    mno = g["L0_attn_b_memory_norms"]
    bank = g["L0_attn_b_bank_weights"]
    by_row = lambda a: a.reshape(KC, P, -1).transpose(1, 0, 2)
    small = {
        "wqkv": by_row(np.concatenate([g["L0_attn_a_wq"], g["L0_attn_a_wk"], g["L0_attn_a_wv"]], 1)),
        "bqkv": rows(np.concatenate([g["L0_attn_a_bq"], g["L0_attn_a_bk"], g["L0_attn_a_bv"]]), QKV),
        "nscale": np.stack([scales(qs, ks), scales(swap(qs), swap(ks))], 1), "turns": np.stack([cos, sin], 1),
        "wo": by_row(g["L0_attn_a_wo"]), "bo": rows(g["L0_attn_a_bo"], D),
        "wr": by_row(g["L0_ffn_Wr"]), "mwq": by_row(g["L0_attn_b_Wq"].T), "mwo": by_row(g["L0_attn_b_Wo"].T),
        "mem": f(mem.reshape(NB, KC, HP, MD, MD).transpose(2, 4, 0, 1, 3).reshape(P, NB, KC, MD)),
        "mnorm": f(mno.reshape(NB, KC, P).transpose(2, 1, 0)),
        "mnorm_all": rows(mno.reshape(NB, MH * MD), NB, MH * MD),
        "bank": f(np.repeat(bank, MD, axis=0).reshape(KC, P, NB).transpose(1, 0, 2)),
        "ident": ident, "mask": mask, "headmask": headmask, "iota": iota, "selr": selr,
    }
    packed = lambda pack: f(np.concatenate([small[n].reshape(P, -1) for n in pack], 1))
    arrays = {
        "x": f(g["L0_attn_a_x"]),
        "first_pack": packed(FIRST_PACK), "once_pack": packed(ONCE_PACK), "late_pack": packed(LATE_PACK),
        "selc": selc,
        "wg": f(g["L0_ffn_Wg"].transpose(1, 0, 2).reshape(D, FT)),
        "wu": f(g["L0_ffn_Wu"].transpose(1, 0, 2).reshape(D, FT)),
        "wd": f(g["L0_ffn_Wd"].reshape(FT, D)),
    }
    nc = _bacc.Bacc("TRN2", target_bir_lowering=False, num_devices=1)
    args = {n: nc.dram_tensor(f"in_{n}", a.shape, F32, kind="ExternalInput").ap() for n, a in arrays.items()}
    out = nc.dram_tensor("out", (B, S, D), F32, kind="ExternalOutput").ap()
    build(nc, **args, out=out)
    r = _run(nc, [{f"in_{n}": a for n, a in arrays.items()}], core_ids=[0])
    return r.results[0]["out"]
```
